# Optimizing a Trainium2 kernel written in Bass

```python
import numpy as np
import jax
import jax.numpy as jnp

def _softmax(x, axis=-1):
    return jax.nn.softmax(x, axis=axis)

def _gelu(x):
    return jax.nn.gelu(x, approximate=True)

def _silu(x):
    return jax.nn.silu(x)

def _sigmoid(x):
    return jax.nn.sigmoid(x)

def _layernorm(x, axis=-1, eps=1e-05):
    m = jnp.mean(x, axis=axis, keepdims=True)
    v = jnp.var(x, axis=axis, keepdims=True)
    return (x - m) / jnp.sqrt(v + eps)

def _scatter_add(tgt, idx, src, axis=0):
    return tgt.at[idx].add(src)

def _segment_sum(src, seg, n):
    return jax.ops.segment_sum(src, seg, n)
kernel_name = 'mk_vit_tower_d2_tok_img512_r4_62cc87'

def setup_inputs(seed: int=0):
    np.random.seed(seed)
    _w = jnp.asarray

    def _rec_inputs():
        import jax
        import jax.numpy as jnp
        _rk = jax.random.key(seed)
        x = -0.000178447 + 0.99995 * jax.random.normal(jax.random.fold_in(_rk, 1), (64, 3, 176, 208), jnp.float32)
        return x
    x = _rec_inputs()

    def _L0_tok_setup():
        import jax, jax.numpy as jnp
        import numpy as np
        P1, P2, C = (16, 16, 3)
        PW, PH = (176 // P1, 208 // P2)
        key = jax.random.key(seed)
        k1, k2, k3, k4, k5 = jax.random.split(key, 5)
        B, D = (64, 128)
        patch_dim = P1 * P2 * C
        return {'x': jax.random.normal(k1, (B, C, PW * P1, PH * P2), dtype=jnp.float32), 'W': jax.random.normal(k2, (D, patch_dim), dtype=jnp.float32) * 0.02, 'b': jax.random.normal(k3, (D,), dtype=jnp.float32) * 0.02, 'cls_token': jax.random.uniform(k4, (1, 1, D), dtype=jnp.float32), 'pos_emb': jax.random.normal(k5, (1, PW * PH + 1, 1), dtype=jnp.float32)}
    _L0_tok_all = _L0_tok_setup()
    _L0_tok_in = {k: v for k, v in _L0_tok_all.items() if k in ('W', 'b', 'cls_token', 'pos_emb')}
    del _L0_tok_all

    def _L0_attn_setup():
        import jax, jax.numpy as jnp
        import numpy as np
        EPS = 1e-05

        def _ln(x, w, b, axes):
            mu = jnp.mean(x, axis=axes, keepdims=True)
            var = jnp.mean((x - mu) ** 2, axis=axes, keepdims=True)
            return (x - mu) / jnp.sqrt(var + EPS) * w + b
        key = jax.random.key(seed)
        ks = jax.random.split(key, 6)
        B, L, D, A, H, F = (1, 256, 128, 32, 8, 512)
        s = 0.02
        return {'x': jax.random.normal(ks[0], (B, L, D), jnp.float32), 'ln0_w': jnp.ones((D,), jnp.float32), 'ln0_b': jnp.zeros((D,), jnp.float32), 'ln1_w': jnp.ones((D, H), jnp.float32), 'ln1_b': jnp.zeros((D, H), jnp.float32), 'qw': jax.random.normal(ks[1], (D, A * H), jnp.float32) * s, 'qb': jnp.zeros((A * H,), jnp.float32), 'kw': jax.random.normal(ks[2], (D, A * H), jnp.float32) * s, 'kb': jnp.zeros((A * H,), jnp.float32), 'vw': jax.random.normal(ks[3], (D, D * H), jnp.float32) * s, 'vb': jnp.zeros((D * H,), jnp.float32), 'w1': jax.random.normal(ks[4], (D * H, F), jnp.float32) * s, 'b1': jnp.zeros((F,), jnp.float32), 'w2': jax.random.normal(ks[5], (F, D), jnp.float32) * s, 'b2': jnp.zeros((D,), jnp.float32)}
    _L0_attn_all = _L0_attn_setup()
    _L0_attn_in = {k: v for k, v in _L0_attn_all.items() if k in ('ln0_w', 'ln0_b', 'ln1_w', 'ln1_b', 'qw', 'qb', 'kw', 'kb', 'vw', 'vb', 'w1', 'b1', 'w2', 'b2')}
    del _L0_attn_all

    def _L0_ffn_setup():
        import jax, jax.numpy as jnp
        import numpy as np
        TOP_K = 2

        def quick_gelu(x):
            return x * jax.nn.sigmoid(1.702 * x)
        key = jax.random.key(seed)
        ks = jax.random.split(key, 6)
        B, S, H, I, E = (8, 1024, 128, 256, 8)
        s_h = 1.0 / np.sqrt(H).astype(np.float32)
        s_i = 1.0 / np.sqrt(I).astype(np.float32)
        return {'hidden_states': jax.random.normal(ks[0], (B, S, H), jnp.float32), 'router_w': jax.random.normal(ks[1], (H, E), jnp.float32) * s_h, 'router_b': jnp.zeros((E,), jnp.float32), 'gate_up_proj': jax.random.normal(ks[2], (E, H, 2 * I), jnp.float32) * s_h, 'gate_up_proj_bias': jnp.zeros((E, 2 * I), jnp.float32), 'down_proj': jax.random.normal(ks[3], (E, I, H), jnp.float32) * s_i, 'down_proj_bias': jnp.zeros((E, H), jnp.float32)}
    _L0_ffn_all = _L0_ffn_setup()
    _L0_ffn_in = {k: v for k, v in _L0_ffn_all.items() if k in ('router_w', 'router_b', 'gate_up_proj', 'gate_up_proj_bias', 'down_proj', 'down_proj_bias')}
    del _L0_ffn_all

    def _L1_attn_setup():
        import jax, jax.numpy as jnp
        import numpy as np
        from jax import lax
        B, L, D = (8, 512, 128)

        def _mlp(x, w1, w2):
            return x + jax.nn.gelu(x @ w1, approximate=False) @ w2

        def _l2norm(t):
            n = jnp.linalg.norm(t, axis=-1, keepdims=True)
            return t / jnp.maximum(n, 1e-12)

        def _forward(x, conv_w, conv_b, q_w, mem_w1, mem_w2, eta_w1, eta_w2, alpha_w1, alpha_w2):
            xc = lax.conv_general_dilated(jnp.transpose(x, (0, 2, 1)), conv_w, window_strides=(1,), padding=[(3, 0)], feature_group_count=D, dimension_numbers=('NCH', 'OIH', 'NCH')) + conv_b[None, :, None]
            xc = jnp.transpose(xc, (0, 2, 1))
            q = _l2norm(xc @ q_w.T)
            eta_mean = jax.nn.sigmoid(_mlp(xc, eta_w1, eta_w2)).mean(axis=(0, 2))
            alpha_mean = jax.nn.sigmoid(_mlp(xc, alpha_w1, alpha_w2)).mean(axis=(0, 2))

            def step(carry, inp):
                w1, w2 = carry
                q_t, a_t, e_t = inp
                o_t = _mlp(q_t, w1, w2)
                new_w1 = w1 * a_t - e_t * 0.01
                new_w2 = w2 * a_t - e_t * 0.01
                return ((new_w1, new_w2), o_t)
            qs = jnp.transpose(q, (1, 0, 2))
            (_, _), outs = lax.scan(step, (mem_w1, mem_w2), (qs, alpha_mean, eta_mean))
            return jnp.transpose(outs, (1, 0, 2))
        key = jax.random.key(seed)
        ks = jax.random.split(key, 12)
        s = 0.02
        return {'x': jax.random.normal(ks[0], (B, L, D), jnp.float32), 'conv_w': jax.random.normal(ks[1], (D, 1, 4), jnp.float32) * s, 'conv_b': jax.random.normal(ks[2], (D,), jnp.float32) * s, 'q_w': jax.random.normal(ks[3], (D, D), jnp.float32) * s, 'mem_w1': jax.random.normal(ks[4], (D, D), jnp.float32) * s, 'mem_w2': jax.random.normal(ks[5], (D, D), jnp.float32) * s, 'eta_w1': jax.random.normal(ks[6], (D, D), jnp.float32) * s, 'eta_w2': jax.random.normal(ks[7], (D, D), jnp.float32) * s, 'alpha_w1': jax.random.normal(ks[8], (D, D), jnp.float32) * s, 'alpha_w2': jax.random.normal(ks[9], (D, D), jnp.float32) * s}
    _L1_attn_all = _L1_attn_setup()
    _L1_attn_in = {k: v for k, v in _L1_attn_all.items() if k in ('conv_w', 'conv_b', 'q_w', 'mem_w1', 'mem_w2', 'eta_w1', 'eta_w2', 'alpha_w1', 'alpha_w2')}
    del _L1_attn_all

    def _L1_ffn_setup():
        import jax, jax.numpy as jnp
        import numpy as np
        K_INPUT, K_PROCESS, K_OUTPUT = (64, 128, 64)

        def _gelu(x):
            return jax.nn.gelu(x, approximate=False)
        key = jax.random.key(seed)
        ks = jax.random.split(key, 6)
        d_model, n_in, n_proc, n_out, d_pv = (128, 512, 256, 512, 64)
        B, S = (2, 256)

        def xavier(k, shape):
            std = (2.0 / (shape[0] + shape[1])) ** 0.5
            return jax.random.normal(k, shape, dtype=jnp.float32) * std
        return {'x': jax.random.normal(ks[0], (B, S, d_model), dtype=jnp.float32), 'input_patterns': xavier(ks[1], (n_in, d_model)), 'process_input_weights': xavier(ks[2], (n_proc, n_in)), 'process_values': xavier(ks[3], (n_proc, d_pv)), 'output_input_weights': xavier(ks[4], (n_out, d_pv)), 'output_patterns': xavier(ks[5], (n_out, d_model))}
    _L1_ffn_all = _L1_ffn_setup()
    _L1_ffn_in = {k: v for k, v in _L1_ffn_all.items() if k in ('input_patterns', 'process_input_weights', 'process_values', 'output_input_weights', 'output_patterns')}
    del _L1_ffn_all
    return {'x': x, 'L0_tok_W': _L0_tok_in['W'], 'L0_tok_b': _L0_tok_in['b'], 'L0_tok_cls_token': _L0_tok_in['cls_token'], 'L0_tok_pos_emb': _L0_tok_in['pos_emb'], 'L0_attn_ln0_w': _L0_attn_in['ln0_w'], 'L0_attn_ln0_b': _L0_attn_in['ln0_b'], 'L0_attn_ln1_w': _L0_attn_in['ln1_w'], 'L0_attn_ln1_b': _L0_attn_in['ln1_b'], 'L0_attn_qw': _L0_attn_in['qw'], 'L0_attn_qb': _L0_attn_in['qb'], 'L0_attn_kw': _L0_attn_in['kw'], 'L0_attn_kb': _L0_attn_in['kb'], 'L0_attn_vw': _L0_attn_in['vw'], 'L0_attn_vb': _L0_attn_in['vb'], 'L0_attn_w1': _L0_attn_in['w1'], 'L0_attn_b1': _L0_attn_in['b1'], 'L0_attn_w2': _L0_attn_in['w2'], 'L0_attn_b2': _L0_attn_in['b2'], 'L0_ffn_router_w': _L0_ffn_in['router_w'], 'L0_ffn_router_b': _L0_ffn_in['router_b'], 'L0_ffn_gate_up_proj': _L0_ffn_in['gate_up_proj'], 'L0_ffn_gate_up_proj_bias': _L0_ffn_in['gate_up_proj_bias'], 'L0_ffn_down_proj': _L0_ffn_in['down_proj'], 'L0_ffn_down_proj_bias': _L0_ffn_in['down_proj_bias'], 'L1_attn_conv_w': _L1_attn_in['conv_w'], 'L1_attn_conv_b': _L1_attn_in['conv_b'], 'L1_attn_q_w': _L1_attn_in['q_w'], 'L1_attn_mem_w1': _L1_attn_in['mem_w1'], 'L1_attn_mem_w2': _L1_attn_in['mem_w2'], 'L1_attn_eta_w1': _L1_attn_in['eta_w1'], 'L1_attn_eta_w2': _L1_attn_in['eta_w2'], 'L1_attn_alpha_w1': _L1_attn_in['alpha_w1'], 'L1_attn_alpha_w2': _L1_attn_in['alpha_w2'], 'L1_ffn_input_patterns': _L1_ffn_in['input_patterns'], 'L1_ffn_process_input_weights': _L1_ffn_in['process_input_weights'], 'L1_ffn_process_values': _L1_ffn_in['process_values'], 'L1_ffn_output_input_weights': _L1_ffn_in['output_input_weights'], 'L1_ffn_output_patterns': _L1_ffn_in['output_patterns']}

def reference(x, L0_tok_W, L0_tok_b, L0_tok_cls_token, L0_tok_pos_emb, L0_attn_ln0_w, L0_attn_ln0_b, L0_attn_ln1_w, L0_attn_ln1_b, L0_attn_qw, L0_attn_qb, L0_attn_kw, L0_attn_kb, L0_attn_vw, L0_attn_vb, L0_attn_w1, L0_attn_b1, L0_attn_w2, L0_attn_b2, L0_ffn_router_w, L0_ffn_router_b, L0_ffn_gate_up_proj, L0_ffn_gate_up_proj_bias, L0_ffn_down_proj, L0_ffn_down_proj_bias, L1_attn_conv_w, L1_attn_conv_b, L1_attn_q_w, L1_attn_mem_w1, L1_attn_mem_w2, L1_attn_eta_w1, L1_attn_eta_w2, L1_attn_alpha_w1, L1_attn_alpha_w2, L1_ffn_input_patterns, L1_ffn_process_input_weights, L1_ffn_process_values, L1_ffn_output_input_weights, L1_ffn_output_patterns):
    import jax
    import jax.numpy as jnp

    def _L0_tok_ref(x, W, b, cls_token, pos_emb):
        import jax, jax.numpy as jnp
        import numpy as np
        P1, P2, C = (16, 16, 3)
        PW, PH = (176 // P1, 208 // P2)
        B = x.shape[0]
        patches = x.reshape(B, C, PW, P1, PH, P2)
        patches = patches.transpose(0, 2, 4, 3, 5, 1).reshape(B, PW * PH, P1 * P2 * C)
        proj = jnp.einsum('bnp,dp->bnd', patches, W) + b
        cls = jnp.broadcast_to(cls_token, (B, 1, cls_token.shape[-1]))
        out = jnp.concatenate([cls, proj], axis=1) + pos_emb
        return out

    def _L0_attn_ref(x, ln0_w, ln0_b, ln1_w, ln1_b, qw, qb, kw, kb, vw, vb, w1, b1, w2, b2):
        import jax, jax.numpy as jnp
        import numpy as np
        EPS = 1e-05

        def _ln(x, w, b, axes):
            mu = jnp.mean(x, axis=axes, keepdims=True)
            var = jnp.mean((x - mu) ** 2, axis=axes, keepdims=True)
            return (x - mu) / jnp.sqrt(var + EPS) * w + b
        B, L, D = x.shape
        H = ln1_w.shape[-1]
        _x = _ln(x, ln0_w, ln0_b, -1)
        q = jnp.exp(jnp.clip(_x @ qw + qb, -10.0, 10.0)).reshape(B, L, -1, H)
        k = jnp.exp(jnp.clip(_x @ kw + kb, -10.0, 10.0)).reshape(B, L, -1, H)
        v = (x @ vw + vb).reshape(B, L, D, H)
        kv = jnp.cumsum(jnp.einsum('blah,bldh->bladh', k, v), axis=1)
        qkv = jnp.einsum('blah,bladh->bldh', q, kv)
        den = jnp.einsum('blah,blah->blh', q, jnp.cumsum(k, axis=1))[..., None, :]
        y = x[..., None] + _ln(qkv / den, ln1_w, ln1_b, (-2, -1))
        y = y.reshape(B, L, D * H)
        h1 = jax.nn.relu(y @ w1 + b1)
        return jax.nn.relu(h1 @ w2 + b2) + x

    def _L0_ffn_ref(hidden_states, router_w, router_b, gate_up_proj, gate_up_proj_bias, down_proj, down_proj_bias):
        import jax, jax.numpy as jnp
        import numpy as np
        TOP_K = 2

        def quick_gelu(x):
            return x * jax.nn.sigmoid(1.702 * x)
        B, S, H = hidden_states.shape
        E = router_b.shape[0]
        x = hidden_states.reshape(-1, H)
        T = x.shape[0]
        logits = x @ router_w + router_b
        top_w, sel = jax.lax.top_k(logits, TOP_K)
        top_w = jax.nn.softmax(top_w, axis=-1)
        tok_w = jnp.zeros((T, E), x.dtype).at[jnp.arange(T)[:, None], sel].add(top_w)

        def body(acc, params):
            Wgu, bgu, Wd, bd, w_e = params
            gu = x @ Wgu + bgu
            gate, up = jnp.split(gu, 2, axis=-1)
            act = (up + 1.0) * quick_gelu(gate)
            out = act @ Wd + bd
            return (acc + out * w_e[:, None], None)
        acc0 = jnp.zeros((T, H), x.dtype)
        acc, _ = jax.lax.scan(body, acc0, (gate_up_proj, gate_up_proj_bias, down_proj, down_proj_bias, tok_w.T))
        return acc.reshape(B, S, H)

    def _L1_attn_ref(x, conv_w, conv_b, q_w, mem_w1, mem_w2, eta_w1, eta_w2, alpha_w1, alpha_w2):
        import jax, jax.numpy as jnp
        import numpy as np
        from jax import lax
        B, L, D = (8, 512, 128)

        def _mlp(x, w1, w2):
            return x + jax.nn.gelu(x @ w1, approximate=False) @ w2

        def _l2norm(t):
            n = jnp.linalg.norm(t, axis=-1, keepdims=True)
            return t / jnp.maximum(n, 1e-12)

        def _forward(x, conv_w, conv_b, q_w, mem_w1, mem_w2, eta_w1, eta_w2, alpha_w1, alpha_w2):
            xc = lax.conv_general_dilated(jnp.transpose(x, (0, 2, 1)), conv_w, window_strides=(1,), padding=[(3, 0)], feature_group_count=D, dimension_numbers=('NCH', 'OIH', 'NCH')) + conv_b[None, :, None]
            xc = jnp.transpose(xc, (0, 2, 1))
            q = _l2norm(xc @ q_w.T)
            eta_mean = jax.nn.sigmoid(_mlp(xc, eta_w1, eta_w2)).mean(axis=(0, 2))
            alpha_mean = jax.nn.sigmoid(_mlp(xc, alpha_w1, alpha_w2)).mean(axis=(0, 2))

            def step(carry, inp):
                w1, w2 = carry
                q_t, a_t, e_t = inp
                o_t = _mlp(q_t, w1, w2)
                new_w1 = w1 * a_t - e_t * 0.01
                new_w2 = w2 * a_t - e_t * 0.01
                return ((new_w1, new_w2), o_t)
            qs = jnp.transpose(q, (1, 0, 2))
            (_, _), outs = lax.scan(step, (mem_w1, mem_w2), (qs, alpha_mean, eta_mean))
            return jnp.transpose(outs, (1, 0, 2))
        return _forward(x, conv_w, conv_b, q_w, mem_w1, mem_w2, eta_w1, eta_w2, alpha_w1, alpha_w2)

    def _L1_ffn_ref(x, input_patterns, process_input_weights, process_values, output_input_weights, output_patterns):
        import jax, jax.numpy as jnp
        import numpy as np
        K_INPUT, K_PROCESS, K_OUTPUT = (64, 128, 64)

        def _gelu(x):
            return jax.nn.gelu(x, approximate=False)
        B, S, d_model = x.shape
        n_in = input_patterns.shape[0]
        input_acts = _gelu(jnp.einsum('bsd,nd->bsn', x, input_patterns))
        top_in_acts, top_in_idx = jax.lax.top_k(input_acts, K_INPUT)
        bi = jnp.arange(B)[:, None, None]
        si = jnp.arange(S)[None, :, None]
        input_repr = jnp.zeros((B, S, n_in), dtype=x.dtype).at[bi, si, top_in_idx].set(top_in_acts)
        process_acts = _gelu(jnp.einsum('bsn,pn->bsp', input_repr, process_input_weights))
        top_p_acts, top_p_idx = jax.lax.top_k(process_acts, K_PROCESS)
        sel_values = process_values[top_p_idx]
        p_weights = jax.nn.softmax(top_p_acts, axis=-1)
        agg_value = jnp.einsum('bsk,bskd->bsd', p_weights, sel_values)
        output_acts = _gelu(jnp.einsum('bsd,od->bso', agg_value, output_input_weights))
        top_o_acts, top_o_idx = jax.lax.top_k(output_acts, K_OUTPUT)
        sel_patterns = output_patterns[top_o_idx]
        out = jnp.einsum('bsk,bskm->bsm', top_o_acts, sel_patterns)
        return out
    h = _L0_tok_ref(x, L0_tok_W, L0_tok_b, L0_tok_cls_token, L0_tok_pos_emb)
    h = h + _L0_attn_ref(_layernorm(h, axis=-1), L0_attn_ln0_w, L0_attn_ln0_b, L0_attn_ln1_w, L0_attn_ln1_b, L0_attn_qw, L0_attn_qb, L0_attn_kw, L0_attn_kb, L0_attn_vw, L0_attn_vb, L0_attn_w1, L0_attn_b1, L0_attn_w2, L0_attn_b2)
    h = h + _L0_ffn_ref(_layernorm(h, axis=-1), L0_ffn_router_w, L0_ffn_router_b, L0_ffn_gate_up_proj, L0_ffn_gate_up_proj_bias, L0_ffn_down_proj, L0_ffn_down_proj_bias)
    h = h + _L1_attn_ref(_layernorm(h, axis=-1), L1_attn_conv_w, L1_attn_conv_b, L1_attn_q_w, L1_attn_mem_w1, L1_attn_mem_w2, L1_attn_eta_w1, L1_attn_eta_w2, L1_attn_alpha_w1, L1_attn_alpha_w2)
    h = h + _L1_ffn_ref(_layernorm(h, axis=-1), L1_ffn_input_patterns, L1_ffn_process_input_weights, L1_ffn_process_values, L1_ffn_output_input_weights, L1_ffn_output_patterns)
    return h

_drawn_inputs = setup_inputs


def setup_inputs(seed=0):
    import zlib

    import numpy as np

    out = dict(_drawn_inputs(seed))
    spreads = {'L0_attn_ln0_w': (1.0, 0.6),
     'L0_attn_ln0_b': (0.0, 0.8),
     'L0_attn_ln1_w': (1.0, 0.2),
     'L0_attn_ln1_b': (0.0, 0.315),
     'L0_attn_qb': (0.0, 0.8),
     'L0_attn_kb': (0.0, 0.8),
     'L0_attn_vb': (0.0, 0.1),
     'L0_attn_b1': (0.0, 0.1),
     'L0_attn_b2': (0.0, 0.1),
     'L0_ffn_router_b': (0.0, 0.1),
     'L0_ffn_gate_up_proj_bias': (0.0, 0.1),
     'L0_ffn_down_proj_bias': (0.0, 0.1)}
    factors = {'L0_attn_qw': 8.0,
     'L0_attn_kw': 5.601,
     'L1_attn_conv_b': 2.909,
     'L1_attn_mem_w1': 8.0,
     'L1_attn_mem_w2': 8.0,
     'L1_attn_eta_w1': 64.0,
     'L1_attn_eta_w2': 64.0,
     'L1_attn_alpha_w1': 64.0,
     'L1_attn_alpha_w2': 42.874,
     'L1_ffn_input_patterns': 8.0,
     'L1_ffn_process_input_weights': 8.0,
     'L1_ffn_process_values': 8.0,
     'L1_ffn_output_input_weights': 8.0,
     'L1_ffn_output_patterns': 8.0}
    for name, (base, spread) in spreads.items():
        noise = np.random.default_rng([zlib.crc32(name.encode()), seed]).standard_normal(out[name].shape)
        drawn = base * np.exp(spread * noise) if base else spread * noise
        out[name] = jnp.asarray(drawn.astype(out[name].dtype))
    for name, factor in factors.items():
        out[name] = (out[name] * factor).astype(out[name].dtype)
    return out
```

```python
import math
from contextlib import ExitStack

import numpy as np

import concourse.bass as bass
from concourse import mybir

F32 = mybir.dt.float32
U32 = mybir.dt.uint32
ALU = mybir.AluOpType
ACT = mybir.ActivationFunctionType
AX = mybir.AxisListType

P = 128
NIMG, CH, IMG_H, IMG_W, PATCH = 64, 3, 176, 208, 16
PW, PH = IMG_H // PATCH, IMG_W // PATCH
NPATCH = PW * PH
L = NPATCH + 1
D = 128
TOK = NIMG * L
HEADS, KDIM = 8, 32
F1 = 512
EXPERTS, INTER = 8, 256
NIN, NPROC, NOUT, DPV = 512, 256, 512, 64
K_IN, K_PROC, K_OUT = 64, 128, 64
EPS = 1e-5
REM = L - P
PAIR = 2 * L
NPAIR = NIMG // 2
CHUNK = 3 * P
NCHUNK = TOK // CHUNK
TAPS = 4
NEG = -3.0e38

C_IDENT, C_CENTER, C_MEAN, C_MEANH, C_BLK, C_NEG1 = 0, 128, 256, 384, 512, 640
C_MASK = 768
C_MASKR = C_MASK + L
C_IOTA = C_MASKR + REM
C_ONES = C_IOTA + 8
C_EPS = C_ONES + L
C_COLS = C_EPS + 3


def constants():
    c = np.zeros((P, C_COLS), np.float32)
    c[:, C_IDENT:C_IDENT + P] = np.eye(P)
    c[:, C_CENTER:C_CENTER + P] = np.eye(P) - 1.0 / D
    c[:, C_MEAN:C_MEAN + P] = 1.0 / D
    c[:, C_MEANH:C_MEANH + P] = 1.0 / (D * HEADS)
    c[:, C_BLK:C_BLK + P] = np.kron(np.eye(P // KDIM), np.ones((KDIM, KDIM)))
    c[:, C_NEG1:C_NEG1 + P] = -1.0
    c[:, C_MASK:C_MASK + L] = np.arange(P)[:, None] <= np.arange(L)[None, :]
    c[:REM, C_MASKR:C_MASKR + REM] = np.arange(REM)[:, None] <= np.arange(REM)[None, :]
    c[:, C_IOTA:C_IOTA + 8] = np.arange(8)[None, :]
    c[:, C_ONES:C_ONES + L] = 1.0
    c[:, C_EPS], c[:, C_EPS + 1], c[:, C_EPS + 2] = EPS, 1.0 + EPS, math.log(1024.0)
    return c


def steps(eng, n, step):
    step(0, 0, 0)
    step(1, 1, 0)
    with eng.Fori(0, (n - 2) // 2) as t:
        step(t * 2 + 2, 0, t + 1)
        step(t * 2 + 3, 1, t + 1)


def both(eng, n, step):
    step(0, 0, b=False)
    step(1, 1)
    with eng.Fori(0, (n - 2) // 2) as t:
        step(t * 2 + 2, 0)
        step(t * 2 + 3, 1)
    step(n, n % 2, a=False)


def at_least(eng, sem, value):
    if not (isinstance(value, int) and value <= 0):
        eng.wait_ge(sem, value)


class Chain:

    def __init__(self, eng, sem, per_step):
        self.eng, self.sem, self.per_step = eng, sem, per_step

    def begin(self, j):
        self.base, self.n = j * self.per_step, 0

    def link(self, instruction):
        self.n += 1
        instruction.then_inc(self.sem, 1)
        self.eng.wait_ge(self.sem, self.base + self.n)

    def end(self):
        assert self.n == self.per_step, (self.n, self.per_step)


class LocalChain:

    def __init__(self, eng, sem):
        self.eng, self.sem = eng, sem

    def begin(self):
        self.n = 0
        self.eng.sem_clear(self.sem)

    def link(self, instruction):
        self.n += 1
        instruction.then_inc(self.sem, 1)
        self.eng.wait_ge(self.sem, self.n)


class Core:

    def __init__(self, nc, ctx, dram):
        self.nc, self.ctx, self.dram = nc, ctx, dram
        self.hT = self.sb("hT", [P, TOK])
        self.const = self.sb("const", [P, C_COLS])
        c = self.const
        self.ident = c[:, C_IDENT:C_IDENT + P]
        self.center = c[:, C_CENTER:C_CENTER + P]
        self.mean = c[:, C_MEAN:C_MEAN + P]
        self.meanh = c[:, C_MEANH:C_MEANH + P]
        self.blk = c[:, C_BLK:C_BLK + P]
        self.neg1 = c[:, C_NEG1:C_NEG1 + P]
        self.mask = c[:, C_MASK:C_MASK + L]
        self.mask_r = c[0:REM, C_MASKR:C_MASKR + REM]
        self.iota = c[:, C_IOTA:C_IOTA + EXPERTS]
        self.ones = c[:, C_ONES:C_ONES + L]
        self.eps = c[:, C_EPS:C_EPS + 1]
        self.one_eps = c[:, C_EPS + 1:C_EPS + 2]
        self.ln1024 = c[:, C_EPS + 2:C_EPS + 3]
        self.dbl = [self.ctx.enter_context(nc.psum_tensor(f"banks{i}", [P, 1024], F32))[:, :] for i in range(4)]
        self.bank = [self.dbl[i // 2][:, 512 * (i % 2):512 * (i % 2 + 1)] for i in range(8)]

    def sb(self, name, shape, ctx=None, dt=F32):
        return (ctx or self.ctx).enter_context(self.nc.sbuf_tensor(name, shape, dt))

    def tiles(self, phase, mem):
        return lambda name, *shape, dt=F32: self.sb(f"{phase}_{name}", list(shape), mem, dt)

    def sem(self, name):
        return self.ctx.enter_context(self.nc.semaphore(name))


def heads(ap, n):
    return ap.rearrange("p (n m) -> p n m", n=n)


def over(ap, n):
    return ap.unsqueeze(1).to_broadcast([ap.shape[0], n, ap.shape[1]])


def embed(core):
    nc, hT, dram = core.nc, core.hT, core.dram
    KP = CH * PATCH
    SHIFT = 64
    KALL = SHIFT + KP
    NBUF = 4
    NG = NIMG // 4
    AREA = PW * IMG_W
    with ExitStack() as mem:
        x = [core.sb(f"x{i}", [P, 2 * AREA], mem) for i in range(NBUF)]
        w = core.sb("tok_w", [P, PATCH // 2 * D], mem)
        pos = core.sb("tok_pos", [P, L], mem)
        cols = core.sb("tok_cols", [P, 2], mem)
        s_clear = core.sem("tok_cleared")
        s_w = core.sem("tok_weights_in")
        s_x = [core.sem(f"tok_x_in{i}") for i in range(NBUF)]
        s_shift = core.sem("tok_shifted")
        s_proj = core.sem("tok_projected")
        s_tok = core.sem("tok_stored")
        images = dram["x"]

        with nc.Block() as block:
            @block.sync
            def _(sp):
                sp.wait_ge(s_clear, 1)
                sp.dma_start(core.const[:, :], dram["const"]).then_inc(s_w, 16)
                sp.dma_start(w[0:KP, :], dram["tok_w"][0:KP, :]).then_inc(s_w, 16)
                sp.dma_start(w[SHIFT:KALL, :], dram["tok_w"][KP:2 * KP, :]).then_inc(s_w, 16)
                sp.dma_start(cols[:, :], dram["tok_cols"]).then_inc(s_w, 16)
                sp.dma_start(pos[:, :], dram["tok_pos"].to_broadcast([P, L])).then_inc(s_w, 16)
                sp.wait_ge(s_clear, 1 + NBUF)

                def step(j, par, k):
                    for s in range(2):
                        buf = 2 * par + s
                        at_least(sp, s_proj, 2 * j - 3 + s)
                        for b in range(2):
                            for c in range(CH):
                                src = images[bass.ds(j * 4 + 2 * s + b, 1), c, :, :]
                                dst = heads(x[buf][PATCH * c:PATCH * (c + 1), b * AREA:(b + 1) * AREA], PW)
                                sp.dma_start(dst, src.rearrange("b (a p) w -> p (b a) w", p=PATCH)
                                             ).then_inc(s_x[buf], 16)

                steps(sp, NG, step)

            @block.gpsimd
            def _(pool):
                nc.gpsimd.memset(w[:, :], 0.0).then_inc(s_clear, 1)
                for buf in range(NBUF):
                    nc.gpsimd.memset(x[buf][:, :], 0.0).then_inc(s_clear, 1)

            @block.scalar
            def _(act):
                def step(j, par, k):
                    for s in range(2):
                        buf = 2 * par + s
                        act.wait_ge(s_x[buf], (k + 1) * 16 * 2 * CH)
                        nc.scalar.copy(x[buf][SHIFT:KALL, 0:2 * AREA - 1],
                                       x[buf][0:KP, 1:2 * AREA]).then_inc(s_shift, 1)

                steps(act, NG, step)

            @block.tensor
            def _(pe):
                pe.wait_ge(s_w, 16 * 5)

                def step(j, par, k):
                    for s in range(2):
                        buf = 2 * par + s
                        pe.wait_ge(s_shift, 2 * j + s + 1)
                        at_least(pe, s_tok, 2 * j - 3 + s)
                        src = x[buf][0:KALL, :].rearrange("p (n w) -> p n w", w=PATCH)
                        for col in range(0, PATCH, 2):
                            mm = nc.tensor.matmul(core.bank[buf][:, 0:2 * NPATCH],
                                                  w[0:KALL, col // 2 * D:(col // 2 + 1) * D], src[:, :, col],
                                                  start=col == 0, stop=col == PATCH - 2)
                        mm.then_inc(s_proj, 1)

                steps(pe, NG, step)

            @block.vector
            def _(dve):
                dve.wait_ge(s_w, 16 * 5)
                nc.vector.tensor_scalar(hT[:, :].rearrange("p (b l) -> p b l", l=L)[:, :, 0],
                                        cols[:, 1:2].to_broadcast([P, NIMG]), pos[:, 0:1], None, ALU.add)

                def step(j, par, k):
                    for s in range(2):
                        buf = 2 * par + s
                        dve.wait_ge(s_proj, 2 * j + s + 1)
                        out = heads(hT[:, bass.ds(j * (4 * L) + s * PAIR, PAIR)], 2)
                        nc.vector.scalar_tensor_tensor(
                            out=out[:, :, 1:L], in0=heads(core.bank[buf][:, 0:2 * NPATCH], 2),
                            scalar=cols[:, 0:1], in1=over(pos[:, 1:L], 2), op0=ALU.add, op1=ALU.add
                        ).then_inc(s_tok, 1)

                steps(dve, NG, step)


def attend(core):
    nc, hT, dram, bank = core.nc, core.hT, core.dram, core.bank
    HD = HEADS * D
    GROUPS = [(0, 3), (3, 6), (6, 8)]
    Z_BANK = [3, 4, 5, 6, 7, 0, 1, 2]
    QK_ORDER = [2, 3, 0, 1]
    CLIP_LO, CLIP_HI = float(np.exp(np.float32(-10))), float(np.exp(np.float32(10)))
    with ExitStack() as mem:
        sb = core.tiles("att", mem)
        w_qk, w_v = sb("w_qk", P, 4 * P), sb("w_v", P, HD)
        w_1, w_2 = sb("w_1", P, HEADS * F1), sb("w_2", P, F1)
        w_1x = sb("w_1x", P, F1)
        cols = sb("cols", P, 35)
        ln0_w, ln0_b, b_qk, b_v = cols[:, 0:1], cols[:, 1:2], cols[:, 2:6], cols[:, 6:14]
        ln1_w, ln1_b = cols[:, 14:22], cols[:, 22:30]
        b_1, b_2 = cols[:, 30:34], cols[:, 34:35]
        square, lnv, rstd = sb("square", P, PAIR), sb("lnv", P, PAIR), sb("rstd", P, PAIR)
        rsq, rstd0, xh, x0 = (sb(n, P, PAIR) for n in ("rsq", "rstd0", "xh", "x0"))
        xn = [sb(f"xn{i}", P, PAIR) for i in range(2)]
        qk, ksum, qc = sb("qk", P, 4 * PAIR), sb("ksum", P, 2 * PAIR), sb("qc", P, 2 * PAIR)
        lnd, rden, qs = sb("lnd", P, 2 * PAIR), sb("rden", P, 2 * PAIR), sb("qs", P, 2 * PAIR)
        xtok, xtok_r = sb("xtok", P, 2 * P), sb("xtok_r", REM, 2 * P)
        sc = [sb(f"scores{i}", P, HEADS * L) for i in range(2)]
        sc_r = [sb(f"scores_r{i}", REM, HEADS * REM) for i in range(2)]
        u = sb("u", P, HEADS * PAIR)
        z = [sb(f"z{i}", P, HEADS * PAIR) for i in range(2)]
        zz = sb("zz", P, HEADS * PAIR)
        z4, z2, z1 = sb("zs4", P, 4 * PAIR), sb("zs2", P, 2 * PAIR), sb("zs1", P, PAIR)
        lnz, rstdz = sb("lnz", P, PAIR), sb("rstdz", P, PAIR)
        hid, r, xr = sb("hid", P, 4 * PAIR), sb("r", P, PAIR), sb("xr", P, PAIR)

        s_w = core.sem("att_weights_in")
        names = ("w1x b1_sum b1 w1_scaled ch sq ssq rstd xn r0 xh x0 qk exp qc den rden qs scores mask tr "
                 "xtok u u_out z z_out zsum mean zc zz var rstdz znorm w1 hid w2 r out dve_a dve_b act_a act_b pool")
        s = {n: core.sem("att_" + n) for n in names.split()}

        with nc.Block() as block:
            @block.sync
            def _(sp):
                for dst, name in ((w_qk, "att_qk"), (w_v, "att_v"), (w_1, "att_w1"), (w_2, "att_w2")):
                    sp.dma_start(dst[:, :], dram[name]).then_inc(s_w, 16)
                sp.dma_start(cols[:, :], dram["att_cols"]).then_inc(s_w, 16)

            @block.gpsimd
            def _(pool):
                chain = Chain(pool, s["pool"], 2)

                def step(j, par, k):
                    chain.begin(j)
                    pool.wait_ge(s["z_out"], 8 * j + 8)
                    zj = z[par]
                    chain.link(nc.gpsimd.tensor_tensor(z4[:, :], zj[:, 0:4 * PAIR], zj[:, 4 * PAIR:], ALU.add))
                    chain.link(nc.gpsimd.tensor_tensor(z2[:, :], z4[:, 0:2 * PAIR], z4[:, 2 * PAIR:], ALU.add))
                    at_least(pool, s["mean"], j)
                    nc.gpsimd.tensor_tensor(z1[:, :], z2[:, 0:PAIR], z2[:, PAIR:], ALU.add).then_inc(s["zsum"], 1)
                    chain.end()

                steps(pool, NPAIR, step)

            @block.tensor
            def _(pe):
                mm = nc.tensor.matmul
                pe.wait_ge(s_w, 16 * 5)
                for f in range(4):
                    for h in range(HEADS):
                        last = mm(bank[0][:, f:f + 1], w_1[:, h * F1 + f * P:h * F1 + (f + 1) * P],
                                  ln1_b[:, h:h + 1], start=h == 0, stop=h == HEADS - 1)
                last.then_inc(s["b1_sum"], 1)

                def mlp1(i, par, f, out):
                    for h in range(HEADS):
                        mm(out[:, 0:PAIR], w_1[:, h * F1 + f * P:h * F1 + (f + 1) * P],
                           z[par][:, h * PAIR:(h + 1) * PAIR], start=h == 0, stop=False)
                    mm(out[:, 0:PAIR], w_1x[:, f * P:(f + 1) * P], xn[par][:, :], start=False, stop=True
                       ).then_inc(s["w1"], 1)

                def step(j, par, a=True, b=True):
                    i, bpar = j - 1, 1 - par
                    if a:
                        at_least(pe, s["z_out"], 8 * j)
                        mm(bank[0][:, 0:PAIR], core.center, hT[:, bass.ds(j * PAIR, PAIR)],
                           start=True, stop=True).then_inc(s["ch"], 1)
                    if b:
                        pe.wait_ge(s["zsum"], i + 1)
                        mm(bank[2][:, 0:PAIR], core.meanh, z1[:, :], start=True, stop=True).then_inc(s["mean"], 1)
                    if a:
                        pe.wait_ge(s["sq"], j + 1)
                        mm(bank[1][:, 0:PAIR], core.mean, square[:, :], start=True, stop=True).then_inc(s["ssq"], 1)
                    if b:
                        pe.wait_ge(s["zz"], i + 1)
                        for h in range(HEADS):
                            last = mm(bank[3][:, 0:PAIR], core.meanh, zz[:, h * PAIR:(h + 1) * PAIR],
                                      start=h == 0, stop=h == HEADS - 1)
                        last.then_inc(s["var"], 1)
                    if a:
                        pe.wait_ge(s["x0"], j + 1)
                        for m in QK_ORDER:
                            mm(bank[4 + m][:, 0:PAIR], w_qk[:, m * P:(m + 1) * P], x0[:, :],
                               start=True, stop=True).then_inc(s["qk"], 1)
                        pe.wait_ge(s["xn"], j + 1)
                        for b_ in range(2):
                            nc.tensor.transpose(bank[1][:, 2 * b_ * P:(2 * b_ + 1) * P],
                                                xn[par][:, b_ * L:b_ * L + P], core.ident)
                            last = nc.tensor.transpose(bank[1][0:REM, (2 * b_ + 1) * P:(2 * b_ + 2) * P],
                                                       xn[par][:, b_ * L + P:(b_ + 1) * L], core.ident)
                        last.then_inc(s["tr"], 1)
                    if b:
                        pe.wait_ge(s["znorm"], i + 1)
                        mlp1(i, bpar, 0, bank[2])
                        mlp1(i, bpar, 1, bank[3])
                    if a:
                        for half in range(2):
                            pe.wait_ge(s["qc"], 2 * j + half + 1)
                            if half:
                                pe.wait_ge(s["xtok"], j + 1)
                            mm(bank[half][:, 0:PAIR], core.blk, qc[:, half * PAIR:(half + 1) * PAIR],
                               start=True, stop=True).then_inc(s["den"], 1)
                    if b:
                        for f in (2, 3):
                            pe.wait_ge(s["hid"], 4 * i + f - 1)
                            mlp1(i, bpar, f, bank[f])
                    if a:
                        pe.wait_ge(s["qs"], 2 * j + 2)
                        for b_ in range(2):
                            if b and b_:
                                pe.wait_ge(s["hid"], 4 * i + 4)
                            for half in range(2):
                                for r_ in range(4):
                                    out = bank[4 * (1 - b_) + r_]
                                    rows = slice(KDIM * r_, KDIM * (r_ + 1))
                                    k0, q0 = (2 + half) * PAIR + b_ * L, half * PAIR + b_ * L
                                    mm(out[:, half * L:(half + 1) * L], qk[rows, k0:k0 + P], qs[rows, q0:q0 + L],
                                       start=True, stop=True)
                                    last = mm(out[0:REM, 2 * L + half * REM:2 * L + (half + 1) * REM],
                                              qk[rows, k0 + P:k0 + L], qs[rows, q0 + P:q0 + L],
                                              start=True, stop=True)
                            last.then_inc(s["scores"], 1)
                    if b:
                        if a:
                            pe.wait_ge(s["mask"], 2 * j + 1)
                        else:
                            pe.wait_ge(s["z_out"], 8 * i + 8)
                        pe.wait_ge(s["hid"], 4 * i + 4)
                        for f in range(4):
                            last = mm(bank[4][:, 0:PAIR], w_2[:, f * P:(f + 1) * P], hid[:, f * PAIR:(f + 1) * PAIR],
                                      start=f == 0, stop=f == 3)
                        last.then_inc(s["w2"], 1)
                    if a:
                        for b_ in range(2):
                            pe.wait_ge(s["mask"], 2 * j + b_ + 1)
                            for g, (h0, h1) in enumerate(GROUPS):
                                out = bank[5 + g if b_ == 0 else g][:, 0:(h1 - h0) * L]
                                mm(out, xtok[:, b_ * P:(b_ + 1) * P], sc[b_][:, h0 * L:h1 * L], start=True, stop=False)
                                mm(heads(out, h1 - h0)[:, :, P:L], xtok_r[:, b_ * P:(b_ + 1) * P],
                                   heads(sc_r[b_][:, h0 * REM:h1 * REM], h1 - h0), start=False, stop=True
                                   ).then_inc(s["u"], 1)
                        pe.wait_ge(s["u_out"], 6 * j + 6)
                        for h in range(HEADS):
                            if b and h == 1:
                                pe.wait_ge(s["r"], i + 1)
                            mm(bank[Z_BANK[h]][:, 0:PAIR], w_v[:, h * D:(h + 1) * D], u[:, h * PAIR:(h + 1) * PAIR],
                               start=True, stop=True).then_inc(s["z"], 1)

                pe.wait_ge(s["w1_scaled"], 1)
                both(pe, NPAIR, step)

            @block.scalar
            def _(act):
                f = nc.scalar.activation
                nc.scalar.preload_act_table_set("natural_log_exp_and_others")
                chain_a, chain_b = Chain(act, s["act_a"], 4), Chain(act, s["act_b"], 1)
                act.wait_ge(s["b1"], 1)

                def hidden(i, fs):
                    for m in fs:
                        act.wait_ge(s["w1"], 4 * i + m + 1)
                        f(hid[:, m * PAIR:(m + 1) * PAIR], bank[2 + m % 2][:, 0:PAIR], ACT.Relu,
                          bias=b_1[:, m:m + 1]).then_inc(s["hid"], 1)

                def step(j, par, a=True, b=True):
                    i = j - 1
                    if a:
                        chain_a.begin(j)
                        act.wait_ge(s["ch"], j + 1)
                        at_least(act, s["ssq"], j)
                        f(square[:, :], bank[0][:, 0:PAIR], ACT.Square).then_inc(s["sq"], 1)
                        act.wait_ge(s["ssq"], j + 1)
                        at_least(act, s["xn"], j)
                        chain_a.link(f(lnv[:, :], bank[1][:, 0:PAIR], ACT.Ln, bias=core.eps))
                        f(rstd[:, :], lnv[:, :], ACT.Exp, scale=-0.5).then_inc(s["rstd"], 1)
                        chain_a.link(f(rsq[:, :], lnv[:, :], ACT.Exp, scale=-1.0))
                        chain_a.link(f(rsq[:, :], rsq[:, :], ACT.Ln, scale=-EPS, bias=core.one_eps))
                        at_least(act, s["xh"], j)
                        f(rstd0[:, :], rsq[:, :], ACT.Exp, scale=-0.5).then_inc(s["r0"], 1)
                    if b:
                        chain_b.begin(i)
                        act.wait_ge(s["zc"], i + 1)
                        at_least(act, s["var"], i)
                        f(zz[:, :], z[1 - par][:, :], ACT.Square).then_inc(s["zz"], 1)
                    if a:
                        act.wait_ge(s["xh"], j + 1)
                        at_least(act, s["qk"], 4 * j)
                        f(x0[:, :], xh[:, :], ACT.Identity, scale=ln0_w, bias=ln0_b).then_inc(s["x0"], 1)
                    if b:
                        act.wait_ge(s["var"], i + 1)
                        at_least(act, s["znorm"], i)
                        chain_b.link(f(lnz[:, :], bank[3][:, 0:PAIR], ACT.Ln, bias=core.eps))
                        f(rstdz[:, :], lnz[:, :], ACT.Exp, scale=-0.5).then_inc(s["rstdz"], 1)
                        chain_b.end()
                    if a:
                        at_least(act, s["scores"], 2 * j)
                        at_least(act, s["qs"], 2 * j)
                        for n, m in enumerate(QK_ORDER):
                            act.wait_ge(s["qk"], 4 * j + n + 1)
                            f(qk[:, m * PAIR:(m + 1) * PAIR], bank[4 + m][:, 0:PAIR], ACT.Exp,
                              bias=b_qk[:, m:m + 1]).then_inc(s["exp"], 1)
                        act.wait_ge(s["tr"], j + 1)
                        at_least(act, s["u"], 6 * j)
                        nc.scalar.copy(heads(xtok[:, :], 2), heads(bank[1][:, :], 2)[:, :, 0:P])
                        nc.scalar.copy(heads(xtok_r[:, :], 2), heads(bank[1][0:REM, :], 2)[:, :, P:2 * P]
                                       ).then_inc(s["xtok"], 1)
                    if b:
                        at_least(act, s["w2"], i)
                        hidden(i, (0, 1))
                    if a:
                        for half in range(2):
                            act.wait_ge(s["den"], 2 * j + half + 1)
                            nx = slice(half * PAIR, (half + 1) * PAIR)
                            ln_den = f(lnd[:, nx], bank[half][:, 0:PAIR], ACT.Ln)
                            if half:
                                chain_a.link(ln_den)
                        f(rden[:, :], lnd[:, :], ACT.Exp, scale=-1.0).then_inc(s["rden"], 1)
                        chain_a.end()
                    if b:
                        hidden(i, (2, 3))
                        act.wait_ge(s["w2"], i + 1)
                        at_least(act, s["out"], i)
                        f(r[:, :], bank[4][:, 0:PAIR], ACT.Relu, bias=b_2[:, 0:1]).then_inc(s["r"], 1)
                    if a:
                        at_least(act, s["w1"], 4 * (j - 1))
                        for h in range(HEADS):
                            act.wait_ge(s["z"], 8 * j + h + 1)
                            f(z[par][:, h * PAIR:(h + 1) * PAIR], bank[Z_BANK[h]][:, 0:PAIR], ACT.Identity,
                              bias=b_v[:, h:h + 1]).then_inc(s["z_out"], 1)

                both(act, NPAIR, step)

            @block.vector
            def _(dve):
                tt, v = nc.vector.tensor_tensor, nc.vector
                dve.wait_ge(s_w, 16 * 5)
                v.tensor_reduce(w_1x[:, :], w_1[:, :].rearrange("p (h f) -> p f h", h=HEADS), AX.X, ALU.add
                                ).then_inc(s["w1x"], 1)
                dve.wait_ge(s["b1_sum"], 1)
                tt(b_1[:, :], b_1[:, :], bank[0][:, 0:4], ALU.add).then_inc(s["b1"], 1)
                dve.wait_ge(s["w1x"], 1)
                tt(heads(w_1[:, :], HEADS), heads(w_1[:, :], HEADS),
                   ln1_w.unsqueeze(2).to_broadcast([P, HEADS, F1]), ALU.mult).then_inc(s["w1_scaled"], 1)
                chain_a, chain_b = Chain(dve, s["dve_a"], 3), Chain(dve, s["dve_b"], 1)

                def step(j, par, a=True, b=True):
                    i, zi = j - 1, z[1 - par]
                    if a:
                        chain_a.begin(j)
                        dve.wait_ge(s["rstd"], j + 1)
                        at_least(dve, s["w1"], 4 * (j - 1))
                        tt(xn[par][:, :], bank[0][:, 0:PAIR], rstd[:, :], ALU.mult).then_inc(s["xn"], 1)
                    if b:
                        chain_b.begin(i)
                        dve.wait_ge(s["mean"], i + 1)
                        tt(heads(zi[:, :], HEADS), heads(zi[:, :], HEADS), over(bank[2][:, 0:PAIR], HEADS),
                           ALU.subtract).then_inc(s["zc"], 1)
                    if a:
                        dve.wait_ge(s["xn"], j + 1)
                        dve.wait_ge(s["r0"], j + 1)
                        at_least(dve, s["x0"], j)
                        tt(xh[:, :], xn[par][:, :], rstd0[:, :], ALU.mult).then_inc(s["xh"], 1)
                    if b:
                        dve.wait_ge(s["rstdz"], i + 1)
                        tt(heads(zi[:, :], HEADS), heads(zi[:, :], HEADS), over(rstdz[:, :], HEADS),
                           ALU.mult).then_inc(s["znorm"], 1)
                    if a:
                        q, kk = qk[:, 0:2 * PAIR], qk[:, 2 * PAIR:4 * PAIR]
                        dve.wait_ge(s["exp"], 4 * j + 2)
                        chain_a.link(v.tensor_scalar(kk, kk, CLIP_HI, CLIP_LO, ALU.min, ALU.max))
                        for n in range(4):
                            run = v.tensor_tensor_scan(ksum[:, n * L:(n + 1) * L], core.ones, kk[:, n * L:(n + 1) * L],
                                                       0.0, ALU.mult, ALU.add)
                        chain_a.link(run)
                        dve.wait_ge(s["exp"], 4 * j + 4)
                        chain_a.link(v.tensor_scalar(q, q, CLIP_HI, CLIP_LO, ALU.min, ALU.max))
                        at_least(dve, s["den"], 2 * j)
                        for half in range(2):
                            nx = slice(half * PAIR, (half + 1) * PAIR)
                            tt(qc[:, nx], q[:, nx], ksum[:, nx], ALU.mult).then_inc(s["qc"], 1)
                        dve.wait_ge(s["rden"], j + 1)
                        at_least(dve, s["scores"], 2 * j)
                        for half in range(2):
                            nx = slice(half * PAIR, (half + 1) * PAIR)
                            tt(qs[:, nx], q[:, nx], rden[:, nx], ALU.mult).then_inc(s["qs"], 1)
                        chain_a.end()
                        for b_ in range(2):
                            dve.wait_ge(s["scores"], 2 * j + b_ + 1)
                            at_least(dve, s["u"], 6 * j - 3 + 3 * b_)
                            for r_ in range(4):
                                src = bank[4 * (1 - b_) + r_]
                                dst = sc[b_][:, :].rearrange("p (a r l) -> p r a l", a=2, r=4)[:, r_]
                                dst_r = sc_r[b_][:, :].rearrange("p (a r l) -> p r a l", a=2, r=4)[:, r_]
                                tt(dst, heads(src[:, 0:2 * L], 2), over(core.mask, 2), ALU.mult)
                                last = tt(dst_r, heads(src[0:REM, 2 * L:2 * L + 2 * REM], 2), over(core.mask_r, 2),
                                          ALU.mult)
                            last.then_inc(s["mask"], 1)
                    if a:
                        for b_ in range(2):
                            at_least(dve, s["z"], 8 * j)
                            for g, (h0, h1) in enumerate(GROUPS):
                                dve.wait_ge(s["u"], 6 * j + 3 * b_ + g + 1)
                                src = bank[5 + g if b_ == 0 else g][:, 0:(h1 - h0) * L]
                                dst = u[:, :].rearrange("p (h b l) -> p h b l", h=HEADS, b=2)[:, h0:h1, b_]
                                v.tensor_copy(dst, heads(src, h1 - h0)).then_inc(s["u_out"], 1)
                    if b:
                        dve.wait_ge(s["r"], i + 1)
                        chain_b.link(tt(xr[:, :], r[:, :], xn[1 - par][:, :], ALU.add))
                        rows = hT[:, bass.ds(i * PAIR, PAIR)]
                        tt(rows, rows, xr[:, :], ALU.add).then_inc(s["out"], 1)
                        chain_b.end()

                both(dve, NPAIR, step)


def experts(core):
    nc, hT, dram, bank = core.nc, core.hT, core.dram, core.bank
    E, NT = EXPERTS, CHUNK // P
    with ExitStack() as mem:
        sb = core.tiles("moe", mem)
        w_up, w_down = sb("w_up", P, E * 4 * P), sb("w_down", P, E * 2 * D)
        router, router_b, down_b, up_b = sb("router", P, E), sb("router_b", P, E), sb("down_b", E, D), sb("up_b", P, 4 * E)
        up_b1 = sb("up_b1", P, 4 * E)
        square, lnv, rstd = sb("square", P, CHUNK), sb("lnv", P, CHUNK), sb("rstd", P, CHUNK)
        xn = [sb(f"xn{i}", P, CHUNK) for i in range(2)]
        logits = sb("logits", P, NT * E)
        top, index = sb("top", P, NT * E), sb("index", P, NT * E, dt=U32)
        chosen = [sb(f"chosen{i}", P, NT * E) for i in range(2)]
        gap = [sb(f"gap{i}", P, NT) for i in range(2)]
        e2, w_a, w_b, pick = sb("e2", P, NT), sb("w_a", P, NT), sb("w_b", P, NT), sb("pick", P, NT * E)
        tokw, tokwT = sb("tokw", P, NT * E), sb("tokwT", E, CHUNK)
        gel = [sb(f"gel{i}", P, CHUNK) for i in range(2)]
        hid = [sb(f"hid{i}", P, 2 * CHUNK) for i in range(2)]
        acc = sb("acc", P, CHUNK)

        s_w = core.sem("moe_weights_in")
        names = ("lnv b1 ch sq ssq rstd xn router gap e2 tokw tokwT_ps tokwT up gelu hid down acc fin out chain_a chain_b")
        s = {n: core.sem("moe_" + n) for n in names.split()}

        with nc.Block() as block:
            @block.sync
            def _(sp):
                for dst, src in ((w_up, dram["moe_up"]), (w_down, dram["moe_down"]), (router, dram["moe_router"]),
                                 (router_b, dram["moe_router_b"].to_broadcast([P, E])),
                                 (down_b, dram["moe_down_b"]), (up_b, dram["moe_up_b"])):
                    sp.dma_start(dst[:, :], src).then_inc(s_w, 16)

            @block.tensor
            def _(pe):
                mm = nc.tensor.matmul
                pe.wait_ge(s_w, 16 * 6)

                def up(i, par, e):
                    for c in range(2):
                        n = 16 * i + 2 * e + c
                        at_least(pe, s["hid"], n - 1)
                        for kind in range(2):
                            m = 4 * e + 2 * kind + c
                            last = mm(bank[2 * c + kind][:, 0:CHUNK], w_up[:, m * P:(m + 1) * P], xn[par][:, :],
                                      start=True, stop=True)
                        last.then_inc(s["up"], 1)

                def down(i, e):
                    pe.wait_ge(s["hid"], 16 * i + 2 * e + 2)
                    at_least(pe, s["acc"], 8 * i + e - 1)
                    for t in range(NT):
                        for c in range(2):
                            last = mm(bank[4 + e % 2][:, t * P:(t + 1) * P],
                                      hid[e % 2][:, c * CHUNK + t * P:c * CHUNK + (t + 1) * P],
                                      w_down[:, (2 * e + c) * D:(2 * e + c + 1) * D], start=c == 0, stop=c == 1)
                    last.then_inc(s["down"], 1)

                def step(j, par, a=True, b=True):
                    i, bpar = j - 1, 1 - par
                    if a:
                        at_least(pe, s["out"], j - 1)
                        mm(bank[6][:, 0:CHUNK], core.center, hT[:, bass.ds(j * CHUNK, CHUNK)],
                           start=True, stop=True).then_inc(s["ch"], 1)
                    if b:
                        up(i, bpar, 0)
                    if a:
                        pe.wait_ge(s["sq"], j + 1)
                        at_least(pe, s["tokwT"], j - 1)
                        at_least(pe, s["gap"], j)
                        mm(bank[7][:, 0:CHUNK], core.mean, square[:, :], start=True, stop=True).then_inc(s["ssq"], 1)
                    if b:
                        for e in range(1, 4):
                            up(i, bpar, e)
                            down(i, e - 1)
                    if a:
                        pe.wait_ge(s["xn"], j + 1)
                        for t in range(NT):
                            last = mm(bank[7][:, t * E:(t + 1) * E], xn[par][:, t * P:(t + 1) * P], router[:, :],
                                      start=True, stop=True)
                        last.then_inc(s["router"], 1)
                    if b:
                        for e in range(4, E):
                            up(i, bpar, e)
                            down(i, e - 1)
                            if e == 4:
                                pe.wait_ge(s["tokw"], i + 1)
                                if a:
                                    pe.wait_ge(s["gap"], j + 1)
                                for t in range(NT):
                                    last = nc.tensor.transpose(bank[7][0:E, P + t * P:P + (t + 1) * P],
                                                               tokw[:, t * E:(t + 1) * E], core.ident)
                                last.then_inc(s["tokwT_ps"], 1)
                        down(i, E - 1)
                        pe.wait_ge(s["tokwT"], i + 1)
                        if not a:
                            pe.wait_ge(s["out"], i)
                        mm(bank[6][:, 0:CHUNK], down_b[:, :], tokwT[:, :], start=True, stop=False)
                        pe.wait_ge(s["acc"], 8 * i + 8)
                        for t in range(NT):
                            last = mm(bank[6][:, t * P:(t + 1) * P], acc[:, t * P:(t + 1) * P], core.ident,
                                      start=False, stop=t == NT - 1)
                        last.then_inc(s["fin"], 1)

                both(pe, NCHUNK, step)

            @block.scalar
            def _(act):
                f = nc.scalar.activation
                act.wait_ge(s_w, 16 * 6)

                def gelu(i, e, c):
                    n = 16 * i + 2 * e + c
                    act.wait_ge(s["up"], n + 1)
                    at_least(act, s["hid"], n - 1)
                    f(gel[c][:, :], bank[2 * c][:, 0:CHUNK], ACT.Gelu_apprx_sigmoid,
                      bias=up_b[:, 4 * e + c:4 * e + c + 1]).then_inc(s["gelu"], 1)

                def step(j, par, a=True, b=True):
                    i = j - 1
                    if a:
                        act.wait_ge(s["ch"], j + 1)
                        at_least(act, s["ssq"], j)
                        f(square[:, :], bank[6][:, 0:CHUNK], ACT.Square).then_inc(s["sq"], 1)
                    if b:
                        gelu(i, 0, 0)
                        gelu(i, 0, 1)
                    nc.scalar.preload_act_table_set("natural_log_exp_and_others")
                    if b:
                        act.wait_ge(s["gap"], i + 1)
                        at_least(act, s["tokw"], i)
                        f(e2[:, :], gap[1 - par][:, :], ACT.Exp).then_inc(s["e2"], 1)
                    if a:
                        act.wait_ge(s["ssq"], j + 1)
                        at_least(act, s["xn"], j)
                        f(lnv[:, :], bank[7][:, 0:CHUNK], ACT.Ln, bias=core.eps).then_inc(s["lnv"], 1)
                        act.wait_ge(s["lnv"], j + 1)
                        f(rstd[:, :], lnv[:, :], ACT.Exp, scale=-0.5).then_inc(s["rstd"], 1)
                    if b:
                        for e in range(1, E):
                            gelu(i, e, 0)
                            gelu(i, e, 1)

                both(act, NCHUNK, step)

            @block.vector
            def _(dve):
                tt, v = nc.vector.tensor_tensor, nc.vector
                dve.wait_ge(s_w, 16 * 6)
                v.tensor_scalar(up_b1[:, :], up_b[:, :], 1.0, None, ALU.add).then_inc(s["b1"], 1)
                dve.wait_ge(s["b1"], 1)
                by_tile = lambda ap: heads(ap[:, :], NT)
                wide = lambda ap: ap.unsqueeze(2).to_broadcast([P, NT, E])
                chain_a, chain_b = LocalChain(dve, s["chain_a"]), Chain(dve, s["chain_b"], 5)

                def hidden(i, e, c):
                    dve.wait_ge(s["gelu"], 16 * i + 2 * e + c + 1)
                    if c == 0:
                        at_least(dve, s["down"], 8 * i + e - 1)
                    m = 4 * e + 2 + c
                    v.scalar_tensor_tensor(out=hid[e % 2][:, c * CHUNK:(c + 1) * CHUNK], in0=bank[2 * c + 1][:, 0:CHUNK],
                                           scalar=up_b1[:, m:m + 1], in1=gel[c][:, :], op0=ALU.add,
                                           op1=ALU.mult).then_inc(s["hid"], 1)

                def add(i, e):
                    dve.wait_ge(s["down"], 8 * i + e + 1)
                    if e:
                        dve.wait_ge(s["acc"], 8 * i + e)
                    else:
                        at_least(dve, s["fin"], i)
                    for t in range(NT):
                        cut, w = slice(t * P, (t + 1) * P), tokw[:, t * E + e:t * E + e + 1]
                        src = bank[4 + e % 2][:, cut]
                        if e:
                            last = v.scalar_tensor_tensor(out=acc[:, cut], in0=src, scalar=w, in1=acc[:, cut],
                                                          op0=ALU.mult, op1=ALU.add)
                        else:
                            last = v.tensor_scalar(acc[:, cut], src, w, None, ALU.mult)
                    last.then_inc(s["acc"], 1)

                def step(j, par, a=True, b=True):
                    i = j - 1
                    if b:
                        hidden(i, 0, 0)
                        hidden(i, 0, 1)
                        first, second = (by_tile(chosen[1 - par])[:, :, n] for n in range(2))
                        chain_b.begin(i)
                        dve.wait_ge(s["e2"], i + 1)
                        chain_b.link(v.tensor_scalar(w_a[:, :], e2[:, :], 1.0, None, ALU.add))
                        chain_b.link(v.reciprocal(w_a[:, :], w_a[:, :]))
                        chain_b.link(tt(w_b[:, :], w_a[:, :], e2[:, :], ALU.mult))
                        at_least(dve, s["tokwT_ps"], i)
                        tt(by_tile(tokw), over(core.iota, NT), wide(first), ALU.is_equal)
                        chain_b.link(tt(by_tile(pick), over(core.iota, NT), wide(second), ALU.is_equal))
                        tt(by_tile(tokw), by_tile(tokw), wide(w_a[:, :]), ALU.mult)
                        chain_b.link(tt(by_tile(pick), by_tile(pick), wide(w_b[:, :]), ALU.mult))
                        tt(tokw[:, :], tokw[:, :], pick[:, :], ALU.add).then_inc(s["tokw"], 1)
                        dve.wait_ge(s["tokw"], i + 1)
                        chain_b.end()
                    if a:
                        dve.wait_ge(s["rstd"], j + 1)
                        at_least(dve, s["up"], 16 * (j - 1))
                        tt(xn[par][:, :], bank[6][:, 0:CHUNK], rstd[:, :], ALU.mult).then_inc(s["xn"], 1)
                    if b:
                        for e in range(1, 4):
                            hidden(i, e, 0)
                            hidden(i, e, 1)
                            add(i, e - 1)
                    if a:
                        chain_a.begin()
                        dve.wait_ge(s["router"], j + 1)
                        chain_a.link(tt(by_tile(logits), heads(bank[7][:, 0:NT * E], NT), over(router_b[:, :], NT), ALU.add))
                        for t in range(NT):
                            last = v.max(top[:, t * E:(t + 1) * E], logits[:, t * E:(t + 1) * E])
                        chain_a.link(last)
                        for t in range(NT):
                            last = v.max_index(index[:, t * E:(t + 1) * E], top[:, t * E:(t + 1) * E],
                                               logits[:, t * E:(t + 1) * E])
                        chain_a.link(last)
                        v.tensor_copy(chosen[par][:, :], index[:, :])
                        tt(gap[par][:, :], by_tile(top)[:, :, 1], by_tile(top)[:, :, 0], ALU.subtract
                           ).then_inc(s["gap"], 1)
                    if b:
                        for e in range(4, E):
                            hidden(i, e, 0)
                            hidden(i, e, 1)
                            add(i, e - 1)
                            if e == 4:
                                dve.wait_ge(s["tokwT_ps"], i + 1)
                                at_least(dve, s["fin"], i)
                                v.tensor_copy(tokwT[:, :], bank[7][0:E, P:P + CHUNK]).then_inc(s["tokwT"], 1)
                        add(i, E - 1)
                        dve.wait_ge(s["fin"], i + 1)
                        rows = hT[:, bass.ds(i * CHUNK, CHUNK)]
                        tt(rows, rows, bank[6][:, 0:CHUNK], ALU.add).then_inc(s["out"], 1)

                both(dve, NCHUNK, step)


QUAD = 4 * L
NQUAD = NIMG // 4


def halves(double_bank):
    return heads(double_bank, 2)[:, :, 0:PAIR]


def images(double_bank):
    return double_bank.rearrange("p (h x) -> p h x", h=2)[:, :, 0:PAIR].rearrange("p h (b l) -> p h b l", b=2)


def project(core, out, lhsT, rhs, start=True, stop=True):
    for half in range(2):
        last = core.nc.tensor.matmul(out[:, 512 * half:512 * half + PAIR], lhsT, rhs(half), start=start, stop=stop)
    return last


def quad(tile, j):
    return tile[:, bass.ds(j * QUAD, QUAD)]


def half_of(tile, j=None):
    if j is None:
        return lambda half: tile[:, half * PAIR:(half + 1) * PAIR]
    return lambda half: tile[:, bass.ds(j * QUAD + half * PAIR, PAIR)]


def convolve(core, res):
    nc, hT, dram, dbl = core.nc, core.hT, core.dram, core.dbl
    PAD = TAPS - 1
    with ExitStack() as mem:
        sb = core.tiles("conv", mem)
        taps = sb("taps", P, TAPS + 1)
        padded = sb("padded", P, 4 * (L + PAD))
        square, lnv, rstd = sb("square", P, QUAD), sb("lnv", P, QUAD), sb("rstd", P, QUAD)
        qsq, qss, lnq, rnorm = sb("qsq", P, QUAD), sb("qss", P, QUAD), sb("lnq", P, QUAD), sb("rnorm", P, QUAD)
        s_w = core.sem("conv_weights_in")
        s = {n: core.sem("conv_" + n) for n in
             "pad ch sq ssq rstd xn x q qsq qss bounded rnorm qn dve_a act_a act_b".split()}

        with nc.Block() as block:
            @block.sync
            def _(sp):
                sp.dma_start(taps[:, :], dram["mem_conv"]).then_inc(s_w, 16)
                sp.dma_start(res["w"][:, :], dram["mem_w"]).then_inc(s_w, 16)

            @block.gpsimd
            def _(pool):
                nc.gpsimd.memset(padded[:, :], 0.0).then_inc(s["pad"], 1)

            @block.tensor
            def _(pe):
                pe.wait_ge(s_w, 16 * 2)

                def step(j, par, a=True, b=True):
                    i = j - 1
                    if a:
                        at_least(pe, s["xn"], j)
                        project(core, dbl[0], core.center, half_of(hT, j)).then_inc(s["ch"], 1)
                    if b:
                        pe.wait_ge(s["x"], i + 1)
                        at_least(pe, s["qn"], i)
                        project(core, dbl[2], res["w"][:, 0:P], half_of(res["x"], i)).then_inc(s["q"], 1)
                    if a:
                        pe.wait_ge(s["sq"], j + 1)
                        at_least(pe, s["rstd"], j)
                        project(core, dbl[1], core.mean, half_of(square)).then_inc(s["ssq"], 1)
                    if b:
                        pe.wait_ge(s["qsq"], i + 1)
                        at_least(pe, s["bounded"], i)
                        project(core, dbl[3], core.mean, half_of(qsq)).then_inc(s["qss"], 1)

                both(pe, NQUAD, step)

            @block.scalar
            def _(act):
                f = nc.scalar.activation
                nc.scalar.preload_act_table_set("natural_log_exp_and_others")
                chain_a, chain_b = Chain(act, s["act_a"], 1), Chain(act, s["act_b"], 1)

                def step(j, par, a=True, b=True):
                    i = j - 1
                    if a:
                        act.wait_ge(s["ch"], j + 1)
                        at_least(act, s["ssq"], j)
                        f(heads(square[:, :], 2), halves(dbl[0]), ACT.Square).then_inc(s["sq"], 1)
                    if b:
                        act.wait_ge(s["q"], i + 1)
                        at_least(act, s["qss"], i)
                        f(heads(qsq[:, :], 2), halves(dbl[2]), ACT.Square).then_inc(s["qsq"], 1)
                    if a:
                        chain_a.begin(j)
                        act.wait_ge(s["ssq"], j + 1)
                        at_least(act, s["xn"], j)
                        chain_a.link(f(heads(lnv[:, :], 2), halves(dbl[1]), ACT.Ln, bias=core.eps))
                        f(rstd[:, :], lnv[:, :], ACT.Exp, scale=-0.5).then_inc(s["rstd"], 1)
                    if b:
                        chain_b.begin(i)
                        act.wait_ge(s["bounded"], i + 1)
                        at_least(act, s["qn"], i)
                        chain_b.link(f(lnq[:, :], qss[:, :], ACT.Ln, scale=float(D * 2 ** 20)))
                        f(rnorm[:, :], lnq[:, :], ACT.Exp, scale=-0.5, bias=core.ln1024).then_inc(s["rnorm"], 1)

                both(act, NQUAD, step)

            @block.vector
            def _(dve):
                tt, v = nc.vector.tensor_tensor, nc.vector
                dve.wait_ge(s_w, 16 * 2)
                dve.wait_ge(s["pad"], 1)
                chain_a = Chain(dve, s["dve_a"], 3)
                shifted = lambda t: heads(padded[:, :], 4)[:, :, t:t + L]

                def step(j, par, a=True, b=True):
                    i = j - 1
                    if a:
                        chain_a.begin(j)
                        dve.wait_ge(s["rstd"], j + 1)
                        tt(heads(padded[:, :], 4)[:, :, PAD:].rearrange("p (h b) l -> p h b l", h=2), images(dbl[0]),
                           rstd[:, :].rearrange("p (h b l) -> p h b l", h=2, b=2), ALU.mult).then_inc(s["xn"], 1)
                    if b:
                        dve.wait_ge(s["qss"], i + 1)
                        at_least(dve, s["rnorm"], i)
                        v.tensor_scalar(heads(qss[:, :], 2), halves(dbl[3]), 1e-24 / D, None, ALU.max
                                        ).then_inc(s["bounded"], 1)
                    if a:
                        out = heads(quad(res["x"], j), 4)
                        dve.wait_ge(s["xn"], j + 1)
                        chain_a.link(v.tensor_scalar(out, shifted(0), taps[:, 0:1], taps[:, TAPS:TAPS + 1],
                                                     ALU.mult, ALU.add))
                        for t in range(1, TAPS):
                            conv = v.scalar_tensor_tensor(out=out, in0=shifted(t), scalar=taps[:, t:t + 1], in1=out,
                                                          op0=ALU.mult, op1=ALU.add)
                            if t < TAPS - 1:
                                chain_a.link(conv)
                        conv.then_inc(s["x"], 1)
                        chain_a.end()
                    if b:
                        dve.wait_ge(s["rnorm"], i + 1)
                        tt(heads(quad(res["q"], i), 2), halves(dbl[2]), heads(rnorm[:, :], 2), ALU.mult
                           ).then_inc(s["qn"], 1)

                both(dve, NQUAD, step)


def gates(core, res):
    nc, dbl = core.nc, core.dbl
    with ExitStack() as mem:
        sb = core.tiles("gate", mem)
        g = [[sb(f"g{n}{par}", P, QUAD) for par in range(2)] for n in range(2)]
        pre = [sb(f"pre{n}", P, QUAD) for n in range(2)]
        th = [sb(f"tanh{n}", P, QUAD) for n in range(2)]
        total = [sb(f"total{n}", P, QUAD) for n in range(2)]
        two = [sb(f"two{n}", P, PAIR) for n in range(2)]
        one = [sb(f"one{n}", P, L) for n in range(2)]
        eta, alpha, zeros = sb("eta", P, L), sb("alpha", P, L), sb("zeros", P, L)
        s = {n: core.sem("gate_" + n) for n in "hid gelu out pre tanh sum clear fold mean read scan".split()}
        w = lambda n, layer: res["w"][:, (1 + 2 * n + layer) * P:(2 + 2 * n + layer) * P]

        with nc.Block() as block:
            @block.tensor
            def _(pe):
                def step(j, par, a=True, b=True):
                    i = j - 1
                    if a:
                        for n in range(2):
                            at_least(pe, s["gelu"], 2 * (j - 1) + n + 1)
                            project(core, dbl[n], w(n, 0), half_of(res["x"], j)).then_inc(s["hid"], 1)
                    if b:
                        for n in range(2):
                            pe.wait_ge(s["gelu"], 2 * i + n + 1)
                            at_least(pe, s["pre"], 2 * (i - 1) + n + 1)
                            project(core, dbl[2 + n], w(n, 1), half_of(g[n][1 - par])).then_inc(s["out"], 1)

                both(pe, NQUAD, step)
                for n in range(2):
                    pe.wait_ge(s["fold"], 2 * n + 2)
                    nc.tensor.matmul(core.bank[n][:, 0:L], core.mean, one[n][:, :], start=True, stop=True
                                     ).then_inc(s["mean"], 1)

            @block.scalar
            def _(act):
                f = nc.scalar.activation
                nc.scalar.preload_act_table_set("gelu_and_others")

                def step(j, par, a=True, b=True):
                    i = j - 1
                    if a:
                        for n in range(2):
                            act.wait_ge(s["hid"], 2 * j + n + 1)
                            at_least(act, s["out"], 2 * (j - 2) + n + 1)
                            f(heads(g[n][par][:, :], 2), halves(dbl[n]), ACT.Gelu).then_inc(s["gelu"], 1)
                    if b:
                        for n in range(2):
                            act.wait_ge(s["pre"], 2 * i + n + 1)
                            at_least(act, s["sum"], 2 * (i - 1) + n + 1)
                            f(th[n][:, :], pre[n][:, :], ACT.Tanh, scale=0.5).then_inc(s["tanh"], 1)

                both(act, NQUAD, step)

            @block.vector
            def _(dve):
                tt, v = nc.vector.tensor_tensor, nc.vector
                v.memset(zeros[:, :], 0.0)
                v.memset(res["decay"][:, 0:1], 1.0)
                v.memset(res["shift"][:, 0:1], 0.0)

                def step(j, par, a=True, b=True):
                    i = j - 1
                    if b:
                        for n in range(2):
                            dve.wait_ge(s["out"], 2 * i + n + 1)
                            at_least(dve, s["tanh"], 2 * (i - 1) + n + 1)
                            tt(heads(pre[n][:, :], 2), halves(dbl[2 + n]), heads(quad(res["x"], i), 2), ALU.add
                               ).then_inc(s["pre"], 1)

                both(dve, NQUAD, step)
                for n in range(2):
                    dve.wait_ge(s["mean"], n + 1)
                v.tensor_scalar(eta[:, :], core.bank[0][:, 0:L], 0.01 * 0.5 / NIMG, 0.01 * 0.5, ALU.mult, ALU.add)
                v.tensor_scalar(alpha[:, :], core.bank[1][:, 0:L], 0.5 / NIMG, 0.5, ALU.mult, ALU.add
                                ).then_inc(s["read"], 1)
                dve.wait_ge(s["read"], 1)
                v.tensor_tensor_scan(res["decay"][:, 1:L], alpha[:, 0:L - 1], zeros[:, 0:L - 1], 1.0, ALU.mult, ALU.add)
                v.tensor_tensor_scan(res["shift"][:, 1:L], alpha[:, 0:L - 1], eta[:, 0:L - 1], 0.0, ALU.mult, ALU.add)

            @block.gpsimd
            def _(pool):
                for n in range(2):
                    nc.gpsimd.memset(total[n][:, :], 0.0).then_inc(s["clear"], 1)
                pool.wait_ge(s["clear"], 2)

                def step(j, par, a=True, b=True):
                    i = j - 1
                    if b:
                        for n in range(2):
                            pool.wait_ge(s["tanh"], 2 * i + n + 1)
                            at_least(pool, s["sum"], 2 * i + n - 1)
                            nc.gpsimd.tensor_tensor(total[n][:, :], total[n][:, :], th[n][:, :], ALU.add
                                                    ).then_inc(s["sum"], 1)

                both(pool, NQUAD, step)
                pool.wait_ge(s["sum"], 2 * NQUAD)
                for n in range(2):
                    nc.gpsimd.tensor_tensor(two[n][:, :], total[n][:, 0:PAIR], total[n][:, PAIR:], ALU.add
                                            ).then_inc(s["fold"], 1)
                    pool.wait_ge(s["fold"], 2 * n + 1)
                    nc.gpsimd.tensor_tensor(one[n][:, :], two[n][:, 0:L], two[n][:, L:], ALU.add
                                            ).then_inc(s["fold"], 1)


def recall(core, res):
    nc, hT, dbl = core.nc, core.hT, core.dbl
    with ExitStack() as mem:
        sb = core.tiles("recall", mem)
        qd, qs = sb("q_decay", P, QUAD), sb("q_shift", P, QUAD)
        gd, gs = sb("g_decay", P, QUAD), sb("g_shift", P, QUAD)
        g = [sb(f"g{i}", P, QUAD) for i in range(2)]
        o = sb("o", P, QUAD)
        s = {n: core.sem("recall_" + n) for n in "q hid gelu g out o stored".split()}
        w = lambda layer: res["w"][:, (5 + layer) * P:(6 + layer) * P]

        with nc.Block() as block:
            @block.tensor
            def _(pe):
                def step(j, par, a=True, b=True):
                    i = j - 1
                    if a:
                        pe.wait_ge(s["q"], j + 1)
                        at_least(pe, s["gelu"], j)
                        for half in range(2):
                            out = dbl[0][:, 512 * half:512 * half + PAIR]
                            nc.tensor.matmul(out, w(0), half_of(qd)(half), start=True, stop=False)
                            last = nc.tensor.matmul(out, core.neg1, half_of(qs)(half), start=False, stop=True)
                        last.then_inc(s["hid"], 1)
                    if b:
                        pe.wait_ge(s["g"], i + 1)
                        at_least(pe, s["o"], i)
                        for half in range(2):
                            out = dbl[1][:, 512 * half:512 * half + PAIR]
                            nc.tensor.matmul(out, w(1), half_of(gd)(half), start=True, stop=False)
                            last = nc.tensor.matmul(out, core.neg1, half_of(gs)(half), start=False, stop=True)
                        last.then_inc(s["out"], 1)

                both(pe, NQUAD, step)

            @block.scalar
            def _(act):
                def step(j, par, a=True, b=True):
                    if a:
                        act.wait_ge(s["hid"], j + 1)
                        at_least(act, s["g"], j - 1)
                        nc.scalar.activation(heads(g[par][:, :], 2), halves(dbl[0]), ACT.Gelu).then_inc(s["gelu"], 1)

                both(act, NQUAD, step)

            @block.vector
            def _(dve):
                tt = nc.vector.tensor_tensor
                by = lambda tile: over(tile[:, :], 4)

                def step(j, par, a=True, b=True):
                    i = j - 1
                    if a:
                        at_least(dve, s["hid"], j)
                        q = heads(quad(res["q"], j), 4)
                        tt(heads(qd[:, :], 4), q, by(res["decay"]), ALU.mult)
                        tt(heads(qs[:, :], 4), q, by(res["shift"]), ALU.mult).then_inc(s["q"], 1)
                    if b:
                        dve.wait_ge(s["gelu"], i + 1)
                        at_least(dve, s["out"], i)
                        gi = heads(g[1 - par][:, :], 4)
                        tt(heads(gd[:, :], 4), gi, by(res["decay"]), ALU.mult)
                        tt(heads(gs[:, :], 4), gi, by(res["shift"]), ALU.mult).then_inc(s["g"], 1)
                        dve.wait_ge(s["out"], i + 1)
                        tt(heads(o[:, :], 2), halves(dbl[1]), heads(quad(res["q"], i), 2), ALU.add).then_inc(s["o"], 1)
                        dve.wait_ge(s["o"], i + 1)
                        tt(quad(hT, i), quad(hT, i), o[:, :], ALU.add).then_inc(s["stored"], 1)

                both(dve, NQUAD, step)


def renorm(core, res):
    nc, hT, dbl = core.nc, core.hT, core.dbl
    with ExitStack() as mem:
        sb = core.tiles("renorm", mem)
        square = [sb(f"square{i}", P, QUAD) for i in range(2)]
        lnv, rstd = sb("lnv", P, QUAD), sb("rstd", P, QUAD)
        s = {n: core.sem("renorm_" + n) for n in "ch sq ssq lnv rstd xn".split()}
        with nc.Block() as block:
            @block.tensor
            def _(pe):
                def step(j, par, a=True, b=True):
                    i = j - 1
                    if a:
                        at_least(pe, s["xn"], j - 1)
                        project(core, dbl[par], core.center, half_of(hT, j)).then_inc(s["ch"], 1)
                    if b:
                        pe.wait_ge(s["sq"], i + 1)
                        at_least(pe, s["rstd"], i - 1)
                        project(core, dbl[3 - par], core.mean, half_of(square[1 - par])).then_inc(s["ssq"], 1)

                both(pe, NQUAD, step)

            @block.scalar
            def _(act):
                f = nc.scalar.activation
                nc.scalar.preload_act_table_set("natural_log_exp_and_others")

                def step(j, par, a=True, b=True):
                    i = j - 1
                    if a:
                        act.wait_ge(s["ch"], j + 1)
                        at_least(act, s["ssq"], j - 1)
                        f(heads(square[par][:, :], 2), halves(dbl[par]), ACT.Square).then_inc(s["sq"], 1)
                    if b:
                        act.wait_ge(s["ssq"], i + 1)
                        at_least(act, s["xn"], i)
                        f(heads(lnv[:, :], 2), halves(dbl[3 - par]), ACT.Ln, bias=core.eps).then_inc(s["lnv"], 1)
                        act.wait_ge(s["lnv"], i + 1)
                        f(rstd[:, :], lnv[:, :], ACT.Exp, scale=-0.5).then_inc(s["rstd"], 1)

                both(act, NQUAD, step)

            @block.vector
            def _(dve):
                def step(j, par, a=True, b=True):
                    i = j - 1
                    if b:
                        dve.wait_ge(s["rstd"], i + 1)
                        nc.vector.tensor_tensor(heads(quad(res["x"], i), 2), halves(dbl[1 - par]), heads(rstd[:, :], 2),
                                                ALU.mult).then_inc(s["xn"], 1)

                both(dve, NQUAD, step)


def memory(core):
    res = {"x": core.sb("x", [P, TOK]), "decay": core.sb("decay", [P, L]), "shift": core.sb("shift", [P, L])}
    core.x = res["x"]
    with ExitStack() as mem:
        res["q"] = core.sb("q", [P, TOK], mem)
        res["w"] = core.sb("mem_w", [P, 7 * P], mem)
        convolve(core, res)
        gates(core, res)
        recall(core, res)
        renorm(core, res)


def patterns(core):
    nc, hT, dram, bank = core.nc, core.hT, core.dram, core.bank
    NT = CHUNK // P
    with ExitStack() as mem:
        sb = core.tiles("pat", mem)
        w_in, w_proc, w_val = sb("w_in", P, NIN), sb("w_proc", P, NIN // P * NPROC), sb("w_val", P, NPROC // P * DPV)
        w_ow, w_out = sb("w_ow", DPV, NOUT), sb("w_out", P, NOUT // P * D)
        xs = [sb(f"xs{i}", P, CHUNK) for i in range(2)]
        hs = [sb(f"hs{i}", P, CHUNK) for i in range(2)]
        act_in = [sb(f"act_in{i}", P, NT * NIN) for i in range(2)]
        act_proc, act_out = sb("act_proc", P, NT * NPROC), sb("act_out", P, NT * NOUT)
        best, top, left = sb("best", P, 8), sb("top", P, 8), sb("left", P, NIN)
        kept_in = [sb(f"kept_in{i}", P, NIN) for i in range(2)]
        kept_out = [sb(f"kept_out{i}", P, NOUT) for i in range(2)]
        keptT, expo = sb("keptT", P, NIN), sb("expo", P, NPROC)
        neg_best, prob, probT = sb("neg_best", P, 1), sb("prob", P, NPROC), sb("probT", P, NPROC)
        carrier = sb("carrier", P, 2)
        psum_, rsum = sb("prob_sum", P, 1), sb("rsum", P, NT)
        aggT, outT = sb("aggT", DPV, P), sb("outT", P, NOUT)
        final = [sb(f"final{i}", P, CHUNK) for i in range(2)]

        s_w = core.sem("pat_weights_in")
        s_dram = [core.sem(f"pat_stored{i}") for i in range(2)]
        names = ("stage act gelu kept_in tr_in keptT proc act_proc best neg_best expo prob tr_prob probT agg aggT "
                 "out act_out kept_out tr_out outT fin final chain")
        s = {n: core.sem("pat_" + n) for n in names.split()}

        def chunks(eng, step):
            step(0, 0, 0)
            step(1, 1, 0)
            with eng.Fori(0, (NCHUNK - 4) // 2) as t:
                step(t * 2 + 2, 0, t + 1)
                step(t * 2 + 3, 1, t + 1)
            step(NCHUNK - 2, 0, NCHUNK // 2 - 1)
            step(NCHUNK - 1, 1, NCHUNK // 2 - 1, ahead=False)

        with nc.Block() as block:
            @block.sync
            def _(sp):
                for dst, name in ((w_in, "pat_in"), (w_proc, "pat_proc"), (w_val, "pat_val"), (w_ow, "pat_ow"),
                                  (w_out, "pat_out")):
                    sp.dma_start(dst[:, :], dram[name]).then_inc(s_w, 16)

                def step(j, par, k, ahead=True):
                    sp.wait_ge(s["final"], NT * (j + 1))
                    rows = dram["out"][bass.ds(j * CHUNK, CHUNK), :].rearrange("(t p) d -> p t d", p=P)
                    sp.dma_start(rows, heads(final[par][:, :], NT)).then_inc(s_dram[par], 16)

                chunks(sp, step)
                for par in range(2):
                    sp.wait_ge(s_dram[par], 16 * (NCHUNK // 2))

            @block.gpsimd
            def _(pool):
                def step(j, par, k, ahead=True):
                    at_least(pool, s["act"], NT * (j - 1))
                    nc.gpsimd.tensor_copy(xs[par][:, :], core.x[:, bass.ds(j * CHUNK, CHUNK)]).then_inc(s["stage"], 1)
                    at_least(pool, s["fin"], NT * (j - 1))
                    nc.gpsimd.tensor_copy(hs[par][:, :], hT[:, bass.ds(j * CHUNK, CHUNK)]).then_inc(s["stage"], 1)

                chunks(pool, step)

            @block.tensor
            def _(pe):
                mm, tr = nc.tensor.matmul, nc.tensor.transpose
                pe.wait_ge(s_w, 16 * 5)

                def first(j, par):
                    pe.wait_ge(s["stage"], 2 * j + 2)
                    for t in range(NT):
                        n = NT * j + t
                        at_least(pe, s["gelu"], n - 1)
                        bk = bank[(NT * par + t) % 2]
                        mm(bk, xs[par][:, t * P:(t + 1) * P], w_in[:, :], start=True, stop=True).then_inc(s["act"], 1)

                def step(j, par, k, ahead=True):
                    for t in range(NT):
                        n = NT * j + t
                        pe.wait_ge(s["kept_in"], n + 1)
                        at_least(pe, s["keptT"], n)
                        for c in range(NIN // P):
                            last = tr(bank[2][:, c * P:(c + 1) * P], kept_in[(NT * par + t) % 2][:, c * P:(c + 1) * P],
                                      core.ident)
                        last.then_inc(s["tr_in"], 1)
                        pe.wait_ge(s["keptT"], n + 1)
                        at_least(pe, s["act_proc"], n)
                        for c in range(NIN // P):
                            last = mm(bank[3][:, 0:NPROC], keptT[:, c * P:(c + 1) * P],
                                      w_proc[:, c * NPROC:(c + 1) * NPROC], start=c == 0, stop=c == NIN // P - 1)
                        last.then_inc(s["proc"], 1)
                    for t in range(NT):
                        n = NT * j + t
                        pe.wait_ge(s["prob"], n + 1)
                        at_least(pe, s["aggT"], n)
                        for c in range(NPROC // P):
                            last = tr(bank[4][:, c * P:(c + 1) * P], prob[:, c * P:(c + 1) * P], core.ident)
                        last.then_inc(s["tr_prob"], 1)
                        pe.wait_ge(s["probT"], n + 1)
                        for c in range(NPROC // P):
                            last = mm(bank[4][0:DPV, NPROC:NPROC + P], w_val[:, c * DPV:(c + 1) * DPV],
                                      probT[:, c * P:(c + 1) * P], start=c == 0, stop=c == NPROC // P - 1)
                        last.then_inc(s["agg"], 1)
                        pe.wait_ge(s["aggT"], n + 1)
                        at_least(pe, s["act_out"], n)
                        mm(bank[5], aggT[:, :], w_ow[:, :], start=True, stop=True).then_inc(s["out"], 1)
                    if ahead:
                        first(j + 1, 1 - par)
                    for t in range(NT):
                        n = NT * j + t
                        pe.wait_ge(s["kept_out"], n + 1)
                        at_least(pe, s["outT"], n)
                        for c in range(NOUT // P):
                            last = tr(bank[6][:, c * P:(c + 1) * P], kept_out[(NT * par + t) % 2][:, c * P:(c + 1) * P],
                                      core.ident)
                        last.then_inc(s["tr_out"], 1)
                        pe.wait_ge(s["outT"], n + 1)
                        at_least(pe, s["final"], n)
                        for c in range(NOUT // P):
                            mm(bank[7][:, 0:D], outT[:, c * P:(c + 1) * P], w_out[:, c * D:(c + 1) * D],
                               start=c == 0, stop=False)
                        mm(bank[7][:, 0:D], hs[par][:, t * P:(t + 1) * P], core.ident, start=False, stop=True
                           ).then_inc(s["fin"], 1)

                first(0, 0)
                chunks(pe, step)

            @block.scalar
            def _(act):
                f = nc.scalar.activation

                def first(j, par):
                    for t in range(NT):
                        n = NT * j + t
                        act.wait_ge(s["act"], n + 1)
                        at_least(act, s["kept_in"], n - NT * 2 + 1)
                        f(act_in[par][:, t * NIN:(t + 1) * NIN], bank[(NT * par + t) % 2], ACT.Gelu
                          ).then_inc(s["gelu"], 1)

                def step(j, par, k, ahead=True):
                    for t in range(NT):
                        n = NT * j + t
                        act.wait_ge(s["tr_in"], n + 1)
                        at_least(act, s["proc"], n)
                        nc.scalar.copy(keptT[:, :], bank[2]).then_inc(s["keptT"], 1)
                        act.wait_ge(s["proc"], n + 1)
                        at_least(act, s["prob"], n - NT + 1)
                        f(act_proc[:, t * NPROC:(t + 1) * NPROC], bank[3][:, 0:NPROC], ACT.Gelu
                          ).then_inc(s["act_proc"], 1)
                    for t in range(NT):
                        n = NT * j + t
                        act.wait_ge(s["best"], n + 1)
                        at_least(act, s["expo"], n)
                        nc.scalar.mul(neg_best[:, :], best[:, 0:1], -1.0).then_inc(s["neg_best"], 1)
                        act.wait_ge(s["neg_best"], n + 1)
                        at_least(act, s["prob"], n)
                        f(expo[:, :], act_proc[:, t * NPROC:(t + 1) * NPROC], ACT.Exp, bias=neg_best[:, 0:1]
                          ).then_inc(s["expo"], 1)
                        act.wait_ge(s["tr_prob"], n + 1)
                        at_least(act, s["agg"], n)
                        nc.scalar.copy(probT[:, :], bank[4][:, 0:NPROC]).then_inc(s["probT"], 1)
                        act.wait_ge(s["agg"], n + 1)
                        at_least(act, s["out"], n)
                        nc.scalar.copy(aggT[:, :], bank[4][0:DPV, NPROC:NPROC + P]).then_inc(s["aggT"], 1)
                        act.wait_ge(s["out"], n + 1)
                        at_least(act, s["kept_out"], n - NT + 1)
                        f(act_out[:, t * NOUT:(t + 1) * NOUT], bank[5], ACT.Gelu, scale=rsum[:, t:t + 1]
                          ).then_inc(s["act_out"], 1)
                    if ahead:
                        first(j + 1, 1 - par)
                    for t in range(NT):
                        n = NT * j + t
                        act.wait_ge(s["tr_out"], n + 1)
                        at_least(act, s["fin"], n)
                        nc.scalar.copy(outT[:, :], bank[6]).then_inc(s["outT"], 1)
                        act.wait_ge(s["fin"], n + 1)
                        at_least(act, s_dram[par], 16 * k)
                        nc.scalar.copy(final[par][:, t * D:(t + 1) * D], bank[7][:, 0:D]).then_inc(s["final"], 1)

                first(0, 0)
                chunks(act, step)

            @block.vector
            def _(dve):
                v = nc.vector
                chain = LocalChain(dve, s["chain"])

                def take(src, width, count, ready, n):
                    dve.wait_ge(ready, n + 1)
                    chain.link(v.memset(carrier[:, 0:1], 0.0))
                    for r in range(0, count, 8):
                        from_ = left[:, 0:width] if r else src
                        chain.link(v.max(top[:, :], from_))
                        chain.link(v.match_replace(left[:, 0:width], top[:, :], from_, NEG))

                def keep(dst, src, width):
                    return v.scalar_tensor_tensor(out=dst, in0=left[:, 0:width], scalar=NEG / 2, in1=src,
                                                  op0=ALU.is_lt, op1=ALU.mult)

                def step(j, par, k, ahead=True):
                    v.memset(carrier[:, 1:2], 0.0)
                    chain.begin()
                    for t in range(NT):
                        n, src = NT * j + t, act_in[par][:, t * NIN:(t + 1) * NIN]
                        take(src, NIN, K_IN, s["gelu"], n)
                        at_least(dve, s["tr_in"], n - 1)
                        keep(kept_in[(NT * par + t) % 2][:, :], src, NIN).then_inc(s["kept_in"], 1)
                        dve.wait_ge(s["kept_in"], n + 1)
                    for t in range(NT):
                        n, src = NT * j + t, act_proc[:, t * NPROC:(t + 1) * NPROC]
                        dve.wait_ge(s["act_proc"], n + 1)
                        at_least(dve, s["neg_best"], n)
                        v.tensor_reduce(best[:, 0:1], src, AX.X, ALU.max).then_inc(s["best"], 1)
                        take(src, NPROC, K_PROC, s["act_proc"], n)
                        dve.wait_ge(s["expo"], n + 1)
                        at_least(dve, s["tr_prob"], n)
                        at_least(dve, s["act_out"], n - NT + 1)
                        chain.link(v.scalar_tensor_tensor(out=prob[:, :], in0=left[:, 0:NPROC], scalar=NEG / 2,
                                                          in1=expo[:, :], op0=ALU.is_lt, op1=ALU.mult,
                                                          accum_out=psum_[:, :]))
                        v.reciprocal(rsum[:, t:t + 1], psum_[:, :]).then_inc(s["prob"], 1)
                        dve.wait_ge(s["prob"], n + 1)
                    for t in range(NT):
                        n, src = NT * j + t, act_out[:, t * NOUT:(t + 1) * NOUT]
                        take(src, NOUT, K_OUT, s["act_out"], n)
                        at_least(dve, s["tr_out"], n - 1)
                        keep(kept_out[(NT * par + t) % 2][:, :], src, NOUT).then_inc(s["kept_out"], 1)
                        dve.wait_ge(s["kept_out"], n + 1)

                chunks(dve, step)


def vit_tower(nc, dram):
    with ExitStack() as ctx:
        core = Core(nc, ctx, dram)
        embed(core)
        attend(core)
        experts(core)
        memory(core)
        patterns(core)


def laid_out(i):
    a = {k: np.asarray(v) for k, v in i.items()}
    col = lambda v: v.reshape(-1, 1)
    stack = lambda *v: np.stack(v, axis=1)
    r = {"x": a["x"], "const": constants()}
    r["tok_w"] = a["L0_tok_W"].reshape(D, PATCH, PATCH, CH).transpose(3, 1, 2, 0)
    r["tok_w"] = np.concatenate([r["tok_w"][:, :, c::2].reshape(CH * PATCH, -1) for c in (0, 1)])
    r["tok_cols"] = stack(a["L0_tok_b"], a["L0_tok_cls_token"].reshape(D))
    r["tok_pos"] = a["L0_tok_pos_emb"].reshape(1, L)
    by_head = lambda w: w.reshape(-1, KDIM, HEADS).transpose(0, 2, 1).reshape(-1, KDIM * HEADS)
    r["att_qk"] = np.concatenate([by_head(a["L0_attn_qw"]), by_head(a["L0_attn_kw"])], axis=1)
    qkb = np.concatenate([by_head(a["L0_attn_qb"]), by_head(a["L0_attn_kb"])], axis=1)
    r["att_v"] = a["L0_attn_vw"].reshape(D, D, HEADS).transpose(0, 2, 1).reshape(D, HEADS * D)
    r["att_w1"] = a["L0_attn_w1"].reshape(D, HEADS * F1)
    r["att_w2"] = a["L0_attn_w2"].reshape(F1 // P, P, D).transpose(1, 0, 2).reshape(P, F1)
    r["att_cols"] = np.concatenate([col(a["L0_attn_ln0_w"]), col(a["L0_attn_ln0_b"]), qkb.reshape(4, P).T,
                                    a["L0_attn_vb"].reshape(D, HEADS), a["L0_attn_ln1_w"], a["L0_attn_ln1_b"],
                                    a["L0_attn_b1"].reshape(F1 // P, P).T, col(a["L0_attn_b2"])], axis=1)
    r["moe_router"] = a["L0_ffn_router_w"]
    r["moe_router_b"] = a["L0_ffn_router_b"].reshape(1, EXPERTS)
    r["moe_up"] = a["L0_ffn_gate_up_proj"].transpose(1, 0, 2).reshape(D, EXPERTS * 2 * INTER)
    r["moe_up_b"] = a["L0_ffn_gate_up_proj_bias"].reshape(EXPERTS * 4, P).T
    r["moe_down"] = a["L0_ffn_down_proj"].reshape(EXPERTS, 2, P, D).transpose(2, 0, 1, 3).reshape(P, EXPERTS * INTER)
    r["moe_down_b"] = a["L0_ffn_down_proj_bias"]
    r["mem_w"] = np.concatenate([a["L1_attn_q_w"].T, a["L1_attn_eta_w1"], a["L1_attn_eta_w2"], a["L1_attn_alpha_w1"],
                                 a["L1_attn_alpha_w2"], a["L1_attn_mem_w1"], a["L1_attn_mem_w2"]], axis=1)
    r["mem_conv"] = np.concatenate([a["L1_attn_conv_w"].reshape(D, TAPS), col(a["L1_attn_conv_b"])], axis=1)
    r["pat_in"] = a["L1_ffn_input_patterns"].T
    r["pat_proc"] = a["L1_ffn_process_input_weights"].T.reshape(NIN // P, P, NPROC).transpose(1, 0, 2).reshape(P, -1)
    r["pat_val"] = a["L1_ffn_process_values"].reshape(NPROC // P, P, DPV).transpose(1, 0, 2).reshape(P, -1)
    r["pat_ow"] = a["L1_ffn_output_input_weights"].T
    r["pat_out"] = a["L1_ffn_output_patterns"].reshape(NOUT // P, P, D).transpose(1, 0, 2).reshape(P, -1)
    return {k: np.ascontiguousarray(v) for k, v in r.items()}


def kernel(**inputs):
    import concourse.bacc as bacc
    from concourse.bass_utils import run_bass_kernel_spmd

    nc = bacc.Bacc("TRN2", target_bir_lowering=False, num_devices=1)
    arrays = laid_out(inputs)
    dram = {k: nc.dram_tensor(f"in_{k}", v.shape, mybir.dt.from_np(v.dtype), kind="ExternalInput").ap()
            for k, v in arrays.items()}
    dram["out"] = nc.dram_tensor("out_tokens", (TOK, D), F32, kind="ExternalOutput").ap()
    vit_tower(nc, dram)
    r = run_bass_kernel_spmd(nc, [{f"in_{k}": v for k, v in arrays.items()}], core_ids=[0])
    return r.results[0]["out_tokens"].reshape(NIMG, L, D)
```

```python
import math
from contextlib import ExitStack

import numpy as np

import concourse.bass as bass
from concourse import mybir

F32 = mybir.dt.float32
U32 = mybir.dt.uint32
ALU = mybir.AluOpType
ACT = mybir.ActivationFunctionType
AX = mybir.AxisListType

P = 128
NIMG, CH, IMG_H, IMG_W, PATCH = 64, 3, 176, 208, 16
PW, PH = IMG_H // PATCH, IMG_W // PATCH
NPATCH = PW * PH
L = NPATCH + 1
D = 128
TOK = NIMG * L
HEADS, KDIM = 8, 32
F1 = 512
EXPERTS, INTER = 8, 256
NIN, NPROC, NOUT, DPV = 512, 256, 512, 64
K_IN, K_PROC, K_OUT = 64, 128, 64
EPS = 1e-5
REM = L - P
PAIR = 2 * L
NPAIR = NIMG // 2
CHUNK = 3 * P
NCHUNK = TOK // CHUNK
TAPS = 4
NEG = -3.0e38

C_IDENT, C_CENTER, C_MEAN, C_MEANH, C_BLK, C_NEG1 = 0, 128, 256, 384, 512, 640
C_MASK = 768
C_MASKR = C_MASK + L
C_IOTA = C_MASKR + REM
C_ONES = C_IOTA + 48
C_EPS = C_ONES + L
C_COLS = C_EPS + 3


def constants():
    c = np.zeros((P, C_COLS), np.float32)
    c[:, C_IDENT:C_IDENT + P] = np.eye(P)
    c[:, C_CENTER:C_CENTER + P] = np.eye(P) - 1.0 / D
    c[:, C_MEAN:C_MEAN + P] = 1.0 / D
    c[:, C_MEANH:C_MEANH + P] = 1.0 / (D * HEADS)
    c[:, C_BLK:C_BLK + P] = np.kron(np.eye(P // KDIM), np.ones((KDIM, KDIM)))
    c[:, C_NEG1:C_NEG1 + P] = -1.0
    c[:, C_MASK:C_MASK + L] = np.arange(P)[:, None] <= np.arange(L)[None, :]
    c[:REM, C_MASKR:C_MASKR + REM] = np.arange(REM)[:, None] <= np.arange(REM)[None, :]
    c[:, C_IOTA:C_IOTA + 48] = np.arange(48)[None, :]
    c[:, C_ONES:C_ONES + L] = 1.0
    c[:, C_EPS], c[:, C_EPS + 1], c[:, C_EPS + 2] = EPS, 1.0 + EPS, math.log(1024.0)
    return c


def steps(eng, n, step):
    step(0, 0, 0)
    step(1, 1, 0)
    with eng.Fori(0, (n - 2) // 2) as t:
        step(t * 2 + 2, 0, t + 1)
        step(t * 2 + 3, 1, t + 1)


def both(eng, n, step):
    step(0, 0, b=False)
    step(1, 1)
    with eng.Fori(0, (n - 2) // 2) as t:
        step(t * 2 + 2, 0)
        step(t * 2 + 3, 1)
    step(n, n % 2, a=False)


def at_least(eng, sem, value):
    if not (isinstance(value, int) and value <= 0):
        eng.wait_ge(sem, value)


class Chain:

    def __init__(self, eng, sem, per_step):
        self.eng, self.sem, self.per_step = eng, sem, per_step

    def begin(self, j):
        self.base, self.n = j * self.per_step, 0

    def link(self, instruction):
        self.n += 1
        instruction.then_inc(self.sem, 1)
        self.eng.wait_ge(self.sem, self.base + self.n)

    def end(self):
        assert self.n == self.per_step, (self.n, self.per_step)


class LocalChain:

    def __init__(self, eng, sem):
        self.eng, self.sem = eng, sem

    def begin(self):
        self.n = 0
        self.eng.sem_clear(self.sem)

    def mark(self, instruction):
        self.n += 1
        instruction.then_inc(self.sem, 1)
        return self.n

    def after(self, count):
        self.eng.wait_ge(self.sem, count)

    def link(self, instruction):
        self.after(self.mark(instruction))


class Core:

    def __init__(self, nc, ctx, dram):
        self.nc, self.ctx, self.dram = nc, ctx, dram
        self.hT = self.sb("hT", [P, TOK])
        self.const = self.sb("const", [P, C_COLS])
        c = self.const
        self.ident = c[:, C_IDENT:C_IDENT + P]
        self.center = c[:, C_CENTER:C_CENTER + P]
        self.mean = c[:, C_MEAN:C_MEAN + P]
        self.meanh = c[:, C_MEANH:C_MEANH + P]
        self.blk = c[:, C_BLK:C_BLK + P]
        self.neg1 = c[:, C_NEG1:C_NEG1 + P]
        self.mask = c[:, C_MASK:C_MASK + L]
        self.mask_r = c[0:REM, C_MASKR:C_MASKR + REM]
        self.iota = c[:, C_IOTA:C_IOTA + EXPERTS]
        self.iota48 = c[:, C_IOTA:C_IOTA + 48]
        self.ones = c[:, C_ONES:C_ONES + L]
        self.eps = c[:, C_EPS:C_EPS + 1]
        self.one_eps = c[:, C_EPS + 1:C_EPS + 2]
        self.ln1024 = c[:, C_EPS + 2:C_EPS + 3]
        self.dbl = [self.ctx.enter_context(nc.psum_tensor(f"banks{i}", [P, 1024], F32))[:, :] for i in range(4)]
        self.bank = [self.dbl[i // 2][:, 512 * (i % 2):512 * (i % 2 + 1)] for i in range(8)]

    def sb(self, name, shape, ctx=None, dt=F32):
        return (ctx or self.ctx).enter_context(self.nc.sbuf_tensor(name, shape, dt))

    def tiles(self, phase, mem):
        return lambda name, *shape, dt=F32: self.sb(f"{phase}_{name}", list(shape), mem, dt)

    def sem(self, name):
        return self.ctx.enter_context(self.nc.semaphore(name))


def heads(ap, n):
    return ap.rearrange("p (n m) -> p n m", n=n)


def over(ap, n):
    return ap.unsqueeze(1).to_broadcast([ap.shape[0], n, ap.shape[1]])


def embed(core):
    nc, hT, dram = core.nc, core.hT, core.dram
    KP = CH * PATCH
    SHIFT = 64
    KALL = SHIFT + KP
    NBUF = 4
    NG = NIMG // 4
    AREA = PW * IMG_W
    with ExitStack() as mem:
        x = [core.sb(f"x{i}", [P, 2 * AREA], mem) for i in range(NBUF)]
        w = core.sb("tok_w", [P, PATCH // 2 * D], mem)
        pos = core.sb("tok_pos", [P, L], mem)
        cols = core.sb("tok_cols", [P, 2], mem)
        s_clear = core.sem("tok_cleared")
        s_w = core.sem("tok_weights_in")
        s_x = [core.sem(f"tok_x_in{i}") for i in range(NBUF)]
        s_shift = core.sem("tok_shifted")
        s_proj = core.sem("tok_projected")
        s_tok = core.sem("tok_stored")
        images = dram["x"]

        with nc.Block() as block:
            @block.sync
            def _(sp):
                sp.wait_ge(s_clear, 1)
                sp.dma_start(core.const[:, :], dram["const"]).then_inc(s_w, 16)
                sp.dma_start(w[0:KP, :], dram["tok_w"][0:KP, :]).then_inc(s_w, 16)
                sp.dma_start(w[SHIFT:KALL, :], dram["tok_w"][KP:2 * KP, :]).then_inc(s_w, 16)
                sp.dma_start(cols[:, :], dram["tok_cols"]).then_inc(s_w, 16)
                sp.dma_start(pos[:, :], dram["tok_pos"].to_broadcast([P, L])).then_inc(s_w, 16)
                sp.wait_ge(s_clear, 1 + NBUF)

                def step(j, par, k):
                    for s in range(2):
                        buf = 2 * par + s
                        at_least(sp, s_proj, 2 * j - 3 + s)
                        for b in range(2):
                            for c in range(CH):
                                src = images[bass.ds(j * 4 + 2 * s + b, 1), c, :, :]
                                dst = heads(x[buf][PATCH * c:PATCH * (c + 1), b * AREA:(b + 1) * AREA], PW)
                                sp.dma_start(dst, src.rearrange("b (a p) w -> p (b a) w", p=PATCH)
                                             ).then_inc(s_x[buf], 16)

                steps(sp, NG, step)

            @block.gpsimd
            def _(pool):
                nc.gpsimd.memset(w[:, :], 0.0).then_inc(s_clear, 1)
                for buf in range(NBUF):
                    nc.gpsimd.memset(x[buf][:, :], 0.0).then_inc(s_clear, 1)

            @block.scalar
            def _(act):
                def step(j, par, k):
                    for s in range(2):
                        buf = 2 * par + s
                        act.wait_ge(s_x[buf], (k + 1) * 16 * 2 * CH)
                        nc.scalar.copy(x[buf][SHIFT:KALL, 0:2 * AREA - 1],
                                       x[buf][0:KP, 1:2 * AREA]).then_inc(s_shift, 1)

                steps(act, NG, step)

            @block.tensor
            def _(pe):
                pe.wait_ge(s_w, 16 * 5)

                def step(j, par, k):
                    for s in range(2):
                        buf = 2 * par + s
                        pe.wait_ge(s_shift, 2 * j + s + 1)
                        at_least(pe, s_tok, 2 * j - 3 + s)
                        src = x[buf][0:KALL, :].rearrange("p (n w) -> p n w", w=PATCH)
                        for col in range(0, PATCH, 2):
                            mm = nc.tensor.matmul(core.bank[buf][:, 0:2 * NPATCH],
                                                  w[0:KALL, col // 2 * D:(col // 2 + 1) * D], src[:, :, col],
                                                  start=col == 0, stop=col == PATCH - 2)
                        mm.then_inc(s_proj, 1)

                steps(pe, NG, step)

            @block.vector
            def _(dve):
                dve.wait_ge(s_w, 16 * 5)
                nc.vector.tensor_scalar(hT[:, :].rearrange("p (b l) -> p b l", l=L)[:, :, 0],
                                        cols[:, 1:2].to_broadcast([P, NIMG]), pos[:, 0:1], None, ALU.add)

                def step(j, par, k):
                    for s in range(2):
                        buf = 2 * par + s
                        dve.wait_ge(s_proj, 2 * j + s + 1)
                        out = heads(hT[:, bass.ds(j * (4 * L) + s * PAIR, PAIR)], 2)
                        nc.vector.scalar_tensor_tensor(
                            out=out[:, :, 1:L], in0=heads(core.bank[buf][:, 0:2 * NPATCH], 2),
                            scalar=cols[:, 0:1], in1=over(pos[:, 1:L], 2), op0=ALU.add, op1=ALU.add
                        ).then_inc(s_tok, 1)

                steps(dve, NG, step)


def attend(core):
    nc, hT, dram, bank = core.nc, core.hT, core.dram, core.bank
    HD = HEADS * D
    GROUPS = [(0, 3), (3, 6), (6, 8)]
    Z_BANK = [3, 4, 5, 6, 7, 0, 1, 2]
    QK_ORDER = [2, 3, 0, 1]
    CLIP_LO, CLIP_HI = float(np.exp(np.float32(-10))), float(np.exp(np.float32(10)))
    with ExitStack() as mem:
        sb = core.tiles("att", mem)
        w_qk, w_v = sb("w_qk", P, 4 * P), sb("w_v", P, HD)
        w_1, w_2 = sb("w_1", P, HEADS * F1), sb("w_2", P, F1)
        w_1x = sb("w_1x", P, F1)
        cols = sb("cols", P, 35)
        ln0_w, ln0_b, b_qk, b_v = cols[:, 0:1], cols[:, 1:2], cols[:, 2:6], cols[:, 6:14]
        ln1_w, ln1_b = cols[:, 14:22], cols[:, 22:30]
        b_1, b_2 = cols[:, 30:34], cols[:, 34:35]
        square, lnv, rstd = sb("square", P, PAIR), sb("lnv", P, PAIR), sb("rstd", P, PAIR)
        rsq, rstd0, xh, x0 = (sb(n, P, PAIR) for n in ("rsq", "rstd0", "xh", "x0"))
        xn = [sb(f"xn{i}", P, PAIR) for i in range(2)]
        qk, ksum, qc = sb("qk", P, 4 * PAIR), sb("ksum", P, 2 * PAIR), sb("qc", P, 2 * PAIR)
        lnd, rden, qs = sb("lnd", P, 2 * PAIR), sb("rden", P, 2 * PAIR), sb("qs", P, 2 * PAIR)
        xtok, xtok_r = sb("xtok", P, 2 * P), sb("xtok_r", REM, 2 * P)
        sc = [sb(f"scores{i}", P, HEADS * L) for i in range(2)]
        sc_r = [sb(f"scores_r{i}", REM, HEADS * REM) for i in range(2)]
        u = sb("u", P, HEADS * PAIR)
        z = [sb(f"z{i}", P, HEADS * PAIR) for i in range(2)]
        zz = sb("zz", P, HEADS * PAIR)
        z4, z2, z1 = sb("zs4", P, 4 * PAIR), sb("zs2", P, 2 * PAIR), sb("zs1", P, PAIR)
        lnz, rstdz = sb("lnz", P, PAIR), sb("rstdz", P, PAIR)
        hid, r, xr = sb("hid", P, 4 * PAIR), sb("r", P, PAIR), sb("xr", P, PAIR)

        s_w = core.sem("att_weights_in")
        names = ("w1x b1_sum b1 w1_scaled ch sq ssq rstd xn r0 xh x0 qk exp qc den rden qs scores mask tr "
                 "xtok u u_out z z_out zsum mean zc zz var rstdz znorm w1 hid w2 r out dve_a dve_b act_a act_b pool")
        s = {n: core.sem("att_" + n) for n in names.split()}

        with nc.Block() as block:
            @block.sync
            def _(sp):
                for dst, name in ((w_qk, "att_qk"), (w_v, "att_v"), (w_1, "att_w1"), (w_2, "att_w2")):
                    sp.dma_start(dst[:, :], dram[name]).then_inc(s_w, 16)
                sp.dma_start(cols[:, :], dram["att_cols"]).then_inc(s_w, 16)

            @block.gpsimd
            def _(pool):
                chain = Chain(pool, s["pool"], 2)

                def step(j, par, k):
                    chain.begin(j)
                    pool.wait_ge(s["z_out"], 8 * j + 8)
                    zj = z[par]
                    chain.link(nc.gpsimd.tensor_tensor(z4[:, :], zj[:, 0:4 * PAIR], zj[:, 4 * PAIR:], ALU.add))
                    chain.link(nc.gpsimd.tensor_tensor(z2[:, :], z4[:, 0:2 * PAIR], z4[:, 2 * PAIR:], ALU.add))
                    at_least(pool, s["mean"], j)
                    nc.gpsimd.tensor_tensor(z1[:, :], z2[:, 0:PAIR], z2[:, PAIR:], ALU.add).then_inc(s["zsum"], 1)
                    chain.end()

                steps(pool, NPAIR, step)

            @block.tensor
            def _(pe):
                mm = nc.tensor.matmul
                pe.wait_ge(s_w, 16 * 5)
                for f in range(4):
                    for h in range(HEADS):
                        last = mm(bank[0][:, f:f + 1], w_1[:, h * F1 + f * P:h * F1 + (f + 1) * P],
                                  ln1_b[:, h:h + 1], start=h == 0, stop=h == HEADS - 1)
                last.then_inc(s["b1_sum"], 1)

                def mlp1(i, par, f, out):
                    for h in range(HEADS):
                        mm(out[:, 0:PAIR], w_1[:, h * F1 + f * P:h * F1 + (f + 1) * P],
                           z[par][:, h * PAIR:(h + 1) * PAIR], start=h == 0, stop=False)
                    mm(out[:, 0:PAIR], w_1x[:, f * P:(f + 1) * P], xn[par][:, :], start=False, stop=True
                       ).then_inc(s["w1"], 1)

                def step(j, par, a=True, b=True):
                    i, bpar = j - 1, 1 - par
                    if a:
                        at_least(pe, s["z_out"], 8 * j)
                        mm(bank[0][:, 0:PAIR], core.center, hT[:, bass.ds(j * PAIR, PAIR)],
                           start=True, stop=True).then_inc(s["ch"], 1)
                    if b:
                        pe.wait_ge(s["zsum"], i + 1)
                        mm(bank[2][:, 0:PAIR], core.meanh, z1[:, :], start=True, stop=True).then_inc(s["mean"], 1)
                    if a:
                        pe.wait_ge(s["sq"], j + 1)
                        mm(bank[1][:, 0:PAIR], core.mean, square[:, :], start=True, stop=True).then_inc(s["ssq"], 1)
                    if b:
                        pe.wait_ge(s["zz"], i + 1)
                        for h in range(HEADS):
                            last = mm(bank[3][:, 0:PAIR], core.meanh, zz[:, h * PAIR:(h + 1) * PAIR],
                                      start=h == 0, stop=h == HEADS - 1)
                        last.then_inc(s["var"], 1)
                    if a:
                        pe.wait_ge(s["x0"], j + 1)
                        for m in QK_ORDER:
                            mm(bank[4 + m][:, 0:PAIR], w_qk[:, m * P:(m + 1) * P], x0[:, :],
                               start=True, stop=True).then_inc(s["qk"], 1)
                        pe.wait_ge(s["xn"], j + 1)
                        for b_ in range(2):
                            nc.tensor.transpose(bank[1][:, 2 * b_ * P:(2 * b_ + 1) * P],
                                                xn[par][:, b_ * L:b_ * L + P], core.ident)
                            last = nc.tensor.transpose(bank[1][0:REM, (2 * b_ + 1) * P:(2 * b_ + 2) * P],
                                                       xn[par][:, b_ * L + P:(b_ + 1) * L], core.ident)
                        last.then_inc(s["tr"], 1)
                    if b:
                        pe.wait_ge(s["znorm"], i + 1)
                        mlp1(i, bpar, 0, bank[2])
                        mlp1(i, bpar, 1, bank[3])
                    if a:
                        for half in range(2):
                            pe.wait_ge(s["qc"], 2 * j + half + 1)
                            if half:
                                pe.wait_ge(s["xtok"], j + 1)
                            mm(bank[half][:, 0:PAIR], core.blk, qc[:, half * PAIR:(half + 1) * PAIR],
                               start=True, stop=True).then_inc(s["den"], 1)
                    if b:
                        for f in (2, 3):
                            pe.wait_ge(s["hid"], 4 * i + f - 1)
                            mlp1(i, bpar, f, bank[f])
                    if a:
                        pe.wait_ge(s["qs"], 2 * j + 2)
                        for b_ in range(2):
                            if b and b_:
                                pe.wait_ge(s["hid"], 4 * i + 4)
                            for half in range(2):
                                for r_ in range(4):
                                    out = bank[4 * (1 - b_) + r_]
                                    rows = slice(KDIM * r_, KDIM * (r_ + 1))
                                    k0, q0 = (2 + half) * PAIR + b_ * L, half * PAIR + b_ * L
                                    mm(out[:, half * L:(half + 1) * L], qk[rows, k0:k0 + P], qs[rows, q0:q0 + L],
                                       start=True, stop=True)
                                    last = mm(out[0:REM, 2 * L + half * REM:2 * L + (half + 1) * REM],
                                              qk[rows, k0 + P:k0 + L], qs[rows, q0 + P:q0 + L],
                                              start=True, stop=True)
                            last.then_inc(s["scores"], 1)
                    if b:
                        if a:
                            pe.wait_ge(s["mask"], 2 * j + 1)
                        else:
                            pe.wait_ge(s["z_out"], 8 * i + 8)
                        pe.wait_ge(s["hid"], 4 * i + 4)
                        for f in range(4):
                            last = mm(bank[4][:, 0:PAIR], w_2[:, f * P:(f + 1) * P], hid[:, f * PAIR:(f + 1) * PAIR],
                                      start=f == 0, stop=f == 3)
                        last.then_inc(s["w2"], 1)
                    if a:
                        for b_ in range(2):
                            pe.wait_ge(s["mask"], 2 * j + b_ + 1)
                            for g, (h0, h1) in enumerate(GROUPS):
                                out = bank[5 + g if b_ == 0 else g][:, 0:(h1 - h0) * L]
                                mm(out, xtok[:, b_ * P:(b_ + 1) * P], sc[b_][:, h0 * L:h1 * L], start=True, stop=False)
                                mm(heads(out, h1 - h0)[:, :, P:L], xtok_r[:, b_ * P:(b_ + 1) * P],
                                   heads(sc_r[b_][:, h0 * REM:h1 * REM], h1 - h0), start=False, stop=True
                                   ).then_inc(s["u"], 1)
                        pe.wait_ge(s["u_out"], 6 * j + 6)
                        for h in range(HEADS):
                            if b and h == 1:
                                pe.wait_ge(s["r"], i + 1)
                            mm(bank[Z_BANK[h]][:, 0:PAIR], w_v[:, h * D:(h + 1) * D], u[:, h * PAIR:(h + 1) * PAIR],
                               start=True, stop=True).then_inc(s["z"], 1)

                pe.wait_ge(s["w1_scaled"], 1)
                both(pe, NPAIR, step)

            @block.scalar
            def _(act):
                f = nc.scalar.activation
                nc.scalar.preload_act_table_set("natural_log_exp_and_others")
                chain_a, chain_b = Chain(act, s["act_a"], 4), Chain(act, s["act_b"], 1)
                act.wait_ge(s["b1"], 1)

                def hidden(i, fs):
                    for m in fs:
                        act.wait_ge(s["w1"], 4 * i + m + 1)
                        f(hid[:, m * PAIR:(m + 1) * PAIR], bank[2 + m % 2][:, 0:PAIR], ACT.Relu,
                          bias=b_1[:, m:m + 1]).then_inc(s["hid"], 1)

                def step(j, par, a=True, b=True):
                    i = j - 1
                    if a:
                        chain_a.begin(j)
                        act.wait_ge(s["ch"], j + 1)
                        at_least(act, s["ssq"], j)
                        f(square[:, :], bank[0][:, 0:PAIR], ACT.Square).then_inc(s["sq"], 1)
                        act.wait_ge(s["ssq"], j + 1)
                        at_least(act, s["xn"], j)
                        chain_a.link(f(lnv[:, :], bank[1][:, 0:PAIR], ACT.Ln, bias=core.eps))
                        f(rstd[:, :], lnv[:, :], ACT.Exp, scale=-0.5).then_inc(s["rstd"], 1)
                        chain_a.link(f(rsq[:, :], lnv[:, :], ACT.Exp, scale=-1.0))
                        chain_a.link(f(rsq[:, :], rsq[:, :], ACT.Ln, scale=-EPS, bias=core.one_eps))
                        at_least(act, s["xh"], j)
                        f(rstd0[:, :], rsq[:, :], ACT.Exp, scale=-0.5).then_inc(s["r0"], 1)
                    if b:
                        chain_b.begin(i)
                        act.wait_ge(s["zc"], i + 1)
                        at_least(act, s["var"], i)
                        f(zz[:, :], z[1 - par][:, :], ACT.Square).then_inc(s["zz"], 1)
                    if a:
                        act.wait_ge(s["xh"], j + 1)
                        at_least(act, s["qk"], 4 * j)
                        f(x0[:, :], xh[:, :], ACT.Identity, scale=ln0_w, bias=ln0_b).then_inc(s["x0"], 1)
                    if b:
                        act.wait_ge(s["var"], i + 1)
                        at_least(act, s["znorm"], i)
                        chain_b.link(f(lnz[:, :], bank[3][:, 0:PAIR], ACT.Ln, bias=core.eps))
                        f(rstdz[:, :], lnz[:, :], ACT.Exp, scale=-0.5).then_inc(s["rstdz"], 1)
                        chain_b.end()
                    if a:
                        at_least(act, s["scores"], 2 * j)
                        at_least(act, s["qs"], 2 * j)
                        for n, m in enumerate(QK_ORDER):
                            act.wait_ge(s["qk"], 4 * j + n + 1)
                            f(qk[:, m * PAIR:(m + 1) * PAIR], bank[4 + m][:, 0:PAIR], ACT.Exp,
                              bias=b_qk[:, m:m + 1]).then_inc(s["exp"], 1)
                        act.wait_ge(s["tr"], j + 1)
                        at_least(act, s["u"], 6 * j)
                        nc.scalar.copy(heads(xtok[:, :], 2), heads(bank[1][:, :], 2)[:, :, 0:P])
                        nc.scalar.copy(heads(xtok_r[:, :], 2), heads(bank[1][0:REM, :], 2)[:, :, P:2 * P]
                                       ).then_inc(s["xtok"], 1)
                    if b:
                        at_least(act, s["w2"], i)
                        hidden(i, (0, 1))
                    if a:
                        for half in range(2):
                            act.wait_ge(s["den"], 2 * j + half + 1)
                            nx = slice(half * PAIR, (half + 1) * PAIR)
                            ln_den = f(lnd[:, nx], bank[half][:, 0:PAIR], ACT.Ln)
                            if half:
                                chain_a.link(ln_den)
                        f(rden[:, :], lnd[:, :], ACT.Exp, scale=-1.0).then_inc(s["rden"], 1)
                        chain_a.end()
                    if b:
                        hidden(i, (2, 3))
                        act.wait_ge(s["w2"], i + 1)
                        at_least(act, s["out"], i)
                        f(r[:, :], bank[4][:, 0:PAIR], ACT.Relu, bias=b_2[:, 0:1]).then_inc(s["r"], 1)
                    if a:
                        at_least(act, s["w1"], 4 * (j - 1))
                        for h in range(HEADS):
                            act.wait_ge(s["z"], 8 * j + h + 1)
                            f(z[par][:, h * PAIR:(h + 1) * PAIR], bank[Z_BANK[h]][:, 0:PAIR], ACT.Identity,
                              bias=b_v[:, h:h + 1]).then_inc(s["z_out"], 1)

                both(act, NPAIR, step)

            @block.vector
            def _(dve):
                tt, v = nc.vector.tensor_tensor, nc.vector
                dve.wait_ge(s_w, 16 * 5)
                v.tensor_reduce(w_1x[:, :], w_1[:, :].rearrange("p (h f) -> p f h", h=HEADS), AX.X, ALU.add
                                ).then_inc(s["w1x"], 1)
                dve.wait_ge(s["b1_sum"], 1)
                tt(b_1[:, :], b_1[:, :], bank[0][:, 0:4], ALU.add).then_inc(s["b1"], 1)
                dve.wait_ge(s["w1x"], 1)
                tt(heads(w_1[:, :], HEADS), heads(w_1[:, :], HEADS),
                   ln1_w.unsqueeze(2).to_broadcast([P, HEADS, F1]), ALU.mult).then_inc(s["w1_scaled"], 1)
                chain_a, chain_b = Chain(dve, s["dve_a"], 3), Chain(dve, s["dve_b"], 1)

                def step(j, par, a=True, b=True):
                    i, zi = j - 1, z[1 - par]
                    if a:
                        chain_a.begin(j)
                        dve.wait_ge(s["rstd"], j + 1)
                        at_least(dve, s["w1"], 4 * (j - 1))
                        tt(xn[par][:, :], bank[0][:, 0:PAIR], rstd[:, :], ALU.mult).then_inc(s["xn"], 1)
                    if b:
                        chain_b.begin(i)
                        dve.wait_ge(s["mean"], i + 1)
                        tt(heads(zi[:, :], HEADS), heads(zi[:, :], HEADS), over(bank[2][:, 0:PAIR], HEADS),
                           ALU.subtract).then_inc(s["zc"], 1)
                    if a:
                        dve.wait_ge(s["xn"], j + 1)
                        dve.wait_ge(s["r0"], j + 1)
                        at_least(dve, s["x0"], j)
                        tt(xh[:, :], xn[par][:, :], rstd0[:, :], ALU.mult).then_inc(s["xh"], 1)
                    if b:
                        dve.wait_ge(s["rstdz"], i + 1)
                        tt(heads(zi[:, :], HEADS), heads(zi[:, :], HEADS), over(rstdz[:, :], HEADS),
                           ALU.mult).then_inc(s["znorm"], 1)
                    if a:
                        q, kk = qk[:, 0:2 * PAIR], qk[:, 2 * PAIR:4 * PAIR]
                        dve.wait_ge(s["exp"], 4 * j + 2)
                        chain_a.link(v.tensor_scalar(kk, kk, CLIP_HI, CLIP_LO, ALU.min, ALU.max))
                        for n in range(4):
                            run = v.tensor_tensor_scan(ksum[:, n * L:(n + 1) * L], core.ones, kk[:, n * L:(n + 1) * L],
                                                       0.0, ALU.mult, ALU.add)
                        chain_a.link(run)
                        dve.wait_ge(s["exp"], 4 * j + 4)
                        chain_a.link(v.tensor_scalar(q, q, CLIP_HI, CLIP_LO, ALU.min, ALU.max))
                        at_least(dve, s["den"], 2 * j)
                        for half in range(2):
                            nx = slice(half * PAIR, (half + 1) * PAIR)
                            tt(qc[:, nx], q[:, nx], ksum[:, nx], ALU.mult).then_inc(s["qc"], 1)
                        dve.wait_ge(s["rden"], j + 1)
                        at_least(dve, s["scores"], 2 * j)
                        for half in range(2):
                            nx = slice(half * PAIR, (half + 1) * PAIR)
                            tt(qs[:, nx], q[:, nx], rden[:, nx], ALU.mult).then_inc(s["qs"], 1)
                        chain_a.end()
                        for b_ in range(2):
                            dve.wait_ge(s["scores"], 2 * j + b_ + 1)
                            at_least(dve, s["u"], 6 * j - 3 + 3 * b_)
                            for r_ in range(4):
                                src = bank[4 * (1 - b_) + r_]
                                dst = sc[b_][:, :].rearrange("p (a r l) -> p r a l", a=2, r=4)[:, r_]
                                dst_r = sc_r[b_][:, :].rearrange("p (a r l) -> p r a l", a=2, r=4)[:, r_]
                                tt(dst, heads(src[:, 0:2 * L], 2), over(core.mask, 2), ALU.mult)
                                last = tt(dst_r, heads(src[0:REM, 2 * L:2 * L + 2 * REM], 2), over(core.mask_r, 2),
                                          ALU.mult)
                            last.then_inc(s["mask"], 1)
                    if a:
                        for b_ in range(2):
                            at_least(dve, s["z"], 8 * j)
                            for g, (h0, h1) in enumerate(GROUPS):
                                dve.wait_ge(s["u"], 6 * j + 3 * b_ + g + 1)
                                src = bank[5 + g if b_ == 0 else g][:, 0:(h1 - h0) * L]
                                dst = u[:, :].rearrange("p (h b l) -> p h b l", h=HEADS, b=2)[:, h0:h1, b_]
                                v.tensor_copy(dst, heads(src, h1 - h0)).then_inc(s["u_out"], 1)
                    if b:
                        dve.wait_ge(s["r"], i + 1)
                        chain_b.link(tt(xr[:, :], r[:, :], xn[1 - par][:, :], ALU.add))
                        rows = hT[:, bass.ds(i * PAIR, PAIR)]
                        tt(rows, rows, xr[:, :], ALU.add).then_inc(s["out"], 1)
                        chain_b.end()

                both(dve, NPAIR, step)


def experts(core):
    nc, hT, dram, bank = core.nc, core.hT, core.dram, core.bank
    E, NT = EXPERTS, CHUNK // P
    with ExitStack() as mem:
        sb = core.tiles("moe", mem)
        w_up, w_down = sb("w_up", P, E * 4 * P), sb("w_down", P, E * 2 * D)
        router, router_b, down_b, up_b = sb("router", P, E), sb("router_b", P, E), sb("down_b", E, D), sb("up_b", P, 4 * E)
        up_b1 = sb("up_b1", P, 4 * E)
        square, lnv, rstd = sb("square", P, CHUNK), sb("lnv", P, CHUNK), sb("rstd", P, CHUNK)
        xn = [sb(f"xn{i}", P, CHUNK) for i in range(2)]
        logits = sb("logits", P, NT * E)
        top, index = sb("top", P, NT * E), sb("index", P, NT * E, dt=U32)
        chosen = [sb(f"chosen{i}", P, NT * E) for i in range(2)]
        gap = [sb(f"gap{i}", P, NT) for i in range(2)]
        e2, w_a, w_b, pick = sb("e2", P, NT), sb("w_a", P, NT), sb("w_b", P, NT), sb("pick", P, NT * E)
        tokw, tokwT = sb("tokw", P, NT * E), sb("tokwT", E, CHUNK)
        gel = [sb(f"gel{i}", P, CHUNK) for i in range(2)]
        hid = [sb(f"hid{i}", P, 2 * CHUNK) for i in range(2)]
        acc = sb("acc", P, CHUNK)

        s_w = core.sem("moe_weights_in")
        names = ("lnv b1 ch sq ssq rstd xn router gap e2 tokw tokwT_ps tokwT up gelu hid down acc fin out chain_a chain_b")
        s = {n: core.sem("moe_" + n) for n in names.split()}

        with nc.Block() as block:
            @block.sync
            def _(sp):
                for dst, src in ((w_up, dram["moe_up"]), (w_down, dram["moe_down"]), (router, dram["moe_router"]),
                                 (router_b, dram["moe_router_b"].to_broadcast([P, E])),
                                 (down_b, dram["moe_down_b"]), (up_b, dram["moe_up_b"])):
                    sp.dma_start(dst[:, :], src).then_inc(s_w, 16)

            @block.tensor
            def _(pe):
                mm = nc.tensor.matmul
                pe.wait_ge(s_w, 16 * 6)

                def up(i, par, e):
                    for c in range(2):
                        n = 16 * i + 2 * e + c
                        at_least(pe, s["hid"], n - 1)
                        for kind in range(2):
                            m = 4 * e + 2 * kind + c
                            last = mm(bank[2 * c + kind][:, 0:CHUNK], w_up[:, m * P:(m + 1) * P], xn[par][:, :],
                                      start=True, stop=True)
                        last.then_inc(s["up"], 1)

                def down(i, e):
                    pe.wait_ge(s["hid"], 16 * i + 2 * e + 2)
                    at_least(pe, s["acc"], 8 * i + e - 1)
                    for t in range(NT):
                        for c in range(2):
                            last = mm(bank[4 + e % 2][:, t * P:(t + 1) * P],
                                      hid[e % 2][:, c * CHUNK + t * P:c * CHUNK + (t + 1) * P],
                                      w_down[:, (2 * e + c) * D:(2 * e + c + 1) * D], start=c == 0, stop=c == 1)
                    last.then_inc(s["down"], 1)

                def step(j, par, a=True, b=True):
                    i, bpar = j - 1, 1 - par
                    if a:
                        at_least(pe, s["out"], j - 1)
                        mm(bank[6][:, 0:CHUNK], core.center, hT[:, bass.ds(j * CHUNK, CHUNK)],
                           start=True, stop=True).then_inc(s["ch"], 1)
                    if b:
                        up(i, bpar, 0)
                    if a:
                        pe.wait_ge(s["sq"], j + 1)
                        at_least(pe, s["tokwT"], j - 1)
                        at_least(pe, s["gap"], j)
                        mm(bank[7][:, 0:CHUNK], core.mean, square[:, :], start=True, stop=True).then_inc(s["ssq"], 1)
                    if b:
                        for e in range(1, 4):
                            up(i, bpar, e)
                            down(i, e - 1)
                    if a:
                        pe.wait_ge(s["xn"], j + 1)
                        for t in range(NT):
                            last = mm(bank[7][:, t * E:(t + 1) * E], xn[par][:, t * P:(t + 1) * P], router[:, :],
                                      start=True, stop=True)
                        last.then_inc(s["router"], 1)
                    if b:
                        for e in range(4, E):
                            up(i, bpar, e)
                            down(i, e - 1)
                            if e == 4:
                                pe.wait_ge(s["tokw"], i + 1)
                                if a:
                                    pe.wait_ge(s["gap"], j + 1)
                                for t in range(NT):
                                    last = nc.tensor.transpose(bank[7][0:E, P + t * P:P + (t + 1) * P],
                                                               tokw[:, t * E:(t + 1) * E], core.ident)
                                last.then_inc(s["tokwT_ps"], 1)
                        down(i, E - 1)
                        pe.wait_ge(s["tokwT"], i + 1)
                        if not a:
                            pe.wait_ge(s["out"], i)
                        mm(bank[6][:, 0:CHUNK], down_b[:, :], tokwT[:, :], start=True, stop=False)
                        pe.wait_ge(s["acc"], 8 * i + 8)
                        for t in range(NT):
                            last = mm(bank[6][:, t * P:(t + 1) * P], acc[:, t * P:(t + 1) * P], core.ident,
                                      start=False, stop=t == NT - 1)
                        last.then_inc(s["fin"], 1)

                both(pe, NCHUNK, step)

            @block.scalar
            def _(act):
                f = nc.scalar.activation
                act.wait_ge(s_w, 16 * 6)

                def gelu(i, e, c):
                    n = 16 * i + 2 * e + c
                    act.wait_ge(s["up"], n + 1)
                    at_least(act, s["hid"], n - 1)
                    f(gel[c][:, :], bank[2 * c][:, 0:CHUNK], ACT.Gelu_apprx_sigmoid,
                      bias=up_b[:, 4 * e + c:4 * e + c + 1]).then_inc(s["gelu"], 1)

                def step(j, par, a=True, b=True):
                    i = j - 1
                    if a:
                        act.wait_ge(s["ch"], j + 1)
                        at_least(act, s["ssq"], j)
                        f(square[:, :], bank[6][:, 0:CHUNK], ACT.Square).then_inc(s["sq"], 1)
                    if b:
                        gelu(i, 0, 0)
                        gelu(i, 0, 1)
                    nc.scalar.preload_act_table_set("natural_log_exp_and_others")
                    if b:
                        act.wait_ge(s["gap"], i + 1)
                        at_least(act, s["tokw"], i)
                        f(e2[:, :], gap[1 - par][:, :], ACT.Exp).then_inc(s["e2"], 1)
                    if a:
                        act.wait_ge(s["ssq"], j + 1)
                        at_least(act, s["xn"], j)
                        f(lnv[:, :], bank[7][:, 0:CHUNK], ACT.Ln, bias=core.eps).then_inc(s["lnv"], 1)
                        act.wait_ge(s["lnv"], j + 1)
                        f(rstd[:, :], lnv[:, :], ACT.Exp, scale=-0.5).then_inc(s["rstd"], 1)
                    if b:
                        for e in range(1, E):
                            gelu(i, e, 0)
                            gelu(i, e, 1)

                both(act, NCHUNK, step)

            @block.vector
            def _(dve):
                tt, v = nc.vector.tensor_tensor, nc.vector
                dve.wait_ge(s_w, 16 * 6)
                v.tensor_scalar(up_b1[:, :], up_b[:, :], 1.0, None, ALU.add).then_inc(s["b1"], 1)
                dve.wait_ge(s["b1"], 1)
                by_tile = lambda ap: heads(ap[:, :], NT)
                wide = lambda ap: ap.unsqueeze(2).to_broadcast([P, NT, E])
                chain_a, chain_b = LocalChain(dve, s["chain_a"]), Chain(dve, s["chain_b"], 5)

                def hidden(i, e, c):
                    dve.wait_ge(s["gelu"], 16 * i + 2 * e + c + 1)
                    if c == 0:
                        at_least(dve, s["down"], 8 * i + e - 1)
                    m = 4 * e + 2 + c
                    v.scalar_tensor_tensor(out=hid[e % 2][:, c * CHUNK:(c + 1) * CHUNK], in0=bank[2 * c + 1][:, 0:CHUNK],
                                           scalar=up_b1[:, m:m + 1], in1=gel[c][:, :], op0=ALU.add,
                                           op1=ALU.mult).then_inc(s["hid"], 1)

                def add(i, e):
                    dve.wait_ge(s["down"], 8 * i + e + 1)
                    if e:
                        dve.wait_ge(s["acc"], 8 * i + e)
                    else:
                        at_least(dve, s["fin"], i)
                    for t in range(NT):
                        cut, w = slice(t * P, (t + 1) * P), tokw[:, t * E + e:t * E + e + 1]
                        src = bank[4 + e % 2][:, cut]
                        if e:
                            last = v.scalar_tensor_tensor(out=acc[:, cut], in0=src, scalar=w, in1=acc[:, cut],
                                                          op0=ALU.mult, op1=ALU.add)
                        else:
                            last = v.tensor_scalar(acc[:, cut], src, w, None, ALU.mult)
                    last.then_inc(s["acc"], 1)

                def step(j, par, a=True, b=True):
                    i = j - 1
                    if b:
                        hidden(i, 0, 0)
                        hidden(i, 0, 1)
                        first, second = (by_tile(chosen[1 - par])[:, :, n] for n in range(2))
                        chain_b.begin(i)
                        dve.wait_ge(s["e2"], i + 1)
                        chain_b.link(v.tensor_scalar(w_a[:, :], e2[:, :], 1.0, None, ALU.add))
                        chain_b.link(v.reciprocal(w_a[:, :], w_a[:, :]))
                        chain_b.link(tt(w_b[:, :], w_a[:, :], e2[:, :], ALU.mult))
                        at_least(dve, s["tokwT_ps"], i)
                        tt(by_tile(tokw), over(core.iota, NT), wide(first), ALU.is_equal)
                        chain_b.link(tt(by_tile(pick), over(core.iota, NT), wide(second), ALU.is_equal))
                        tt(by_tile(tokw), by_tile(tokw), wide(w_a[:, :]), ALU.mult)
                        chain_b.link(tt(by_tile(pick), by_tile(pick), wide(w_b[:, :]), ALU.mult))
                        tt(tokw[:, :], tokw[:, :], pick[:, :], ALU.add).then_inc(s["tokw"], 1)
                        dve.wait_ge(s["tokw"], i + 1)
                        chain_b.end()
                    if a:
                        dve.wait_ge(s["rstd"], j + 1)
                        at_least(dve, s["up"], 16 * (j - 1))
                        tt(xn[par][:, :], bank[6][:, 0:CHUNK], rstd[:, :], ALU.mult).then_inc(s["xn"], 1)
                    if b:
                        for e in range(1, 4):
                            hidden(i, e, 0)
                            hidden(i, e, 1)
                            add(i, e - 1)
                    if a:
                        chain_a.begin()
                        dve.wait_ge(s["router"], j + 1)
                        chain_a.link(tt(by_tile(logits), heads(bank[7][:, 0:NT * E], NT), over(router_b[:, :], NT), ALU.add))
                        for t in range(NT):
                            last = v.max(top[:, t * E:(t + 1) * E], logits[:, t * E:(t + 1) * E])
                        chain_a.link(last)
                        for t in range(NT):
                            last = v.max_index(index[:, t * E:(t + 1) * E], top[:, t * E:(t + 1) * E],
                                               logits[:, t * E:(t + 1) * E])
                        chain_a.link(last)
                        v.tensor_copy(chosen[par][:, :], index[:, :])
                        tt(gap[par][:, :], by_tile(top)[:, :, 1], by_tile(top)[:, :, 0], ALU.subtract
                           ).then_inc(s["gap"], 1)
                    if b:
                        for e in range(4, E):
                            hidden(i, e, 0)
                            hidden(i, e, 1)
                            add(i, e - 1)
                            if e == 4:
                                dve.wait_ge(s["tokwT_ps"], i + 1)
                                at_least(dve, s["fin"], i)
                                v.tensor_copy(tokwT[:, :], bank[7][0:E, P:P + CHUNK]).then_inc(s["tokwT"], 1)
                        add(i, E - 1)
                        dve.wait_ge(s["fin"], i + 1)
                        rows = hT[:, bass.ds(i * CHUNK, CHUNK)]
                        tt(rows, rows, bank[6][:, 0:CHUNK], ALU.add).then_inc(s["out"], 1)

                both(dve, NCHUNK, step)


QUAD = 4 * L
NQUAD = NIMG // 4


def halves(double_bank):
    return heads(double_bank, 2)[:, :, 0:PAIR]


def images(double_bank):
    return double_bank.rearrange("p (h x) -> p h x", h=2)[:, :, 0:PAIR].rearrange("p h (b l) -> p h b l", b=2)


def project(core, out, lhsT, rhs, start=True, stop=True):
    for half in range(2):
        last = core.nc.tensor.matmul(out[:, 512 * half:512 * half + PAIR], lhsT, rhs(half), start=start, stop=stop)
    return last


def quad(tile, j):
    return tile[:, bass.ds(j * QUAD, QUAD)]


def half_of(tile, j=None):
    if j is None:
        return lambda half: tile[:, half * PAIR:(half + 1) * PAIR]
    return lambda half: tile[:, bass.ds(j * QUAD + half * PAIR, PAIR)]


def convolve(core, res):
    nc, hT, dram, dbl = core.nc, core.hT, core.dram, core.dbl
    PAD = TAPS - 1
    with ExitStack() as mem:
        sb = core.tiles("conv", mem)
        taps = sb("taps", P, TAPS + 1)
        padded = sb("padded", P, 4 * (L + PAD))
        square, lnv, rstd = sb("square", P, QUAD), sb("lnv", P, QUAD), sb("rstd", P, QUAD)
        qsq, qss, lnq, rnorm = sb("qsq", P, QUAD), sb("qss", P, QUAD), sb("lnq", P, QUAD), sb("rnorm", P, QUAD)
        s_w = core.sem("conv_weights_in")
        s = {n: core.sem("conv_" + n) for n in
             "pad ch sq ssq rstd xn x q qsq qss bounded rnorm qn dve_a act_a act_b".split()}

        with nc.Block() as block:
            @block.sync
            def _(sp):
                sp.dma_start(taps[:, :], dram["mem_conv"]).then_inc(s_w, 16)
                sp.dma_start(res["w"][:, :], dram["mem_w"]).then_inc(s_w, 16)

            @block.gpsimd
            def _(pool):
                nc.gpsimd.memset(padded[:, :], 0.0).then_inc(s["pad"], 1)

            @block.tensor
            def _(pe):
                pe.wait_ge(s_w, 16 * 2)

                def step(j, par, a=True, b=True):
                    i = j - 1
                    if a:
                        at_least(pe, s["xn"], j)
                        project(core, dbl[0], core.center, half_of(hT, j)).then_inc(s["ch"], 1)
                    if b:
                        pe.wait_ge(s["x"], i + 1)
                        at_least(pe, s["qn"], i)
                        project(core, dbl[2], res["w"][:, 0:P], half_of(res["x"], i)).then_inc(s["q"], 1)
                    if a:
                        pe.wait_ge(s["sq"], j + 1)
                        at_least(pe, s["rstd"], j)
                        project(core, dbl[1], core.mean, half_of(square)).then_inc(s["ssq"], 1)
                    if b:
                        pe.wait_ge(s["qsq"], i + 1)
                        at_least(pe, s["bounded"], i)
                        project(core, dbl[3], core.mean, half_of(qsq)).then_inc(s["qss"], 1)

                both(pe, NQUAD, step)

            @block.scalar
            def _(act):
                f = nc.scalar.activation
                nc.scalar.preload_act_table_set("natural_log_exp_and_others")
                chain_a, chain_b = Chain(act, s["act_a"], 1), Chain(act, s["act_b"], 1)

                def step(j, par, a=True, b=True):
                    i = j - 1
                    if a:
                        act.wait_ge(s["ch"], j + 1)
                        at_least(act, s["ssq"], j)
                        f(heads(square[:, :], 2), halves(dbl[0]), ACT.Square).then_inc(s["sq"], 1)
                    if b:
                        act.wait_ge(s["q"], i + 1)
                        at_least(act, s["qss"], i)
                        f(heads(qsq[:, :], 2), halves(dbl[2]), ACT.Square).then_inc(s["qsq"], 1)
                    if a:
                        chain_a.begin(j)
                        act.wait_ge(s["ssq"], j + 1)
                        at_least(act, s["xn"], j)
                        chain_a.link(f(heads(lnv[:, :], 2), halves(dbl[1]), ACT.Ln, bias=core.eps))
                        f(rstd[:, :], lnv[:, :], ACT.Exp, scale=-0.5).then_inc(s["rstd"], 1)
                    if b:
                        chain_b.begin(i)
                        act.wait_ge(s["bounded"], i + 1)
                        at_least(act, s["qn"], i)
                        chain_b.link(f(lnq[:, :], qss[:, :], ACT.Ln, scale=float(D * 2 ** 20)))
                        f(rnorm[:, :], lnq[:, :], ACT.Exp, scale=-0.5, bias=core.ln1024).then_inc(s["rnorm"], 1)

                both(act, NQUAD, step)

            @block.vector
            def _(dve):
                tt, v = nc.vector.tensor_tensor, nc.vector
                dve.wait_ge(s_w, 16 * 2)
                dve.wait_ge(s["pad"], 1)
                chain_a = Chain(dve, s["dve_a"], 3)
                shifted = lambda t: heads(padded[:, :], 4)[:, :, t:t + L]

                def step(j, par, a=True, b=True):
                    i = j - 1
                    if a:
                        chain_a.begin(j)
                        dve.wait_ge(s["rstd"], j + 1)
                        tt(heads(padded[:, :], 4)[:, :, PAD:].rearrange("p (h b) l -> p h b l", h=2), images(dbl[0]),
                           rstd[:, :].rearrange("p (h b l) -> p h b l", h=2, b=2), ALU.mult).then_inc(s["xn"], 1)
                    if b:
                        dve.wait_ge(s["qss"], i + 1)
                        at_least(dve, s["rnorm"], i)
                        v.tensor_scalar(heads(qss[:, :], 2), halves(dbl[3]), 1e-24 / D, None, ALU.max
                                        ).then_inc(s["bounded"], 1)
                    if a:
                        out = heads(quad(res["x"], j), 4)
                        dve.wait_ge(s["xn"], j + 1)
                        chain_a.link(v.tensor_scalar(out, shifted(0), taps[:, 0:1], taps[:, TAPS:TAPS + 1],
                                                     ALU.mult, ALU.add))
                        for t in range(1, TAPS):
                            conv = v.scalar_tensor_tensor(out=out, in0=shifted(t), scalar=taps[:, t:t + 1], in1=out,
                                                          op0=ALU.mult, op1=ALU.add)
                            if t < TAPS - 1:
                                chain_a.link(conv)
                        conv.then_inc(s["x"], 1)
                        chain_a.end()
                    if b:
                        dve.wait_ge(s["rnorm"], i + 1)
                        tt(heads(quad(res["q"], i), 2), halves(dbl[2]), heads(rnorm[:, :], 2), ALU.mult
                           ).then_inc(s["qn"], 1)

                both(dve, NQUAD, step)


def gates(core, res):
    nc, dbl = core.nc, core.dbl
    with ExitStack() as mem:
        sb = core.tiles("gate", mem)
        g = [[sb(f"g{n}{par}", P, QUAD) for par in range(2)] for n in range(2)]
        pre = [sb(f"pre{n}", P, QUAD) for n in range(2)]
        th = [sb(f"tanh{n}", P, QUAD) for n in range(2)]
        total = [sb(f"total{n}", P, QUAD) for n in range(2)]
        two = [sb(f"two{n}", P, PAIR) for n in range(2)]
        one = [sb(f"one{n}", P, L) for n in range(2)]
        eta, alpha, zeros = sb("eta", P, L), sb("alpha", P, L), sb("zeros", P, L)
        s = {n: core.sem("gate_" + n) for n in "hid gelu out pre tanh sum clear fold mean read scan".split()}
        w = lambda n, layer: res["w"][:, (1 + 2 * n + layer) * P:(2 + 2 * n + layer) * P]

        with nc.Block() as block:
            @block.tensor
            def _(pe):
                def step(j, par, a=True, b=True):
                    i = j - 1
                    if a:
                        for n in range(2):
                            at_least(pe, s["gelu"], 2 * (j - 1) + n + 1)
                            project(core, dbl[n], w(n, 0), half_of(res["x"], j)).then_inc(s["hid"], 1)
                    if b:
                        for n in range(2):
                            pe.wait_ge(s["gelu"], 2 * i + n + 1)
                            at_least(pe, s["pre"], 2 * (i - 1) + n + 1)
                            project(core, dbl[2 + n], w(n, 1), half_of(g[n][1 - par])).then_inc(s["out"], 1)

                both(pe, NQUAD, step)
                for n in range(2):
                    pe.wait_ge(s["fold"], 2 * n + 2)
                    nc.tensor.matmul(core.bank[n][:, 0:L], core.mean, one[n][:, :], start=True, stop=True
                                     ).then_inc(s["mean"], 1)

            @block.scalar
            def _(act):
                f = nc.scalar.activation
                nc.scalar.preload_act_table_set("gelu_and_others")

                def step(j, par, a=True, b=True):
                    i = j - 1
                    if a:
                        for n in range(2):
                            act.wait_ge(s["hid"], 2 * j + n + 1)
                            at_least(act, s["out"], 2 * (j - 2) + n + 1)
                            f(heads(g[n][par][:, :], 2), halves(dbl[n]), ACT.Gelu).then_inc(s["gelu"], 1)
                    if b:
                        for n in range(2):
                            act.wait_ge(s["pre"], 2 * i + n + 1)
                            at_least(act, s["sum"], 2 * (i - 1) + n + 1)
                            f(th[n][:, :], pre[n][:, :], ACT.Tanh, scale=0.5).then_inc(s["tanh"], 1)

                both(act, NQUAD, step)

            @block.vector
            def _(dve):
                tt, v = nc.vector.tensor_tensor, nc.vector
                v.memset(zeros[:, :], 0.0)
                v.memset(res["decay"][:, 0:1], 1.0)
                v.memset(res["shift"][:, 0:1], 0.0)

                def step(j, par, a=True, b=True):
                    i = j - 1
                    if b:
                        for n in range(2):
                            dve.wait_ge(s["out"], 2 * i + n + 1)
                            at_least(dve, s["tanh"], 2 * (i - 1) + n + 1)
                            tt(heads(pre[n][:, :], 2), halves(dbl[2 + n]), heads(quad(res["x"], i), 2), ALU.add
                               ).then_inc(s["pre"], 1)

                both(dve, NQUAD, step)
                for n in range(2):
                    dve.wait_ge(s["mean"], n + 1)
                v.tensor_scalar(eta[:, :], core.bank[0][:, 0:L], 0.01 * 0.5 / NIMG, 0.01 * 0.5, ALU.mult, ALU.add)
                v.tensor_scalar(alpha[:, :], core.bank[1][:, 0:L], 0.5 / NIMG, 0.5, ALU.mult, ALU.add
                                ).then_inc(s["read"], 1)
                dve.wait_ge(s["read"], 1)
                v.tensor_tensor_scan(res["decay"][:, 1:L], alpha[:, 0:L - 1], zeros[:, 0:L - 1], 1.0, ALU.mult, ALU.add)
                v.tensor_tensor_scan(res["shift"][:, 1:L], alpha[:, 0:L - 1], eta[:, 0:L - 1], 0.0, ALU.mult, ALU.add)

            @block.gpsimd
            def _(pool):
                for n in range(2):
                    nc.gpsimd.memset(total[n][:, :], 0.0).then_inc(s["clear"], 1)
                pool.wait_ge(s["clear"], 2)

                def step(j, par, a=True, b=True):
                    i = j - 1
                    if b:
                        for n in range(2):
                            pool.wait_ge(s["tanh"], 2 * i + n + 1)
                            at_least(pool, s["sum"], 2 * i + n - 1)
                            nc.gpsimd.tensor_tensor(total[n][:, :], total[n][:, :], th[n][:, :], ALU.add
                                                    ).then_inc(s["sum"], 1)

                both(pool, NQUAD, step)
                pool.wait_ge(s["sum"], 2 * NQUAD)
                for n in range(2):
                    nc.gpsimd.tensor_tensor(two[n][:, :], total[n][:, 0:PAIR], total[n][:, PAIR:], ALU.add
                                            ).then_inc(s["fold"], 1)
                    pool.wait_ge(s["fold"], 2 * n + 1)
                    nc.gpsimd.tensor_tensor(one[n][:, :], two[n][:, 0:L], two[n][:, L:], ALU.add
                                            ).then_inc(s["fold"], 1)


def recall(core, res):
    nc, hT, dbl = core.nc, core.hT, core.dbl
    with ExitStack() as mem:
        sb = core.tiles("recall", mem)
        qd, qs = sb("q_decay", P, QUAD), sb("q_shift", P, QUAD)
        gd, gs = sb("g_decay", P, QUAD), sb("g_shift", P, QUAD)
        g = [sb(f"g{i}", P, QUAD) for i in range(2)]
        o = sb("o", P, QUAD)
        s = {n: core.sem("recall_" + n) for n in "q hid gelu g out o stored".split()}
        w = lambda layer: res["w"][:, (5 + layer) * P:(6 + layer) * P]

        with nc.Block() as block:
            @block.tensor
            def _(pe):
                def step(j, par, a=True, b=True):
                    i = j - 1
                    if a:
                        pe.wait_ge(s["q"], j + 1)
                        at_least(pe, s["gelu"], j)
                        for half in range(2):
                            out = dbl[0][:, 512 * half:512 * half + PAIR]
                            nc.tensor.matmul(out, w(0), half_of(qd)(half), start=True, stop=False)
                            last = nc.tensor.matmul(out, core.neg1, half_of(qs)(half), start=False, stop=True)
                        last.then_inc(s["hid"], 1)
                    if b:
                        pe.wait_ge(s["g"], i + 1)
                        at_least(pe, s["o"], i)
                        for half in range(2):
                            out = dbl[1][:, 512 * half:512 * half + PAIR]
                            nc.tensor.matmul(out, w(1), half_of(gd)(half), start=True, stop=False)
                            last = nc.tensor.matmul(out, core.neg1, half_of(gs)(half), start=False, stop=True)
                        last.then_inc(s["out"], 1)

                both(pe, NQUAD, step)

            @block.scalar
            def _(act):
                def step(j, par, a=True, b=True):
                    if a:
                        act.wait_ge(s["hid"], j + 1)
                        at_least(act, s["g"], j - 1)
                        nc.scalar.activation(heads(g[par][:, :], 2), halves(dbl[0]), ACT.Gelu).then_inc(s["gelu"], 1)

                both(act, NQUAD, step)

            @block.vector
            def _(dve):
                tt = nc.vector.tensor_tensor
                by = lambda tile: over(tile[:, :], 4)

                def step(j, par, a=True, b=True):
                    i = j - 1
                    if a:
                        at_least(dve, s["hid"], j)
                        q = heads(quad(res["q"], j), 4)
                        tt(heads(qd[:, :], 4), q, by(res["decay"]), ALU.mult)
                        tt(heads(qs[:, :], 4), q, by(res["shift"]), ALU.mult).then_inc(s["q"], 1)
                    if b:
                        dve.wait_ge(s["gelu"], i + 1)
                        at_least(dve, s["out"], i)
                        gi = heads(g[1 - par][:, :], 4)
                        tt(heads(gd[:, :], 4), gi, by(res["decay"]), ALU.mult)
                        tt(heads(gs[:, :], 4), gi, by(res["shift"]), ALU.mult).then_inc(s["g"], 1)
                        dve.wait_ge(s["out"], i + 1)
                        tt(heads(o[:, :], 2), halves(dbl[1]), heads(quad(res["q"], i), 2), ALU.add).then_inc(s["o"], 1)
                        dve.wait_ge(s["o"], i + 1)
                        tt(quad(hT, i), quad(hT, i), o[:, :], ALU.add).then_inc(s["stored"], 1)

                both(dve, NQUAD, step)


def renorm(core, res):
    nc, hT, dbl = core.nc, core.hT, core.dbl
    with ExitStack() as mem:
        sb = core.tiles("renorm", mem)
        square = [sb(f"square{i}", P, QUAD) for i in range(2)]
        lnv, rstd = sb("lnv", P, QUAD), sb("rstd", P, QUAD)
        s = {n: core.sem("renorm_" + n) for n in "ch sq ssq lnv rstd xn".split()}
        with nc.Block() as block:
            @block.tensor
            def _(pe):
                def step(j, par, a=True, b=True):
                    i = j - 1
                    if a:
                        at_least(pe, s["xn"], j - 1)
                        project(core, dbl[par], core.center, half_of(hT, j)).then_inc(s["ch"], 1)
                    if b:
                        pe.wait_ge(s["sq"], i + 1)
                        at_least(pe, s["rstd"], i - 1)
                        project(core, dbl[3 - par], core.mean, half_of(square[1 - par])).then_inc(s["ssq"], 1)

                both(pe, NQUAD, step)

            @block.scalar
            def _(act):
                f = nc.scalar.activation
                nc.scalar.preload_act_table_set("natural_log_exp_and_others")

                def step(j, par, a=True, b=True):
                    i = j - 1
                    if a:
                        act.wait_ge(s["ch"], j + 1)
                        at_least(act, s["ssq"], j - 1)
                        f(heads(square[par][:, :], 2), halves(dbl[par]), ACT.Square).then_inc(s["sq"], 1)
                    if b:
                        act.wait_ge(s["ssq"], i + 1)
                        at_least(act, s["xn"], i)
                        f(heads(lnv[:, :], 2), halves(dbl[3 - par]), ACT.Ln, bias=core.eps).then_inc(s["lnv"], 1)
                        act.wait_ge(s["lnv"], i + 1)
                        f(rstd[:, :], lnv[:, :], ACT.Exp, scale=-0.5).then_inc(s["rstd"], 1)

                both(act, NQUAD, step)

            @block.vector
            def _(dve):
                def step(j, par, a=True, b=True):
                    i = j - 1
                    if b:
                        dve.wait_ge(s["rstd"], i + 1)
                        nc.vector.tensor_tensor(heads(quad(res["x"], i), 2), halves(dbl[1 - par]), heads(rstd[:, :], 2),
                                                ALU.mult).then_inc(s["xn"], 1)

                both(dve, NQUAD, step)


def memory(core):
    res = {"x": core.sb("x", [P, TOK]), "decay": core.sb("decay", [P, L]), "shift": core.sb("shift", [P, L])}
    core.x = res["x"]
    with ExitStack() as mem:
        res["q"] = core.sb("q", [P, TOK], mem)
        res["w"] = core.sb("mem_w", [P, 7 * P], mem)
        convolve(core, res)
        gates(core, res)
        recall(core, res)
        renorm(core, res)


def normal_tail(p):
    lo, hi = -8.0, 8.0
    for _ in range(60):
        mid = (lo + hi) / 2
        lo, hi = (mid, hi) if 0.5 * math.erfc(mid / math.sqrt(2.0)) > p else (lo, mid)
    return lo, math.exp(-lo * lo / 2) / math.sqrt(2 * math.pi)


class TopK:

    def __init__(self, width, k, rounds, corrected):
        self.width, self.k, self.rounds = width, k, rounds
        goal = k - 4 * rounds
        z, density = normal_tail(goal / width)
        sigma = math.sqrt(2 * math.pi) / width
        self.guess = z * sigma
        if corrected:
            step = sigma / (width * density)
            self.per_sign = step / 2
            self.base = self.guess + step * (width / 2 - goal)


TAKEN = -1.6e38
SEL_IN = TopK(NIN, K_IN, 3, True)
SEL_PROC = TopK(NPROC, K_PROC, 6, False)
SEL_OUT = TopK(NOUT, K_OUT, 3, True)


def patterns(core):
    nc, hT, dram, bank = core.nc, core.hT, core.dram, core.bank
    NT = CHUNK // P
    with ExitStack() as mem:
        sb = core.tiles("pat", mem)
        w_in, w_proc, w_val = sb("w_in", P, NIN), sb("w_proc", P, NIN // P * NPROC), sb("w_val", P, NPROC // P * DPV)
        w_ow, w_out = sb("w_ow", DPV, NOUT), sb("w_out", P, NOUT // P * D)
        xs = [sb(f"xs{i}", P, CHUNK) for i in range(2)]
        hs = [sb(f"hs{i}", P, CHUNK) for i in range(2)]
        act_in = [sb(f"act_in{i}", P, NT * NIN) for i in range(2)]
        act_proc, act_out = sb("act_proc", P, NT * NPROC), sb("act_out", P, NT * NOUT)
        sum_in = [sb(f"sum_in{i}", P, NT) for i in range(2)]
        sum_proc, sum_out, neg_guess, signs = sb("sum_proc", P, NT), sb("sum_out", P, NT), sb("neg_guess", P, NT), sb("signs", P, NOUT)
        signs_in = [sb(f"signs_in{i}", P, NT) for i in range(2)]
        signs_out = sb("signs_out", P, NT)
        base, thr, count, togo = sb("base", P, NT), sb("thr", P, NT), sb("count", P, NT), sb("togo", P, NT)
        off, far = sb("off", P, NT), sb("far", P, NT)
        rank = [sb(f"rank{t}", P, 8 * SEL_PROC.rounds) for t in range(NT)]
        redo = sb("redo", 1, NT + 1)
        carrier, best = sb("carrier", P, 2), sb("best", P, NT)
        top, masked = [sb(f"top{t}", P, 8) for t in range(NT)], [sb(f"masked{t}", P, 8) for t in range(NT)]
        left = [sb(f"left{t}", P, NIN) for t in range(NT)]
        kept_in, kept_out = sb("kept_in", P, NT * NIN), sb("kept_out", P, NT * NOUT)
        keptT, expo = sb("keptT", P, NIN), sb("expo", P, NT * NPROC)
        neg_best, prob, probT = sb("neg_best", P, NT), sb("prob", P, NT * NPROC), sb("probT", P, NPROC)
        psums, rsum = sb("prob_sums", P, NT), sb("rsum", P, NT)
        aggT, outT = sb("aggT", DPV, P), sb("outT", P, NOUT)
        final = [sb(f"final{i}", P, CHUNK) for i in range(2)]

        s_w = core.sem("pat_weights_in")
        s_dram = [core.sem(f"pat_stored{i}") for i in range(2)]
        names = ("xs hs act gelu kept_in tr_in keptT proc act_proc best neg_best expo prob tr_prob probT agg aggT "
                 "out act_out kept_out tr_out outT fin final guess_in guess_out signs_in signs_out far flags "
                 "chain redone")
        s = {n: core.sem("pat_" + n) for n in names.split()}

        def chunks(eng, step):
            step(0, 0, 0, 2)
            step(1, 1, 0, 2)
            with eng.Fori(0, (NCHUNK - 4) // 2) as t:
                step(t * 2 + 2, 0, t + 1, 2)
                step(t * 2 + 3, 1, t + 1, 2)
            step(NCHUNK - 2, 0, NCHUNK // 2 - 1, 1)
            step(NCHUNK - 1, 1, NCHUNK // 2 - 1, 0)

        with nc.Block() as block:
            @block.sync
            def _(sp):
                for dst, name in ((w_in, "pat_in"), (w_proc, "pat_proc"), (w_val, "pat_val"), (w_ow, "pat_ow"),
                                  (w_out, "pat_out")):
                    sp.dma_start(dst[:, :], dram[name]).then_inc(s_w, 16)

                def step(j, par, k, more):
                    sp.wait_ge(s["final"], NT * (j + 1))
                    rows = dram["out"][bass.ds(j * CHUNK, CHUNK), :].rearrange("(t p) d -> p t d", p=P)
                    sp.dma_start(rows, heads(final[par][:, :], NT)).then_inc(s_dram[par], 16)

                chunks(sp, step)
                for par in range(2):
                    sp.wait_ge(s_dram[par], 16 * (NCHUNK // 2))

            @block.gpsimd
            def _(pool):
                def stage_x(j, par):
                    at_least(pool, s["act"], NT * (j - 1))
                    nc.gpsimd.tensor_copy(xs[par][:, :], core.x[:, bass.ds(j * CHUNK, CHUNK)]).then_inc(s["xs"], 1)

                def step(j, par, k, more):
                    at_least(pool, s["fin"], NT * (j - 1))
                    nc.gpsimd.tensor_copy(hs[par][:, :], hT[:, bass.ds(j * CHUNK, CHUNK)]).then_inc(s["hs"], 1)
                    if more == 2:
                        stage_x(j + 2, par)

                stage_x(0, 0)
                stage_x(1, 1)
                chunks(pool, step)

            @block.tensor
            def _(pe):
                mm, tr = nc.tensor.matmul, nc.tensor.transpose
                pe.wait_ge(s_w, 16 * 5)

                def flags(phase):
                    pe.wait_ge(s["far"], phase + 1)
                    at_least(pe, s["redone"], phase)
                    mm(bank[6][0:1, 0:NT], core.ones[:, 0:1], far[:, :], start=True, stop=True
                       ).then_inc(s["flags"], 1)

                def first(j, par):
                    pe.wait_ge(s["xs"], j + 1)
                    for t in range(NT):
                        n = NT * j + t
                        at_least(pe, s["gelu"], n - 1)
                        bk = bank[(NT * par + t) % 2]
                        mm(bk, xs[par][:, t * P:(t + 1) * P], w_in[:, :], start=True, stop=True).then_inc(s["act"], 1)

                def process(j):
                    for t in range(NT):
                        n = NT * j + t
                        pe.wait_ge(s["kept_in"], n + 1)
                        at_least(pe, s["keptT"], n)
                        if not isinstance(j, int) or j:
                            pe.wait_ge(s["outT"], NT * (j - 1))
                        for c in range(NIN // P):
                            last = tr(bank[2][:, c * P:(c + 1) * P], kept_in[:, t * NIN + c * P:t * NIN + (c + 1) * P],
                                      core.ident)
                        last.then_inc(s["tr_in"], 1)
                        pe.wait_ge(s["keptT"], n + 1)
                        at_least(pe, s["act_proc"], n)
                        for c in range(NIN // P):
                            last = mm(bank[3][:, 0:NPROC], keptT[:, c * P:(c + 1) * P],
                                      w_proc[:, c * NPROC:(c + 1) * NPROC], start=c == 0, stop=c == NIN // P - 1)
                        last.then_inc(s["proc"], 1)

                def step(j, par, k, more):
                    flags(3 * j + 1)
                    for t in range(NT):
                        n = NT * j + t
                        pe.wait_ge(s["prob"], n + 1)
                        at_least(pe, s["aggT"], n)
                        for c in range(NPROC // P):
                            last = tr(bank[4][:, c * P:(c + 1) * P], prob[:, t * NPROC + c * P:t * NPROC + (c + 1) * P],
                                      core.ident)
                        last.then_inc(s["tr_prob"], 1)
                        pe.wait_ge(s["probT"], n + 1)
                        for c in range(NPROC // P):
                            last = mm(bank[4][0:DPV, NPROC:NPROC + P], w_val[:, c * DPV:(c + 1) * DPV],
                                      probT[:, c * P:(c + 1) * P], start=c == 0, stop=c == NPROC // P - 1)
                        last.then_inc(s["agg"], 1)
                        pe.wait_ge(s["aggT"], n + 1)
                        at_least(pe, s["act_out"], n)
                        mm(bank[5], aggT[:, :], w_ow[:, :], start=True, stop=True).then_inc(s["out"], 1)
                    if more:
                        flags(3 * j + 2)
                        process(j + 1)
                    if more == 2:
                        first(j + 2, par)
                    flags(3 * j + (3 if more else 2))
                    pe.wait_ge(s["hs"], j + 1)
                    for t in range(NT):
                        n = NT * j + t
                        pe.wait_ge(s["kept_out"], n + 1)
                        at_least(pe, s["outT"], n)
                        if more:
                            pe.wait_ge(s["keptT"], NT * (j + 2))
                        for c in range(NOUT // P):
                            last = tr(bank[2][:, c * P:(c + 1) * P], kept_out[:, t * NOUT + c * P:t * NOUT + (c + 1) * P],
                                      core.ident)
                        last.then_inc(s["tr_out"], 1)
                        pe.wait_ge(s["outT"], n + 1)
                        at_least(pe, s["final"], n)
                        for c in range(NOUT // P):
                            mm(bank[7][:, 0:D], outT[:, c * P:(c + 1) * P], w_out[:, c * D:(c + 1) * D],
                               start=c == 0, stop=False)
                        mm(bank[7][:, 0:D], hs[par][:, t * P:(t + 1) * P], core.ident, start=False, stop=True
                           ).then_inc(s["fin"], 1)

                first(0, 0)
                first(1, 1)
                flags(0)
                process(0)
                chunks(pe, step)

            @block.scalar
            def _(act):
                f = nc.scalar.activation

                def guesses(sel, sums, sign_sums, tiles, j, s_guess, s_signs):
                    at_least(act, s_signs, NT * j)
                    nc.scalar.mul(neg_guess[:, :], sums[:, :], -sel.guess).then_inc(s_guess, 1)
                    act.wait_ge(s_guess, j + 1)
                    for t in range(NT):
                        f(signs[:, :], tiles[:, t * sel.width:(t + 1) * sel.width], ACT.Sign,
                          bias=neg_guess[:, t:t + 1], accum_out=sign_sums[:, t:t + 1]).then_inc(s_signs, 1)
                        act.wait_ge(s_signs, NT * j + t + 1)

                def first(j, par):
                    at_least(act, s["kept_in"], NT * (j - 1))
                    for t in range(NT):
                        act.wait_ge(s["act"], NT * j + t + 1)
                        f(act_in[par][:, t * NIN:(t + 1) * NIN], bank[(NT * par + t) % 2], ACT.Gelu,
                          accum_out=sum_in[par][:, t:t + 1]).then_inc(s["gelu"], 1)
                    act.wait_ge(s["gelu"], NT * (j + 1))
                    guesses(SEL_IN, sum_in[par], signs_in[par], act_in[par], j, s["guess_in"], s["signs_in"])

                def process(j):
                    for t in range(NT):
                        n = NT * j + t
                        act.wait_ge(s["tr_in"], n + 1)
                        at_least(act, s["proc"], n)
                        nc.scalar.copy(keptT[:, :], bank[2]).then_inc(s["keptT"], 1)
                        act.wait_ge(s["proc"], n + 1)
                        at_least(act, s["prob"], n - NT + 1)
                        f(act_proc[:, t * NPROC:(t + 1) * NPROC], bank[3][:, 0:NPROC], ACT.Gelu,
                          accum_out=sum_proc[:, t:t + 1]).then_inc(s["act_proc"], 1)

                def step(j, par, k, more):
                    act.wait_ge(s["best"], NT * (j + 1))
                    at_least(act, s["prob"], NT * j)
                    nc.scalar.mul(neg_best[:, :], best[:, :], -1.0).then_inc(s["neg_best"], 1)
                    act.wait_ge(s["neg_best"], j + 1)
                    for t in range(NT):
                        f(expo[:, t * NPROC:(t + 1) * NPROC], act_proc[:, t * NPROC:(t + 1) * NPROC], ACT.Exp,
                          bias=neg_best[:, t:t + 1]).then_inc(s["expo"], 1)
                    for t in range(NT):
                        n = NT * j + t
                        act.wait_ge(s["tr_prob"], n + 1)
                        at_least(act, s["agg"], n)
                        nc.scalar.copy(probT[:, :], bank[4][:, 0:NPROC]).then_inc(s["probT"], 1)
                        act.wait_ge(s["agg"], n + 1)
                        at_least(act, s["out"], n)
                        nc.scalar.copy(aggT[:, :], bank[4][0:DPV, NPROC:NPROC + P]).then_inc(s["aggT"], 1)
                        act.wait_ge(s["out"], n + 1)
                        at_least(act, s["kept_out"], n - NT + 1)
                        f(act_out[:, t * NOUT:(t + 1) * NOUT], bank[5], ACT.Gelu, scale=rsum[:, t:t + 1],
                          accum_out=sum_out[:, t:t + 1]).then_inc(s["act_out"], 1)
                    act.wait_ge(s["act_out"], NT * (j + 1))
                    guesses(SEL_OUT, sum_out, signs_out, act_out, j, s["guess_out"], s["signs_out"])
                    if more:
                        process(j + 1)
                    if more == 2:
                        first(j + 2, par)
                    for t in range(NT):
                        n = NT * j + t
                        act.wait_ge(s["tr_out"], n + 1)
                        at_least(act, s["fin"], n)
                        nc.scalar.copy(outT[:, :], bank[2]).then_inc(s["outT"], 1)
                        act.wait_ge(s["fin"], n + 1)
                        at_least(act, s_dram[par], 16 * k)
                        nc.scalar.copy(final[par][:, t * D:(t + 1) * D], bank[7][:, 0:D]).then_inc(s["final"], 1)

                first(0, 0)
                first(1, 1)
                process(0)
                chunks(act, step)

            @block.vector
            def _(dve):
                v, tt = nc.vector, nc.vector.tensor_tensor
                chain = LocalChain(dve, s["chain"])
                flag = core.ctx.enter_context(dve.register("pat_flag"))

                def select(sel, phase, tiles, sums, sign_sums, ready, keep):
                    src = lambda t: tiles[:, t * sel.width:(t + 1) * sel.width]
                    mark = lambda t: left[t][:, 0:sel.width]
                    v.memset(carrier[:, 1:2], 0.0)
                    chain.begin()
                    dve.wait_ge(*ready)
                    if sign_sums is None:
                        chain.link(v.tensor_scalar(thr[:, :], sums[:, :], sel.guess, None, ALU.mult))
                    else:
                        v.tensor_scalar(base[:, :], sums[:, :], sel.base, None, ALU.mult)
                        chain.link(v.scalar_tensor_tensor(out=thr[:, :], in0=sign_sums[:, :], scalar=sel.per_sign,
                                                          in1=sums[:, :], op0=ALU.mult, op1=ALU.mult))
                        chain.link(tt(thr[:, :], thr[:, :], base[:, :], ALU.add))
                    for t in range(NT):
                        counted = v.tensor_scalar(mark(t), src(t), thr[:, t:t + 1], None, ALU.is_ge, ALU.add,
                                                  accum_out=count[:, t:t + 1])
                    chain.link(counted)
                    chain.link(v.tensor_scalar(togo[:, :], count[:, :], -1.0, float(sel.k), ALU.mult, ALU.add))
                    chain.link(v.tensor_scalar(off[:, :], togo[:, :], 4.0 * sel.rounds + 0.5, None, ALU.subtract))
                    chain.link(tt(off[:, :], off[:, :], off[:, :], ALU.mult))
                    v.tensor_scalar(far[:, :], off[:, :], 16.0 * sel.rounds ** 2, None, ALU.is_gt
                                    ).then_inc(s["far"], 1)
                    for t in range(NT):
                        v.scalar_tensor_tensor(out=mark(t), in0=mark(t), scalar=TAKEN, in1=src(t),
                                               op0=ALU.mult, op1=ALU.add)
                        chain.link(v.tensor_scalar(rank[t][:, 0:8 * sel.rounds], core.iota48[:, 0:8 * sel.rounds],
                                                   togo[:, t:t + 1], 0.5, ALU.is_lt, ALU.subtract))
                    replaced = [chain.n] * NT
                    for r in range(sel.rounds):
                        found, cut = [], []
                        for t in range(NT):
                            chain.after(replaced[t])
                            found.append(chain.mark(v.max(top[t][:, :], mark(t))))
                        for t in range(NT):
                            chain.after(found[t])
                            cut.append(chain.mark(v.scalar_tensor_tensor(
                                out=masked[t][:, :], in0=rank[t][:, 8 * r:8 * r + 8], scalar=-2.0 * TAKEN,
                                in1=top[t][:, :], op0=ALU.mult, op1=ALU.min)))
                        for t in range(NT):
                            chain.after(cut[t])
                            replaced[t] = chain.mark(v.match_replace(mark(t), masked[t][:, :], mark(t), TAKEN))
                    dve.wait_ge(s["flags"], phase + 1)
                    v.tensor_copy(redo[:, 0:NT], bank[6][0:1, 0:NT])
                    v.tensor_reduce(redo[:, NT:NT + 1], bank[6][0:1, 0:NT], AX.X, ALU.add).then_inc(s["redone"], 1)
                    dve.wait_ge(s["redone"], phase + 1)
                    chain.link(v.memset(carrier[:, 0:1], 0.0))
                    dve.reg_load(flag, redo[0:1, NT:NT + 1].bitcast(U32))
                    with dve.If_ne(flag, 0):
                        for t in range(NT):
                            dve.reg_load(flag, redo[0:1, t:t + 1].bitcast(U32))
                            with dve.If_ne(flag, 0):
                                full(sel, mark(t), src(t))
                    for t in range(NT):
                        keep(t)

                def full(sel, mark, src):
                    again.begin()
                    for r in range(sel.k // 8):
                        from_ = mark if r else src
                        again.link(v.max(top[0][:, :], from_))
                        again.link(v.match_replace(mark, top[0][:, :], from_, TAKEN))

                again = LocalChain(dve, core.sem("pat_again"))

                def kept(dst, sel, tiles, t):
                    return v.scalar_tensor_tensor(out=dst[:, t * sel.width:(t + 1) * sel.width],
                                                  in0=left[t][:, 0:sel.width], scalar=TAKEN / 2,
                                                  in1=tiles[:, t * sel.width:(t + 1) * sel.width],
                                                  op0=ALU.is_lt, op1=ALU.mult)

                def select_in(j, par, phase):
                    at_least(dve, s["tr_in"], NT * j)
                    select(SEL_IN, phase, act_in[par], sum_in[par], signs_in[par], (s["signs_in"], NT * (j + 1)),
                           lambda t: kept(kept_in, SEL_IN, act_in[par], t).then_inc(s["kept_in"], 1))
                    dve.wait_ge(s["kept_in"], NT * (j + 1))

                def step(j, par, k, more):
                    dve.wait_ge(s["act_proc"], NT * (j + 1))
                    at_least(dve, s["neg_best"], j)
                    for t in range(NT):
                        v.tensor_reduce(best[:, t:t + 1], act_proc[:, t * NPROC:(t + 1) * NPROC], AX.X, ALU.max
                                        ).then_inc(s["best"], 1)

                    def softmax(t):
                        n = NT * j + t
                        dve.wait_ge(s["expo"], n + 1)
                        cut = slice(t * NPROC, (t + 1) * NPROC)
                        chain.link(v.scalar_tensor_tensor(out=prob[:, cut], in0=left[t][:, 0:NPROC], scalar=TAKEN / 2,
                                                          in1=expo[:, cut], op0=ALU.is_lt, op1=ALU.mult,
                                                          accum_out=psums[:, t:t + 1]))
                        v.reciprocal(rsum[:, t:t + 1], psums[:, t:t + 1]).then_inc(s["prob"], 1)
                        if t < NT - 1:
                            chain.link(v.memset(carrier[:, 0:1], 0.0))

                    at_least(dve, s["tr_prob"], NT * j)
                    at_least(dve, s["act_out"], NT * j)
                    select(SEL_PROC, 3 * j + 1, act_proc, sum_proc, None, (s["act_proc"], NT * (j + 1)), softmax)
                    dve.wait_ge(s["prob"], NT * (j + 1))
                    if more:
                        select_in(j + 1, 1 - par, 3 * j + 2)
                    at_least(dve, s["tr_out"], NT * j)
                    select(SEL_OUT, 3 * j + (3 if more else 2), act_out, sum_out, signs_out,
                           (s["signs_out"], NT * (j + 1)),
                           lambda t: kept(kept_out, SEL_OUT, act_out, t).then_inc(s["kept_out"], 1))
                    dve.wait_ge(s["kept_out"], NT * (j + 1))

                select_in(0, 0, 0)
                chunks(dve, step)


def vit_tower(nc, dram):
    with ExitStack() as ctx:
        core = Core(nc, ctx, dram)
        embed(core)
        attend(core)
        experts(core)
        memory(core)
        patterns(core)


def laid_out(i):
    a = {k: np.asarray(v) for k, v in i.items()}
    col = lambda v: v.reshape(-1, 1)
    stack = lambda *v: np.stack(v, axis=1)
    r = {"x": a["x"], "const": constants()}
    r["tok_w"] = a["L0_tok_W"].reshape(D, PATCH, PATCH, CH).transpose(3, 1, 2, 0)
    r["tok_w"] = np.concatenate([r["tok_w"][:, :, c::2].reshape(CH * PATCH, -1) for c in (0, 1)])
    r["tok_cols"] = stack(a["L0_tok_b"], a["L0_tok_cls_token"].reshape(D))
    r["tok_pos"] = a["L0_tok_pos_emb"].reshape(1, L)
    by_head = lambda w: w.reshape(-1, KDIM, HEADS).transpose(0, 2, 1).reshape(-1, KDIM * HEADS)
    r["att_qk"] = np.concatenate([by_head(a["L0_attn_qw"]), by_head(a["L0_attn_kw"])], axis=1)
    qkb = np.concatenate([by_head(a["L0_attn_qb"]), by_head(a["L0_attn_kb"])], axis=1)
    r["att_v"] = a["L0_attn_vw"].reshape(D, D, HEADS).transpose(0, 2, 1).reshape(D, HEADS * D)
    r["att_w1"] = a["L0_attn_w1"].reshape(D, HEADS * F1)
    r["att_w2"] = a["L0_attn_w2"].reshape(F1 // P, P, D).transpose(1, 0, 2).reshape(P, F1)
    r["att_cols"] = np.concatenate([col(a["L0_attn_ln0_w"]), col(a["L0_attn_ln0_b"]), qkb.reshape(4, P).T,
                                    a["L0_attn_vb"].reshape(D, HEADS), a["L0_attn_ln1_w"], a["L0_attn_ln1_b"],
                                    a["L0_attn_b1"].reshape(F1 // P, P).T, col(a["L0_attn_b2"])], axis=1)
    r["moe_router"] = a["L0_ffn_router_w"]
    r["moe_router_b"] = a["L0_ffn_router_b"].reshape(1, EXPERTS)
    r["moe_up"] = a["L0_ffn_gate_up_proj"].transpose(1, 0, 2).reshape(D, EXPERTS * 2 * INTER)
    r["moe_up_b"] = a["L0_ffn_gate_up_proj_bias"].reshape(EXPERTS * 4, P).T
    r["moe_down"] = a["L0_ffn_down_proj"].reshape(EXPERTS, 2, P, D).transpose(2, 0, 1, 3).reshape(P, EXPERTS * INTER)
    r["moe_down_b"] = a["L0_ffn_down_proj_bias"]
    r["mem_w"] = np.concatenate([a["L1_attn_q_w"].T, a["L1_attn_eta_w1"], a["L1_attn_eta_w2"], a["L1_attn_alpha_w1"],
                                 a["L1_attn_alpha_w2"], a["L1_attn_mem_w1"], a["L1_attn_mem_w2"]], axis=1)
    r["mem_conv"] = np.concatenate([a["L1_attn_conv_w"].reshape(D, TAPS), col(a["L1_attn_conv_b"])], axis=1)
    r["pat_in"] = a["L1_ffn_input_patterns"].T
    r["pat_proc"] = a["L1_ffn_process_input_weights"].T.reshape(NIN // P, P, NPROC).transpose(1, 0, 2).reshape(P, -1)
    r["pat_val"] = a["L1_ffn_process_values"].reshape(NPROC // P, P, DPV).transpose(1, 0, 2).reshape(P, -1)
    r["pat_ow"] = a["L1_ffn_output_input_weights"].T
    r["pat_out"] = a["L1_ffn_output_patterns"].reshape(NOUT // P, P, D).transpose(1, 0, 2).reshape(P, -1)
    return {k: np.ascontiguousarray(v) for k, v in r.items()}


def kernel(**inputs):
    import concourse.bacc as bacc
    from concourse.bass_utils import run_bass_kernel_spmd

    nc = bacc.Bacc("TRN2", target_bir_lowering=False, num_devices=1)
    arrays = laid_out(inputs)
    dram = {k: nc.dram_tensor(f"in_{k}", v.shape, mybir.dt.from_np(v.dtype), kind="ExternalInput").ap()
            for k, v in arrays.items()}
    dram["out"] = nc.dram_tensor("out_tokens", (TOK, D), F32, kind="ExternalOutput").ap()
    vit_tower(nc, dram)
    r = run_bass_kernel_spmd(nc, [{f"in_{k}": v for k, v in arrays.items()}], core_ids=[0])
    return r.results[0]["out_tokens"].reshape(NIMG, L, D)
```

```python
import math
from contextlib import ExitStack

import numpy as np

import concourse.bass as bass
from concourse import mybir

F32 = mybir.dt.float32
U32 = mybir.dt.uint32
ALU = mybir.AluOpType
ACT = mybir.ActivationFunctionType
AX = mybir.AxisListType

P = 128
NIMG, CH, IMG_H, IMG_W, PATCH = 64, 3, 176, 208, 16
PW, PH = IMG_H // PATCH, IMG_W // PATCH
NPATCH = PW * PH
L = NPATCH + 1
D = 128
TOK = NIMG * L
HEADS, KDIM = 8, 32
F1 = 512
EXPERTS, INTER = 8, 256
NIN, NPROC, NOUT, DPV = 512, 256, 512, 64
K_IN, K_PROC, K_OUT = 64, 128, 64
EPS = 1e-5
REM = L - P
PAIR = 2 * L
NPAIR = NIMG // 2
CHUNK = 3 * P
NCHUNK = TOK // CHUNK
TAPS = 4
NEG = -3.0e38

C_IDENT, C_CENTER, C_MEAN, C_MEANH, C_BLK, C_NEG1 = 0, 128, 256, 384, 512, 640
C_MASK = 768
C_MASKR = C_MASK + L
C_IOTA = C_MASKR + REM
C_ONES = C_IOTA + 48
C_EPS = C_ONES + L
C_COLS = C_EPS + 3


def constants():
    c = np.zeros((P, C_COLS), np.float32)
    c[:, C_IDENT:C_IDENT + P] = np.eye(P)
    c[:, C_CENTER:C_CENTER + P] = np.eye(P) - 1.0 / D
    c[:, C_MEAN:C_MEAN + P] = 1.0 / D
    c[:, C_MEANH:C_MEANH + P] = 1.0 / (D * HEADS)
    c[:, C_BLK:C_BLK + P] = np.kron(np.eye(P // KDIM), np.ones((KDIM, KDIM)))
    c[:, C_NEG1:C_NEG1 + P] = -1.0
    c[:, C_MASK:C_MASK + L] = np.arange(P)[:, None] <= np.arange(L)[None, :]
    c[:REM, C_MASKR:C_MASKR + REM] = np.arange(REM)[:, None] <= np.arange(REM)[None, :]
    c[:, C_IOTA:C_IOTA + 48] = np.arange(48)[None, :]
    c[:, C_ONES:C_ONES + L] = 1.0
    c[:, C_EPS], c[:, C_EPS + 1], c[:, C_EPS + 2] = EPS, 1.0 + EPS, math.log(1024.0)
    return c


def steps(eng, n, step):
    step(0, 0, 0)
    step(1, 1, 0)
    with eng.Fori(0, (n - 2) // 2) as t:
        step(t * 2 + 2, 0, t + 1)
        step(t * 2 + 3, 1, t + 1)


def both(eng, n, step):
    step(0, 0, b=False)
    step(1, 1)
    with eng.Fori(0, (n - 2) // 2) as t:
        step(t * 2 + 2, 0)
        step(t * 2 + 3, 1)
    step(n, n % 2, a=False)


def at_least(eng, sem, value):
    if not (isinstance(value, int) and value <= 0):
        eng.wait_ge(sem, value)


class Chain:

    def __init__(self, eng, sem, per_step):
        self.eng, self.sem, self.per_step = eng, sem, per_step

    def begin(self, j):
        self.base, self.n = j * self.per_step, 0

    def link(self, instruction):
        self.n += 1
        instruction.then_inc(self.sem, 1)
        self.eng.wait_ge(self.sem, self.base + self.n)

    def end(self):
        assert self.n == self.per_step, (self.n, self.per_step)


class LocalChain:

    def __init__(self, eng, sem):
        self.eng, self.sem = eng, sem

    def begin(self):
        self.n = 0
        self.eng.sem_clear(self.sem)

    def mark(self, instruction):
        self.n += 1
        instruction.then_inc(self.sem, 1)
        return self.n

    def after(self, count):
        self.eng.wait_ge(self.sem, count)

    def link(self, instruction):
        self.after(self.mark(instruction))


class Core:

    def __init__(self, nc, ctx, dram):
        self.nc, self.ctx, self.dram = nc, ctx, dram
        self.hT = self.sb("hT", [P, TOK])
        self.const = self.sb("const", [P, C_COLS])
        c = self.const
        self.ident = c[:, C_IDENT:C_IDENT + P]
        self.center = c[:, C_CENTER:C_CENTER + P]
        self.mean = c[:, C_MEAN:C_MEAN + P]
        self.meanh = c[:, C_MEANH:C_MEANH + P]
        self.blk = c[:, C_BLK:C_BLK + P]
        self.neg1 = c[:, C_NEG1:C_NEG1 + P]
        self.mask = c[:, C_MASK:C_MASK + L]
        self.mask_r = c[0:REM, C_MASKR:C_MASKR + REM]
        self.iota = c[:, C_IOTA:C_IOTA + EXPERTS]
        self.iota48 = c[:, C_IOTA:C_IOTA + 48]
        self.ones = c[:, C_ONES:C_ONES + L]
        self.eps = c[:, C_EPS:C_EPS + 1]
        self.one_eps = c[:, C_EPS + 1:C_EPS + 2]
        self.ln1024 = c[:, C_EPS + 2:C_EPS + 3]
        self.dbl = [self.ctx.enter_context(nc.psum_tensor(f"banks{i}", [P, 1024], F32))[:, :] for i in range(4)]
        self.bank = [self.dbl[i // 2][:, 512 * (i % 2):512 * (i % 2 + 1)] for i in range(8)]

    def sb(self, name, shape, ctx=None, dt=F32):
        return (ctx or self.ctx).enter_context(self.nc.sbuf_tensor(name, shape, dt))

    def tiles(self, phase, mem):
        return lambda name, *shape, dt=F32: self.sb(f"{phase}_{name}", list(shape), mem, dt)

    def sem(self, name, ctx=None):
        return (ctx or self.ctx).enter_context(self.nc.semaphore(name))

    def clear(self, sems):
        share = -(-len(sems) // 4)
        with self.nc.Block() as block:
            @block.gpsimd
            def _(pool):
                for sem in sems[0:share]:
                    pool.sem_clear(sem)

            @block.vector
            def _(dve):
                for sem in sems[share:2 * share]:
                    dve.sem_clear(sem)

            @block.scalar
            def _(act):
                for sem in sems[2 * share:3 * share]:
                    act.sem_clear(sem)

            @block.sync
            def _(sp):
                for sem in sems[3 * share:]:
                    sp.sem_clear(sem)


def heads(ap, n):
    return ap.rearrange("p (n m) -> p n m", n=n)


def over(ap, n):
    return ap.unsqueeze(1).to_broadcast([ap.shape[0], n, ap.shape[1]])


def embed(core):
    nc, hT, dram = core.nc, core.hT, core.dram
    KP = CH * PATCH
    SHIFT = 64
    KALL = SHIFT + KP
    NBUF = 4
    NG = NIMG // 4
    AREA = PW * IMG_W
    with ExitStack() as mem:
        x = [core.sb(f"x{i}", [P, 2 * AREA], mem) for i in range(NBUF)]
        w = core.sb("tok_w", [P, PATCH // 2 * D], mem)
        pos = core.sb("tok_pos", [P, L], mem)
        cols = core.sb("tok_cols", [P, 2], mem)
        s_clear = core.sem("tok_cleared")
        s_w = core.sem("tok_weights_in")
        s_x = [core.sem(f"tok_x_in{i}") for i in range(NBUF)]
        s_shift = core.sem("tok_shifted")
        s_proj = core.sem("tok_projected")
        s_tok = core.sem("tok_stored")
        images = dram["x"]

        with nc.Block() as block:
            @block.sync
            def _(sp):
                sp.wait_ge(s_clear, 1)
                sp.dma_start(core.const[:, :], dram["const"]).then_inc(s_w, 16)
                sp.dma_start(w[0:KP, :], dram["tok_w"][0:KP, :]).then_inc(s_w, 16)
                sp.dma_start(w[SHIFT:KALL, :], dram["tok_w"][KP:2 * KP, :]).then_inc(s_w, 16)
                sp.dma_start(cols[:, :], dram["tok_cols"]).then_inc(s_w, 16)
                sp.dma_start(pos[:, :], dram["tok_pos"].to_broadcast([P, L])).then_inc(s_w, 16)
                sp.wait_ge(s_clear, 1 + NBUF)

                def step(j, par, k):
                    for s in range(2):
                        buf = 2 * par + s
                        at_least(sp, s_proj, 2 * j - 3 + s)
                        for b in range(2):
                            for c in range(CH):
                                src = images[bass.ds(j * 4 + 2 * s + b, 1), c, :, :]
                                dst = heads(x[buf][PATCH * c:PATCH * (c + 1), b * AREA:(b + 1) * AREA], PW)
                                sp.dma_start(dst, src.rearrange("b (a p) w -> p (b a) w", p=PATCH)
                                             ).then_inc(s_x[buf], 16)

                steps(sp, NG, step)

            @block.gpsimd
            def _(pool):
                nc.gpsimd.memset(w[:, :], 0.0).then_inc(s_clear, 1)
                for buf in range(NBUF):
                    nc.gpsimd.memset(x[buf][:, :], 0.0).then_inc(s_clear, 1)

            @block.scalar
            def _(act):
                def step(j, par, k):
                    for s in range(2):
                        buf = 2 * par + s
                        act.wait_ge(s_x[buf], (k + 1) * 16 * 2 * CH)
                        nc.scalar.copy(x[buf][SHIFT:KALL, 0:2 * AREA - 1],
                                       x[buf][0:KP, 1:2 * AREA]).then_inc(s_shift, 1)

                steps(act, NG, step)

            @block.tensor
            def _(pe):
                pe.wait_ge(s_w, 16 * 5)

                def step(j, par, k):
                    for s in range(2):
                        buf = 2 * par + s
                        pe.wait_ge(s_shift, 2 * j + s + 1)
                        at_least(pe, s_tok, 2 * j - 3 + s)
                        src = x[buf][0:KALL, :].rearrange("p (n w) -> p n w", w=PATCH)
                        for col in range(0, PATCH, 2):
                            mm = nc.tensor.matmul(core.bank[buf][:, 0:2 * NPATCH],
                                                  w[0:KALL, col // 2 * D:(col // 2 + 1) * D], src[:, :, col],
                                                  start=col == 0, stop=col == PATCH - 2)
                        mm.then_inc(s_proj, 1)

                steps(pe, NG, step)

            @block.vector
            def _(dve):
                dve.wait_ge(s_w, 16 * 5)
                nc.vector.tensor_scalar(hT[:, :].rearrange("p (b l) -> p b l", l=L)[:, :, 0],
                                        cols[:, 1:2].to_broadcast([P, NIMG]), pos[:, 0:1], None, ALU.add)

                def step(j, par, k):
                    for s in range(2):
                        buf = 2 * par + s
                        dve.wait_ge(s_proj, 2 * j + s + 1)
                        out = heads(hT[:, bass.ds(j * (4 * L) + s * PAIR, PAIR)], 2)
                        nc.vector.scalar_tensor_tensor(
                            out=out[:, :, 1:L], in0=heads(core.bank[buf][:, 0:2 * NPATCH], 2),
                            scalar=cols[:, 0:1], in1=over(pos[:, 1:L], 2), op0=ALU.add, op1=ALU.add
                        ).then_inc(s_tok, 1)

                steps(dve, NG, step)


def three(eng, n, step):
    step(0, 0, b=False, c=False)
    step(1, 1, c=False)
    step(2, 0)
    step(3, 1)
    with eng.Fori(0, (n - 4) // 2) as t:
        step(t * 2 + 4, 0)
        step(t * 2 + 5, 1)
    step(n, n % 2, a=False)
    step(n + 1, 1 - n % 2, a=False, b=False)


def attend(core):
    nc, hT, dram, bank = core.nc, core.hT, core.dram, core.bank
    HD = HEADS * D
    F32R = mybir.dt.float32r
    GROUPS = [(0, 3), (3, 6), (6, 8)]
    Z_BANK = [5, 6, 7, 0, 1, 2, 3, 4]
    SPLIT = 3
    QK_ORDER = [2, 3, 0, 1]
    CLIP_LO, CLIP_HI = float(np.exp(np.float32(-10))), float(np.exp(np.float32(10)))
    with ExitStack() as mem:
        sb = core.tiles("att", mem)
        w_qk, w_v = sb("w_qk", P, 4 * P), sb("w_v", P, HD)
        w_1, w_2 = sb("w_1", P, HEADS * F1), sb("w_2", P, F1)
        w_1h, w_1l = sb("w_1h", P, HEADS * F1, dt=F32R), sb("w_1l", P, HEADS * F1, dt=F32R)
        cols = sb("cols", P, 35)
        ln0_w, ln0_b, b_qk, b_v = cols[:, 0:1], cols[:, 1:2], cols[:, 2:6], cols[:, 6:14]
        ln1_w, ln1_b = cols[:, 14:22], cols[:, 22:30]
        b_1, b_2 = cols[:, 30:34], cols[:, 34:35]
        square, lnv, rstd = sb("square", P, PAIR), sb("lnv", P, PAIR), sb("rstd", P, PAIR)
        rsq, rstd0, xh, x0 = (sb(n, P, PAIR) for n in ("rsq", "rstd0", "xh", "x0"))
        xn = [sb(f"xn{i}", P, PAIR) for i in range(2)]
        qk, ksum, qc = sb("qk", P, 4 * PAIR), sb("ksum", P, 2 * PAIR), sb("qc", P, 2 * PAIR)
        lnd, rden, qs = sb("lnd", P, 2 * PAIR), sb("rden", P, 2 * PAIR), sb("qs", P, 2 * PAIR)
        xtok, xtok_r = sb("xtok", P, 2 * P), sb("xtok_r", REM, 2 * P)
        sc = [sb(f"scores{i}", P, HEADS * L) for i in range(2)]
        sc_r = [sb(f"scores_r{i}", REM, HEADS * REM) for i in range(2)]
        u = sb("u", P, HEADS * PAIR)
        z = [sb(f"z{i}", P, HEADS * PAIR) for i in range(2)]
        zz = sb("zz", P, HEADS * PAIR)
        y_hi, y_lo = sb("y_hi", P, HEADS * PAIR, dt=F32R), sb("y_lo", P, HEADS * PAIR, dt=F32R)
        zs4, zs2, zs1, vs1 = sb("zs4", P, 4 * PAIR), sb("zs2", P, 2 * PAIR), sb("zs1", P, PAIR), sb("vs1", P, PAIR)
        lnz, rstdz = sb("lnz", P, PAIR), sb("rstdz", P, PAIR)
        hid, r = sb("hid", P, 4 * PAIR), sb("r", P, PAIR)

        s_w = core.sem("att_weights_in", mem)
        names = ("b1_sum b1 w1_hi w1_lo ch sq ssq rstd xn hx r0 xh x0 qk exp qc den rden qs scores mask tr "
                 "xtok u u0_out u1_out z z_out zsum vsum mean zc zz var rstdz znorm y y_hi y_lo w1 hid w2 r out "
                 "dve_a act_a act_b pool pool_v")
        s = {n: core.sem("att_" + n, mem) for n in names.split()}

        with nc.Block() as block:
            @block.sync
            def _(sp):
                for dst, name in ((w_qk, "att_qk"), (w_v, "att_v"), (w_1, "att_w1"), (w_2, "att_w2")):
                    sp.dma_start(dst[:, :], dram[name]).then_inc(s_w, 16)
                sp.dma_start(cols[:, :], dram["att_cols"]).then_inc(s_w, 16)

            @block.gpsimd
            def _(pool):
                add = lambda out, a, b: nc.gpsimd.tensor_tensor(out, a, b, ALU.add)
                chain, chain_v = Chain(pool, s["pool"], 2), Chain(pool, s["pool_v"], 2)

                def over_heads(chain, j, src, out):
                    chain.begin(j)
                    chain.link(add(zs4[:, :], src[:, 0:4 * PAIR], src[:, 4 * PAIR:]))
                    chain.link(add(zs2[:, :], zs4[:, 0:2 * PAIR], zs4[:, 2 * PAIR:]))
                    chain.end()
                    return add(out[:, :], zs2[:, 0:PAIR], zs2[:, PAIR:])

                def step(j, par, a=True, b=True, c=True):
                    if b:
                        pool.wait_ge(s["zz"], j)
                        at_least(pool, s["var"], j - 1)
                        over_heads(chain_v, j - 1, zz, vs1).then_inc(s["vsum"], 1)
                        pool.wait_ge(s["vsum"], j)
                    if a:
                        pool.wait_ge(s["z_out"], 8 * j + 8)
                        at_least(pool, s["mean"], j)
                        over_heads(chain, j, z[par], zs1).then_inc(s["zsum"], 1)
                        pool.wait_ge(s["zsum"], j + 1)

                three(pool, NPAIR, step)

            @block.tensor
            def _(pe):
                mm = nc.tensor.matmul
                pe.wait_ge(s_w, 16 * 5)
                for f in range(4):
                    for h in range(HEADS):
                        last = mm(bank[0][:, f:f + 1], w_1[:, h * F1 + f * P:h * F1 + (f + 1) * P],
                                  ln1_b[:, h:h + 1], start=h == 0, stop=h == HEADS - 1)
                last.then_inc(s["b1_sum"], 1)
                pe.wait_ge(s["w1_hi"], 1)
                pe.wait_ge(s["w1_lo"], 1)
                pe.wait_ge(s["b1"], 1)

                def mlp1(g, f, out, part=range(HEADS)):
                    for h in part:
                        if f == 0:
                            pe.wait_ge(s["y_lo"], 8 * g + h + 1)
                        w = slice(h * F1 + f * P, h * F1 + (f + 1) * P)
                        x = slice(h * PAIR, (h + 1) * PAIR)
                        mm(out[:, 0:PAIR], w_1l[:, w], y_hi[:, x], start=h == 0, stop=False)
                        mm(out[:, 0:PAIR], w_1h[:, w], y_hi[:, x], start=False, stop=False)
                        last = mm(out[:, 0:PAIR], w_1h[:, w], y_lo[:, x], start=False, stop=h == HEADS - 1)
                    if part[-1] == HEADS - 1:
                        last.then_inc(s["w1"], 1)

                def scores(j, img):
                    for half in range(2):
                        for r_ in range(4):
                            out = bank[4 * (1 - img) + r_]
                            rows = slice(KDIM * r_, KDIM * (r_ + 1))
                            k0, q0 = (2 + half) * PAIR + img * L, half * PAIR + img * L
                            mm(out[:, half * L:(half + 1) * L], qk[rows, k0:k0 + P], qs[rows, q0:q0 + L],
                               start=True, stop=True)
                            last = mm(out[0:REM, 2 * L + half * REM:2 * L + (half + 1) * REM],
                                      qk[rows, k0 + P:k0 + L], qs[rows, q0 + P:q0 + L], start=True, stop=True)
                    last.then_inc(s["scores"], 1)

                def head_inputs(j, img):
                    for g_, (h0, h1) in enumerate(GROUPS):
                        out = bank[5 + g_ if img == 0 else g_][:, 0:(h1 - h0) * L]
                        mm(out, xtok[:, img * P:(img + 1) * P], sc[img][:, h0 * L:h1 * L], start=True, stop=False)
                        mm(heads(out, h1 - h0)[:, :, P:L], xtok_r[:, img * P:(img + 1) * P],
                           heads(sc_r[img][:, h0 * REM:h1 * REM], h1 - h0), start=False, stop=True
                           ).then_inc(s["u"], 1)

                def step(j, par, a=True, b=True, c=True):
                    i, g = j - 1, j - 2
                    if a:
                        at_least(pe, s["z_out"], 8 * j - 4)
                        mm(bank[0][:, 0:PAIR], core.center, hT[:, bass.ds(j * PAIR, PAIR)],
                           start=True, stop=True).then_inc(s["ch"], 1)
                    elif b:
                        pe.wait_ge(s["z_out"], 8 * j)
                    if c:
                        if a:
                            pe.wait_ge(s["z_out"], 8 * j - 2)
                        mlp1(g, 0, bank[2])
                    if a:
                        at_least(pe, s["z_out"], 8 * j)
                        pe.wait_ge(s["sq"], j + 1)
                        mm(bank[1][:, 0:PAIR], core.mean, square[:, :], start=True, stop=True).then_inc(s["ssq"], 1)
                    if c:
                        mlp1(g, 1, bank[3])
                    if a:
                        pe.wait_ge(s["xn"], j + 1)
                        for img in range(2):
                            nc.tensor.transpose(bank[1][:, 2 * img * P:(2 * img + 1) * P],
                                                xn[par][:, img * L:img * L + P], core.ident)
                            last = nc.tensor.transpose(bank[1][0:REM, (2 * img + 1) * P:(2 * img + 2) * P],
                                                       xn[par][:, img * L + P:(img + 1) * L], core.ident)
                        last.then_inc(s["tr"], 1)
                    if b:
                        pe.wait_ge(s["zsum"], i + 1)
                        mm(bank[0][:, 0:PAIR], core.meanh, zs1[:, :], start=True, stop=True).then_inc(s["mean"], 1)
                    if a:
                        pe.wait_ge(s["x0"], j + 1)
                        for m in QK_ORDER:
                            mm(bank[4 + m][:, 0:PAIR], w_qk[:, m * P:(m + 1) * P], x0[:, :],
                               start=True, stop=True).then_inc(s["qk"], 1)
                    if c:
                        pe.wait_ge(s["hid"], 4 * g + 1)
                        mlp1(g, 2, bank[2])
                        pe.wait_ge(s["hid"], 4 * g + 2)
                        mlp1(g, 3, bank[3], range(0, SPLIT))
                    if a:
                        for half in range(2):
                            pe.wait_ge(s["qc"], 2 * j + half + 1)
                            if half:
                                pe.wait_ge(s["xtok"], j + 1)
                            elif b:
                                pe.wait_ge(s["zc"], i + 1)
                            mm(bank[half][:, 0:PAIR], core.blk, qc[:, half * PAIR:(half + 1) * PAIR],
                               start=True, stop=True).then_inc(s["den"], 1)
                    if c:
                        mlp1(g, 3, bank[3], range(SPLIT, HEADS))
                    if a:
                        pe.wait_ge(s["qs"], 2 * j + 2)
                        scores(j, 0)
                        if c:
                            pe.wait_ge(s["hid"], 4 * g + 4)
                        scores(j, 1)
                        pe.wait_ge(s["mask"], 2 * j + 1)
                    if b:
                        pe.wait_ge(s["vsum"], i + 1)
                        mm(bank[4][:, 0:PAIR], core.meanh, vs1[:, :], start=True, stop=True).then_inc(s["var"], 1)
                    if a:
                        head_inputs(j, 0)
                        pe.wait_ge(s["mask"], 2 * j + 2)
                    if c:
                        pe.wait_ge(s["hid"], 4 * g + 4)
                        for f in range(4):
                            last = mm(bank[3][:, 0:PAIR], w_2[:, f * P:(f + 1) * P], hid[:, f * PAIR:(f + 1) * PAIR],
                                      start=f == 0, stop=f == 3)
                        last.then_inc(s["w2"], 1)
                    if a:
                        head_inputs(j, 1)
                        pe.wait_ge(s["u0_out"], 3 * j + 3)
                        pe.wait_ge(s["u1_out"], 3 * j + 3)
                        for h in range(HEADS):
                            if c and Z_BANK[h] == 3:
                                pe.wait_ge(s["r"], g + 1)
                            if b and Z_BANK[h] == 4:
                                pe.wait_ge(s["rstdz"], i + 1)
                            mm(bank[Z_BANK[h]][:, 0:PAIR], w_v[:, h * D:(h + 1) * D], u[:, h * PAIR:(h + 1) * PAIR],
                               start=True, stop=True).then_inc(s["z"], 1)

                three(pe, NPAIR, step)

            @block.scalar
            def _(act):
                f = nc.scalar.activation
                nc.scalar.preload_act_table_set("natural_log_exp_and_others")
                chain_a, chain_b = Chain(act, s["act_a"], 4), Chain(act, s["act_b"], 1)
                act.wait_ge(s_w, 16 * 5)
                nc.scalar.copy(w_1h[:, :], w_1[:, :]).then_inc(s["w1_hi"], 1)
                act.wait_ge(s["b1"], 1)

                def hidden(g, m):
                    act.wait_ge(s["w1"], 4 * g + m + 1)
                    if m == 0:
                        at_least(act, s["w2"], g)
                    f(hid[:, m * PAIR:(m + 1) * PAIR], bank[2 + m % 2][:, 0:PAIR], ACT.Relu,
                      bias=b_1[:, m:m + 1]).then_inc(s["hid"], 1)

                def step(j, par, a=True, b=True, c=True):
                    i, g = j - 1, j - 2
                    if a:
                        chain_a.begin(j)
                        act.wait_ge(s["ch"], j + 1)
                        at_least(act, s["ssq"], j)
                        f(square[:, :], bank[0][:, 0:PAIR], ACT.Square).then_inc(s["sq"], 1)
                    if c:
                        hidden(g, 0)
                    if a:
                        act.wait_ge(s["ssq"], j + 1)
                        at_least(act, s["xn"], j)
                        chain_a.link(f(lnv[:, :], bank[1][:, 0:PAIR], ACT.Ln, bias=core.eps))
                        f(rstd[:, :], lnv[:, :], ACT.Exp, scale=-0.5).then_inc(s["rstd"], 1)
                        chain_a.link(f(rsq[:, :], lnv[:, :], ACT.Exp, scale=-1.0))
                        chain_a.link(f(rsq[:, :], rsq[:, :], ACT.Ln, scale=-EPS, bias=core.one_eps))
                        at_least(act, s["xh"], j)
                        f(rstd0[:, :], rsq[:, :], ACT.Exp, scale=-0.5).then_inc(s["r0"], 1)
                        act.wait_ge(s["xh"], j + 1)
                        at_least(act, s["qk"], 4 * j)
                        f(x0[:, :], xh[:, :], ACT.Identity, scale=ln0_w, bias=ln0_b).then_inc(s["x0"], 1)
                    if c:
                        hidden(g, 1)
                    if a:
                        at_least(act, s["scores"], 2 * j)
                        at_least(act, s["qs"], 2 * j)
                        for n, m in enumerate(QK_ORDER):
                            act.wait_ge(s["qk"], 4 * j + n + 1)
                            f(qk[:, m * PAIR:(m + 1) * PAIR], bank[4 + m][:, 0:PAIR], ACT.Exp,
                              bias=b_qk[:, m:m + 1]).then_inc(s["exp"], 1)
                        act.wait_ge(s["tr"], j + 1)
                        at_least(act, s["u"], 6 * j)
                        nc.scalar.copy(heads(xtok[:, :], 2), heads(bank[1][:, :], 2)[:, :, 0:P])
                        nc.scalar.copy(heads(xtok_r[:, :], 2), heads(bank[1][0:REM, :], 2)[:, :, P:2 * P]
                                       ).then_inc(s["xtok"], 1)
                    if c:
                        hidden(g, 2)
                    if a:
                        for half in range(2):
                            act.wait_ge(s["den"], 2 * j + half + 1)
                            ln_den = f(lnd[:, half * PAIR:(half + 1) * PAIR], bank[half][:, 0:PAIR], ACT.Ln)
                            if half:
                                chain_a.link(ln_den)
                        f(rden[:, :], lnd[:, :], ACT.Exp, scale=-1.0).then_inc(s["rden"], 1)
                        chain_a.end()
                    if c:
                        hidden(g, 3)
                    if b:
                        act.wait_ge(s["zc"], i + 1)
                        at_least(act, s["vsum"], i)
                        f(zz[:, :], z[1 - par][:, :], ACT.Square).then_inc(s["zz"], 1)
                        chain_b.begin(i)
                        act.wait_ge(s["var"], i + 1)
                        at_least(act, s["znorm"], i)
                        chain_b.link(f(lnz[:, :], bank[4][:, 0:PAIR], ACT.Ln, bias=core.eps))
                        f(rstdz[:, :], lnz[:, :], ACT.Exp, scale=-0.5).then_inc(s["rstdz"], 1)
                        chain_b.end()
                    if c:
                        act.wait_ge(s["w2"], g + 1)
                        at_least(act, s["out"], g)
                        f(r[:, :], bank[3][:, 0:PAIR], ACT.Relu, bias=b_2[:, 0:1]).then_inc(s["r"], 1)
                    if a:
                        for g_, (h0, h1) in enumerate(GROUPS):
                            act.wait_ge(s["u"], 6 * j + 3 + g_ + 1)
                            dst = u[:, :].rearrange("p (h b l) -> p h b l", h=HEADS, b=2)[:, h0:h1, 1]
                            nc.scalar.copy(dst, heads(bank[g_][:, 0:(h1 - h0) * L], h1 - h0)).then_inc(s["u1_out"], 1)
                    for h in range(HEADS):
                        x = slice(h * PAIR, (h + 1) * PAIR)
                        if a:
                            act.wait_ge(s["z"], 8 * j + h + 1)
                            f(z[par][:, x], bank[Z_BANK[h]][:, 0:PAIR], ACT.Identity,
                              bias=b_v[:, h:h + 1]).then_inc(s["z_out"], 1)
                        if b:
                            act.wait_ge(s["y"], 8 * i + h + 1)
                            nc.scalar.copy(y_hi[:, x], z[1 - par][:, x]).then_inc(s["y_hi"], 1)

                three(act, NPAIR, step)

            @block.vector
            def _(dve):
                tt, v = nc.vector.tensor_tensor, nc.vector
                dve.wait_ge(s["b1_sum"], 1)
                tt(b_1[:, :], b_1[:, :], bank[0][:, 0:4], ALU.add).then_inc(s["b1"], 1)
                dve.wait_ge(s["w1_hi"], 1)
                tt(w_1l[:, :], w_1[:, :], w_1h[:, :].bitcast(F32), ALU.subtract).then_inc(s["w1_lo"], 1)
                chain_a = Chain(dve, s["dve_a"], 3)

                def step(j, par, a=True, b=True, c=True):
                    i, g, zi = j - 1, j - 2, z[1 - par]
                    if a:
                        chain_a.begin(j)
                        dve.wait_ge(s["rstd"], j + 1)
                        tt(xn[par][:, :], bank[0][:, 0:PAIR], rstd[:, :], ALU.mult).then_inc(s["xn"], 1)
                        dve.wait_ge(s["xn"], j + 1)
                        dve.wait_ge(s["r0"], j + 1)
                        tt(xh[:, :], xn[par][:, :], rstd0[:, :], ALU.mult).then_inc(s["xh"], 1)
                        rows = hT[:, bass.ds(j * PAIR, PAIR)]
                        tt(rows, rows, xn[par][:, :], ALU.add).then_inc(s["hx"], 1)
                        q, kk = qk[:, 0:2 * PAIR], qk[:, 2 * PAIR:4 * PAIR]
                        dve.wait_ge(s["exp"], 4 * j + 2)
                        chain_a.link(v.tensor_scalar(kk, kk, CLIP_HI, CLIP_LO, ALU.min, ALU.max))
                        for n in range(4):
                            run = v.tensor_tensor_scan(ksum[:, n * L:(n + 1) * L], core.ones, kk[:, n * L:(n + 1) * L],
                                                       0.0, ALU.mult, ALU.add)
                        chain_a.link(run)
                        dve.wait_ge(s["exp"], 4 * j + 4)
                        chain_a.link(v.tensor_scalar(q, q, CLIP_HI, CLIP_LO, ALU.min, ALU.max))
                        for half in range(2):
                            nx = slice(half * PAIR, (half + 1) * PAIR)
                            tt(qc[:, nx], q[:, nx], ksum[:, nx], ALU.mult).then_inc(s["qc"], 1)
                        chain_a.end()
                    if b:
                        dve.wait_ge(s["mean"], i + 1)
                        tt(heads(zi[:, :], HEADS), heads(zi[:, :], HEADS), over(bank[0][:, 0:PAIR], HEADS),
                           ALU.subtract).then_inc(s["zc"], 1)
                    if a:
                        dve.wait_ge(s["rden"], j + 1)
                        for half in range(2):
                            nx = slice(half * PAIR, (half + 1) * PAIR)
                            tt(qs[:, nx], q[:, nx], rden[:, nx], ALU.mult).then_inc(s["qs"], 1)
                        for img in range(2):
                            dve.wait_ge(s["scores"], 2 * j + img + 1)
                            for r_ in range(4):
                                src = bank[4 * (1 - img) + r_]
                                dst = sc[img][:, :].rearrange("p (a r l) -> p r a l", a=2, r=4)[:, r_]
                                dst_r = sc_r[img][:, :].rearrange("p (a r l) -> p r a l", a=2, r=4)[:, r_]
                                tt(dst, heads(src[:, 0:2 * L], 2), over(core.mask, 2), ALU.mult)
                                last = tt(dst_r, heads(src[0:REM, 2 * L:2 * L + 2 * REM], 2), over(core.mask_r, 2),
                                          ALU.mult)
                            last.then_inc(s["mask"], 1)
                        for g_, (h0, h1) in enumerate(GROUPS):
                            dve.wait_ge(s["u"], 6 * j + g_ + 1)
                            dst = u[:, :].rearrange("p (h b l) -> p h b l", h=HEADS, b=2)[:, h0:h1, 0]
                            v.tensor_copy(dst, heads(bank[5 + g_][:, 0:(h1 - h0) * L], h1 - h0)).then_inc(s["u0_out"], 1)
                    if b:
                        dve.wait_ge(s["rstdz"], i + 1)
                        tt(heads(zi[:, :], HEADS), heads(zi[:, :], HEADS), over(rstdz[:, :], HEADS),
                           ALU.mult).then_inc(s["znorm"], 1)
                        dve.wait_ge(s["znorm"], i + 1)

                        def low(h):
                            x = slice(h * PAIR, (h + 1) * PAIR)
                            dve.wait_ge(s["y_hi"], 8 * i + h + 1)
                            tt(y_lo[:, x], zi[:, x], y_hi[:, x].bitcast(F32), ALU.subtract).then_inc(s["y_lo"], 1)

                        for h in range(HEADS):
                            x = slice(h * PAIR, (h + 1) * PAIR)
                            v.scalar_tensor_tensor(out=zi[:, x], in0=zi[:, x], scalar=ln1_w[:, h:h + 1],
                                                   in1=xn[1 - par][:, :], op0=ALU.mult, op1=ALU.add
                                                   ).then_inc(s["y"], 1)
                            if h >= 2:
                                low(h - 2)
                        low(HEADS - 2)
                        low(HEADS - 1)
                    if c:
                        dve.wait_ge(s["r"], g + 1)
                        rows = hT[:, bass.ds(g * PAIR, PAIR)]
                        tt(rows, rows, r[:, :], ALU.add).then_inc(s["out"], 1)

                three(dve, NPAIR, step)

        core.clear([s_w, *s.values()])
def experts(core):
    nc, hT, dram, bank = core.nc, core.hT, core.dram, core.bank
    E, NT = EXPERTS, CHUNK // P
    F32R = mybir.dt.float32r
    PIECE = 4 * P
    with ExitStack() as mem:
        sb = core.tiles("moe", mem)
        w_up, w_down = sb("w_up", P, E * 4 * P), sb("w_down", P, E * 2 * D)
        router, router_b, down_b, up_b = sb("router", P, E), sb("router_b", P, E), sb("down_b", E, D), sb("up_b", P, 4 * E)
        w_hi, w_lo = sb("w_hi", P, E * 4 * P, dt=F32R), sb("w_lo", P, E * 4 * P, dt=F32R)
        x_hi = [sb(f"x_hi{i}", P, CHUNK, dt=F32R) for i in range(2)]
        x_lo = [sb(f"x_lo{i}", P, CHUNK, dt=F32R) for i in range(2)]
        up_b1 = sb("up_b1", P, 4 * E)
        square, lnv, rstd = sb("square", P, CHUNK), sb("lnv", P, CHUNK), sb("rstd", P, CHUNK)
        xn = [sb(f"xn{i}", P, CHUNK) for i in range(2)]
        logits = sb("logits", P, NT * E)
        top, index = sb("top", P, NT * E), sb("index", P, NT * E, dt=U32)
        chosen = [sb(f"chosen{i}", P, NT * E) for i in range(2)]
        gap = [sb(f"gap{i}", P, NT) for i in range(2)]
        e2, w_a, w_b, pick = sb("e2", P, NT), sb("w_a", P, NT), sb("w_b", P, NT), sb("pick", P, NT * E)
        tokw, tokwT = sb("tokw", P, NT * E), sb("tokwT", E, CHUNK)
        gel = [sb(f"gel{i}", P, CHUNK) for i in range(2)]
        hid = [sb(f"hid{i}", P, 2 * CHUNK) for i in range(2)]
        acc = sb("acc", P, CHUNK)

        s_w = core.sem("moe_weights_in")
        names = ("w_hi w_lo x_hi x_lo lnv b1 ch sq ssq rstd xn router gap e2 tokw tokwT_ps tokwT up gelu hid down acc fin out chain_a chain_b")
        s = {n: core.sem("moe_" + n) for n in names.split()}

        with nc.Block() as block:
            @block.sync
            def _(sp):
                for dst, src in ((w_up, dram["moe_up"]), (w_down, dram["moe_down"]), (router, dram["moe_router"]),
                                 (router_b, dram["moe_router_b"].to_broadcast([P, E])),
                                 (down_b, dram["moe_down_b"]), (up_b, dram["moe_up_b"])):
                    sp.dma_start(dst[:, :], src).then_inc(s_w, 16)

            @block.gpsimd
            def _(pool):
                def step(j, par, k):
                    pool.wait_ge(s["x_hi"], j + 1)
                    at_least(pool, s["up"], 16 * (j - 1))
                    nc.gpsimd.tensor_tensor(x_lo[par][:, :], xn[par][:, :], x_hi[par][:, :].bitcast(F32), ALU.subtract
                                            ).then_inc(s["x_lo"], 1)

                steps(pool, NCHUNK, step)

            @block.tensor
            def _(pe):
                mm = nc.tensor.matmul
                pe.wait_ge(s_w, 16 * 6)

                def up(i, par, e):
                    for c in range(2):
                        n = 16 * i + 2 * e + c
                        at_least(pe, s["hid"], n - 1)
                        for kind in range(2):
                            m = 4 * e + 2 * kind + c
                            out, cut = bank[2 * c + kind][:, 0:CHUNK], slice(m * P, (m + 1) * P)
                            mm(out, w_lo[:, cut], x_hi[par][:, :], start=True, stop=False)
                            mm(out, w_hi[:, cut], x_lo[par][:, :], start=False, stop=False)
                            last = mm(out, w_hi[:, cut], x_hi[par][:, :], start=False, stop=True)
                        last.then_inc(s["up"], 1)

                def down(i, e):
                    pe.wait_ge(s["hid"], 16 * i + 2 * e + 2)
                    at_least(pe, s["acc"], 8 * i + e - 1)
                    for t in range(NT):
                        for c in range(2):
                            last = mm(bank[4 + e % 2][:, t * P:(t + 1) * P],
                                      hid[e % 2][:, c * CHUNK + t * P:c * CHUNK + (t + 1) * P],
                                      w_down[:, (2 * e + c) * D:(2 * e + c + 1) * D], start=c == 0, stop=c == 1)
                    last.then_inc(s["down"], 1)

                def step(j, par, a=True, b=True):
                    i, bpar = j - 1, 1 - par
                    if a:
                        at_least(pe, s["out"], j - 1)
                        mm(bank[6][:, 0:CHUNK], core.center, hT[:, bass.ds(j * CHUNK, CHUNK)],
                           start=True, stop=True).then_inc(s["ch"], 1)
                    if b:
                        pe.wait_ge(s["w_lo"], E)
                        pe.wait_ge(s["x_lo"], i + 1)
                        up(i, bpar, 0)
                    if a:
                        pe.wait_ge(s["sq"], j + 1)
                        at_least(pe, s["tokwT"], j - 1)
                        at_least(pe, s["gap"], j)
                        mm(bank[7][:, 0:CHUNK], core.mean, square[:, :], start=True, stop=True).then_inc(s["ssq"], 1)
                    if b:
                        for e in range(1, 4):
                            up(i, bpar, e)
                            down(i, e - 1)
                    if a:
                        pe.wait_ge(s["xn"], j + 1)
                        for t in range(NT):
                            last = mm(bank[7][:, t * E:(t + 1) * E], xn[par][:, t * P:(t + 1) * P], router[:, :],
                                      start=True, stop=True)
                        last.then_inc(s["router"], 1)
                    if b:
                        for e in range(4, E):
                            up(i, bpar, e)
                            down(i, e - 1)
                            if e == 4:
                                pe.wait_ge(s["tokw"], i + 1)
                                if a:
                                    pe.wait_ge(s["gap"], j + 1)
                                for t in range(NT):
                                    last = nc.tensor.transpose(bank[7][0:E, P + t * P:P + (t + 1) * P],
                                                               tokw[:, t * E:(t + 1) * E], core.ident)
                                last.then_inc(s["tokwT_ps"], 1)
                        down(i, E - 1)
                        pe.wait_ge(s["tokwT"], i + 1)
                        if not a:
                            pe.wait_ge(s["out"], i)
                        mm(bank[6][:, 0:CHUNK], down_b[:, :], tokwT[:, :], start=True, stop=False)
                        pe.wait_ge(s["acc"], 8 * i + 8)
                        for t in range(NT):
                            last = mm(bank[6][:, t * P:(t + 1) * P], acc[:, t * P:(t + 1) * P], core.ident,
                                      start=False, stop=t == NT - 1)
                        last.then_inc(s["fin"], 1)

                both(pe, NCHUNK, step)

            @block.scalar
            def _(act):
                f = nc.scalar.activation
                act.wait_ge(s_w, 16 * 6)

                def gelu(i, e, c):
                    n = 16 * i + 2 * e + c
                    act.wait_ge(s["up"], n + 1)
                    at_least(act, s["hid"], n - 1)
                    f(gel[c][:, :], bank[2 * c][:, 0:CHUNK], ACT.Gelu_apprx_sigmoid,
                      bias=up_b[:, 4 * e + c:4 * e + c + 1]).then_inc(s["gelu"], 1)

                def step(j, par, a=True, b=True):
                    i = j - 1
                    if a:
                        act.wait_ge(s["ch"], j + 1)
                        at_least(act, s["ssq"], j)
                        f(square[:, :], bank[6][:, 0:CHUNK], ACT.Square).then_inc(s["sq"], 1)
                    if b:
                        gelu(i, 0, 0)
                        gelu(i, 0, 1)
                    nc.scalar.preload_act_table_set("natural_log_exp_and_others")
                    if b:
                        act.wait_ge(s["gap"], i + 1)
                        at_least(act, s["tokw"], i)
                        f(e2[:, :], gap[1 - par][:, :], ACT.Exp).then_inc(s["e2"], 1)
                    if a:
                        act.wait_ge(s["ssq"], j + 1)
                        at_least(act, s["xn"], j)
                        f(lnv[:, :], bank[7][:, 0:CHUNK], ACT.Ln, bias=core.eps).then_inc(s["lnv"], 1)
                        act.wait_ge(s["lnv"], j + 1)
                        f(rstd[:, :], lnv[:, :], ACT.Exp, scale=-0.5).then_inc(s["rstd"], 1)
                    if b:
                        gelu(i, 1, 0)
                        gelu(i, 1, 1)
                    if a:
                        if not b:
                            for e in range(E):
                                piece = slice(e * PIECE, (e + 1) * PIECE)
                                nc.scalar.copy(w_hi[:, piece], w_up[:, piece]).then_inc(s["w_hi"], 1)
                        act.wait_ge(s["xn"], j + 1)
                        at_least(act, s["up"], 16 * (j - 1))
                        nc.scalar.copy(x_hi[par][:, :], xn[par][:, :]).then_inc(s["x_hi"], 1)
                    if b:
                        for e in range(2, E):
                            gelu(i, e, 0)
                            gelu(i, e, 1)

                both(act, NCHUNK, step)

            @block.vector
            def _(dve):
                tt, v = nc.vector.tensor_tensor, nc.vector
                dve.wait_ge(s_w, 16 * 6)
                v.tensor_scalar(up_b1[:, :], up_b[:, :], 1.0, None, ALU.add).then_inc(s["b1"], 1)
                dve.wait_ge(s["b1"], 1)
                by_tile = lambda ap: heads(ap[:, :], NT)
                wide = lambda ap: ap.unsqueeze(2).to_broadcast([P, NT, E])
                chain_a, chain_b = LocalChain(dve, s["chain_a"]), Chain(dve, s["chain_b"], 5)

                def hidden(i, e, c):
                    dve.wait_ge(s["gelu"], 16 * i + 2 * e + c + 1)
                    if c == 0:
                        at_least(dve, s["down"], 8 * i + e - 1)
                    m = 4 * e + 2 + c
                    v.scalar_tensor_tensor(out=hid[e % 2][:, c * CHUNK:(c + 1) * CHUNK], in0=bank[2 * c + 1][:, 0:CHUNK],
                                           scalar=up_b1[:, m:m + 1], in1=gel[c][:, :], op0=ALU.add,
                                           op1=ALU.mult).then_inc(s["hid"], 1)

                def add(i, e):
                    dve.wait_ge(s["down"], 8 * i + e + 1)
                    if e:
                        dve.wait_ge(s["acc"], 8 * i + e)
                    else:
                        at_least(dve, s["fin"], i)
                    for t in range(NT):
                        cut, w = slice(t * P, (t + 1) * P), tokw[:, t * E + e:t * E + e + 1]
                        src = bank[4 + e % 2][:, cut]
                        if e:
                            last = v.scalar_tensor_tensor(out=acc[:, cut], in0=src, scalar=w, in1=acc[:, cut],
                                                          op0=ALU.mult, op1=ALU.add)
                        else:
                            last = v.tensor_scalar(acc[:, cut], src, w, None, ALU.mult)
                    last.then_inc(s["acc"], 1)

                def step(j, par, a=True, b=True):
                    i = j - 1
                    if b:
                        hidden(i, 0, 0)
                        hidden(i, 0, 1)
                        first, second = (by_tile(chosen[1 - par])[:, :, n] for n in range(2))
                        chain_b.begin(i)
                        dve.wait_ge(s["e2"], i + 1)
                        chain_b.link(v.tensor_scalar(w_a[:, :], e2[:, :], 1.0, None, ALU.add))
                        chain_b.link(v.reciprocal(w_a[:, :], w_a[:, :]))
                        chain_b.link(tt(w_b[:, :], w_a[:, :], e2[:, :], ALU.mult))
                        at_least(dve, s["tokwT_ps"], i)
                        tt(by_tile(tokw), over(core.iota, NT), wide(first), ALU.is_equal)
                        chain_b.link(tt(by_tile(pick), over(core.iota, NT), wide(second), ALU.is_equal))
                        tt(by_tile(tokw), by_tile(tokw), wide(w_a[:, :]), ALU.mult)
                        chain_b.link(tt(by_tile(pick), by_tile(pick), wide(w_b[:, :]), ALU.mult))
                        tt(tokw[:, :], tokw[:, :], pick[:, :], ALU.add).then_inc(s["tokw"], 1)
                        dve.wait_ge(s["tokw"], i + 1)
                        chain_b.end()
                    if a:
                        dve.wait_ge(s["rstd"], j + 1)
                        at_least(dve, s["x_lo"], j - 1)
                        at_least(dve, s["router"], j - 1)
                        tt(xn[par][:, :], bank[6][:, 0:CHUNK], rstd[:, :], ALU.mult).then_inc(s["xn"], 1)
                        if not b:
                            for e in range(E):
                                piece = slice(e * PIECE, (e + 1) * PIECE)
                                dve.wait_ge(s["w_hi"], e + 1)
                                tt(w_lo[:, piece], w_up[:, piece], w_hi[:, piece].bitcast(F32), ALU.subtract
                                   ).then_inc(s["w_lo"], 1)
                    if b:
                        for e in range(1, 4):
                            hidden(i, e, 0)
                            hidden(i, e, 1)
                            add(i, e - 1)
                    if a:
                        chain_a.begin()
                        dve.wait_ge(s["router"], j + 1)
                        chain_a.link(tt(by_tile(logits), heads(bank[7][:, 0:NT * E], NT), over(router_b[:, :], NT), ALU.add))
                        for t in range(NT):
                            last = v.max(top[:, t * E:(t + 1) * E], logits[:, t * E:(t + 1) * E])
                        chain_a.link(last)
                        for t in range(NT):
                            last = v.max_index(index[:, t * E:(t + 1) * E], top[:, t * E:(t + 1) * E],
                                               logits[:, t * E:(t + 1) * E])
                        chain_a.link(last)
                        v.tensor_copy(chosen[par][:, :], index[:, :])
                        tt(gap[par][:, :], by_tile(top)[:, :, 1], by_tile(top)[:, :, 0], ALU.subtract
                           ).then_inc(s["gap"], 1)
                    if b:
                        for e in range(4, E):
                            hidden(i, e, 0)
                            hidden(i, e, 1)
                            add(i, e - 1)
                            if e == 4:
                                dve.wait_ge(s["tokwT_ps"], i + 1)
                                at_least(dve, s["fin"], i)
                                v.tensor_copy(tokwT[:, :], bank[7][0:E, P:P + CHUNK]).then_inc(s["tokwT"], 1)
                        add(i, E - 1)
                        dve.wait_ge(s["fin"], i + 1)
                        rows = hT[:, bass.ds(i * CHUNK, CHUNK)]
                        tt(rows, rows, bank[6][:, 0:CHUNK], ALU.add).then_inc(s["out"], 1)

                both(dve, NCHUNK, step)


QUAD = 4 * L
NQUAD = NIMG // 4


def halves(double_bank):
    return heads(double_bank, 2)[:, :, 0:PAIR]


def images(double_bank):
    return double_bank.rearrange("p (h x) -> p h x", h=2)[:, :, 0:PAIR].rearrange("p h (b l) -> p h b l", b=2)


def project(core, out, lhsT, rhs, start=True, stop=True):
    for half in range(2):
        last = core.nc.tensor.matmul(out[:, 512 * half:512 * half + PAIR], lhsT, rhs(half), start=start, stop=stop)
    return last


def quad(tile, j):
    return tile[:, bass.ds(j * QUAD, QUAD)]


def half_of(tile, j=None):
    if j is None:
        return lambda half: tile[:, half * PAIR:(half + 1) * PAIR]
    return lambda half: tile[:, bass.ds(j * QUAD + half * PAIR, PAIR)]


def convolve(core, res):
    nc, hT, dram, dbl = core.nc, core.hT, core.dram, core.dbl
    PAD = TAPS - 1
    with ExitStack() as mem:
        sb = core.tiles("conv", mem)
        taps = sb("taps", P, TAPS + 1)
        padded = sb("padded", P, 4 * (L + PAD))
        square, lnv, rstd = sb("square", P, QUAD), sb("lnv", P, QUAD), sb("rstd", P, QUAD)
        qsq, qss, lnq, rnorm = sb("qsq", P, QUAD), sb("qss", P, QUAD), sb("lnq", P, QUAD), sb("rnorm", P, QUAD)
        s_w = core.sem("conv_weights_in")
        s = {n: core.sem("conv_" + n) for n in
             "pad ch sq ssq rstd xn x q qsq qss bounded rnorm qn dve_a act_a act_b".split()}

        with nc.Block() as block:
            @block.sync
            def _(sp):
                sp.dma_start(taps[:, :], dram["mem_conv"]).then_inc(s_w, 16)
                sp.dma_start(res["w"][:, :], dram["mem_w"]).then_inc(s_w, 16)

            @block.gpsimd
            def _(pool):
                nc.gpsimd.memset(padded[:, :], 0.0).then_inc(s["pad"], 1)

            @block.tensor
            def _(pe):
                pe.wait_ge(s_w, 16 * 2)

                def step(j, par, a=True, b=True, c=True):
                    i, g = j - 1, j - 2
                    if b:
                        pe.wait_ge(s["sq"], i + 1)
                        at_least(pe, s["rstd"], i)
                        project(core, dbl[1], core.mean, half_of(square)).then_inc(s["ssq"], 1)
                    if c:
                        pe.wait_ge(s["x"], g + 1)
                        at_least(pe, s["qn"], g)
                        project(core, dbl[2], res["w"][:, 0:P], half_of(res["x"], g)).then_inc(s["q"], 1)
                    if a:
                        at_least(pe, s["xn"], j)
                        project(core, dbl[0], core.center, half_of(hT, j)).then_inc(s["ch"], 1)
                    if c:
                        pe.wait_ge(s["qsq"], g + 1)
                        at_least(pe, s["bounded"], g)
                        project(core, dbl[3], core.mean, half_of(qsq)).then_inc(s["qss"], 1)

                three(pe, NQUAD, step)

            @block.scalar
            def _(act):
                f = nc.scalar.activation
                nc.scalar.preload_act_table_set("natural_log_exp_and_others")
                chain_a, chain_b = Chain(act, s["act_a"], 1), Chain(act, s["act_b"], 1)

                def step(j, par, a=True, b=True, c=True):
                    i, g = j - 1, j - 2
                    if b:
                        chain_a.begin(i)
                        act.wait_ge(s["ssq"], i + 1)
                        at_least(act, s["xn"], i)
                        chain_a.link(f(heads(lnv[:, :], 2), halves(dbl[1]), ACT.Ln, bias=core.eps))
                        f(rstd[:, :], lnv[:, :], ACT.Exp, scale=-0.5).then_inc(s["rstd"], 1)
                    if c:
                        act.wait_ge(s["q"], g + 1)
                        at_least(act, s["qss"], g)
                        f(heads(qsq[:, :], 2), halves(dbl[2]), ACT.Square).then_inc(s["qsq"], 1)
                    if a:
                        act.wait_ge(s["ch"], j + 1)
                        at_least(act, s["ssq"], j)
                        f(heads(square[:, :], 2), halves(dbl[0]), ACT.Square).then_inc(s["sq"], 1)
                    if c:
                        chain_b.begin(g)
                        act.wait_ge(s["bounded"], g + 1)
                        at_least(act, s["qn"], g)
                        chain_b.link(f(lnq[:, :], qss[:, :], ACT.Ln, scale=float(D * 2 ** 20)))
                        f(rnorm[:, :], lnq[:, :], ACT.Exp, scale=-0.5, bias=core.ln1024).then_inc(s["rnorm"], 1)

                three(act, NQUAD, step)

            @block.vector
            def _(dve):
                tt, v = nc.vector.tensor_tensor, nc.vector
                dve.wait_ge(s_w, 16 * 2)
                dve.wait_ge(s["pad"], 1)
                chain_a = Chain(dve, s["dve_a"], 3)
                shifted = lambda t: heads(padded[:, :], 4)[:, :, t:t + L]

                def step(j, par, a=True, b=True, c=True):
                    i, g = j - 1, j - 2
                    if b:
                        chain_a.begin(i)
                        dve.wait_ge(s["rstd"], i + 1)
                        at_least(dve, s["x"], i)
                        tt(heads(padded[:, :], 4)[:, :, PAD:].rearrange("p (h b) l -> p h b l", h=2), images(dbl[0]),
                           rstd[:, :].rearrange("p (h b l) -> p h b l", h=2, b=2), ALU.mult).then_inc(s["xn"], 1)
                        out = heads(quad(res["x"], i), 4)
                        dve.wait_ge(s["xn"], i + 1)
                        chain_a.link(v.tensor_scalar(out, shifted(0), taps[:, 0:1], taps[:, TAPS:TAPS + 1],
                                                     ALU.mult, ALU.add))
                        for t in range(1, TAPS):
                            conv = v.scalar_tensor_tensor(out=out, in0=shifted(t), scalar=taps[:, t:t + 1], in1=out,
                                                          op0=ALU.mult, op1=ALU.add)
                            if t < TAPS - 1:
                                chain_a.link(conv)
                        conv.then_inc(s["x"], 1)
                        chain_a.end()
                    if c:
                        dve.wait_ge(s["qss"], g + 1)
                        at_least(dve, s["rnorm"], g)
                        v.tensor_scalar(heads(qss[:, :], 2), halves(dbl[3]), 1e-24 / D, None, ALU.max
                                        ).then_inc(s["bounded"], 1)
                        dve.wait_ge(s["rnorm"], g + 1)
                        tt(heads(quad(res["q"], g), 2), halves(dbl[2]), heads(rnorm[:, :], 2), ALU.mult
                           ).then_inc(s["qn"], 1)

                three(dve, NQUAD, step)


def gates(core, res):
    nc, dbl = core.nc, core.dbl
    with ExitStack() as mem:
        sb = core.tiles("gate", mem)
        g = [[sb(f"g{n}{par}", P, QUAD) for par in range(2)] for n in range(2)]
        pre = [sb(f"pre{n}", P, QUAD) for n in range(2)]
        th = [sb(f"tanh{n}", P, QUAD) for n in range(2)]
        total = [sb(f"total{n}", P, QUAD) for n in range(2)]
        two = [sb(f"two{n}", P, PAIR) for n in range(2)]
        one = [sb(f"one{n}", P, L) for n in range(2)]
        eta, alpha, zeros = sb("eta", P, L), sb("alpha", P, L), sb("zeros", P, L)
        s = {n: core.sem("gate_" + n) for n in "hid gelu out pre tanh sum clear fold mean read scan".split()}
        w = lambda n, layer: res["w"][:, (1 + 2 * n + layer) * P:(2 + 2 * n + layer) * P]

        with nc.Block() as block:
            @block.tensor
            def _(pe):
                def step(j, par, a=True, b=True):
                    i = j - 1
                    if a:
                        for n in range(2):
                            at_least(pe, s["gelu"], 2 * (j - 1) + n + 1)
                            project(core, dbl[n], w(n, 0), half_of(res["x"], j)).then_inc(s["hid"], 1)
                    if b:
                        for n in range(2):
                            pe.wait_ge(s["gelu"], 2 * i + n + 1)
                            at_least(pe, s["pre"], 2 * (i - 1) + n + 1)
                            project(core, dbl[2 + n], w(n, 1), half_of(g[n][1 - par])).then_inc(s["out"], 1)

                both(pe, NQUAD, step)
                for n in range(2):
                    pe.wait_ge(s["fold"], 2 * n + 2)
                    nc.tensor.matmul(core.bank[n][:, 0:L], core.mean, one[n][:, :], start=True, stop=True
                                     ).then_inc(s["mean"], 1)

            @block.scalar
            def _(act):
                f = nc.scalar.activation
                nc.scalar.preload_act_table_set("gelu_and_others")

                def step(j, par, a=True, b=True):
                    i = j - 1
                    if a:
                        for n in range(2):
                            act.wait_ge(s["hid"], 2 * j + n + 1)
                            at_least(act, s["out"], 2 * (j - 2) + n + 1)
                            f(heads(g[n][par][:, :], 2), halves(dbl[n]), ACT.Gelu).then_inc(s["gelu"], 1)
                    if b:
                        for n in range(2):
                            act.wait_ge(s["pre"], 2 * i + n + 1)
                            at_least(act, s["sum"], 2 * (i - 1) + n + 1)
                            f(th[n][:, :], pre[n][:, :], ACT.Tanh, scale=0.5).then_inc(s["tanh"], 1)

                both(act, NQUAD, step)

            @block.vector
            def _(dve):
                tt, v = nc.vector.tensor_tensor, nc.vector
                v.memset(zeros[:, :], 0.0)
                v.memset(res["decay"][:, 0:1], 1.0)
                v.memset(res["shift"][:, 0:1], 0.0)

                def step(j, par, a=True, b=True):
                    i = j - 1
                    if b:
                        for n in range(2):
                            dve.wait_ge(s["out"], 2 * i + n + 1)
                            at_least(dve, s["tanh"], 2 * (i - 1) + n + 1)
                            tt(heads(pre[n][:, :], 2), halves(dbl[2 + n]), heads(quad(res["x"], i), 2), ALU.add
                               ).then_inc(s["pre"], 1)

                both(dve, NQUAD, step)
                for n in range(2):
                    dve.wait_ge(s["mean"], n + 1)
                v.tensor_scalar(eta[:, :], core.bank[0][:, 0:L], 0.01 * 0.5 / NIMG, 0.01 * 0.5, ALU.mult, ALU.add)
                v.tensor_scalar(alpha[:, :], core.bank[1][:, 0:L], 0.5 / NIMG, 0.5, ALU.mult, ALU.add
                                ).then_inc(s["read"], 1)
                dve.wait_ge(s["read"], 1)
                v.tensor_tensor_scan(res["decay"][:, 1:L], alpha[:, 0:L - 1], zeros[:, 0:L - 1], 1.0, ALU.mult, ALU.add)
                v.tensor_tensor_scan(res["shift"][:, 1:L], alpha[:, 0:L - 1], eta[:, 0:L - 1], 0.0, ALU.mult, ALU.add)

            @block.gpsimd
            def _(pool):
                for n in range(2):
                    nc.gpsimd.memset(total[n][:, :], 0.0).then_inc(s["clear"], 1)
                pool.wait_ge(s["clear"], 2)

                def step(j, par, a=True, b=True):
                    i = j - 1
                    if b:
                        for n in range(2):
                            pool.wait_ge(s["tanh"], 2 * i + n + 1)
                            at_least(pool, s["sum"], 2 * i + n - 1)
                            nc.gpsimd.tensor_tensor(total[n][:, :], total[n][:, :], th[n][:, :], ALU.add
                                                    ).then_inc(s["sum"], 1)

                both(pool, NQUAD, step)
                pool.wait_ge(s["sum"], 2 * NQUAD)
                for n in range(2):
                    nc.gpsimd.tensor_tensor(two[n][:, :], total[n][:, 0:PAIR], total[n][:, PAIR:], ALU.add
                                            ).then_inc(s["fold"], 1)
                    pool.wait_ge(s["fold"], 2 * n + 1)
                    nc.gpsimd.tensor_tensor(one[n][:, :], two[n][:, 0:L], two[n][:, L:], ALU.add
                                            ).then_inc(s["fold"], 1)


def recall(core, res):
    nc, hT, dbl = core.nc, core.hT, core.dbl
    with ExitStack() as mem:
        sb = core.tiles("recall", mem)
        qd, qs = sb("q_decay", P, QUAD), sb("q_shift", P, QUAD)
        gd, gs = sb("g_decay", P, QUAD), sb("g_shift", P, QUAD)
        g = [sb(f"g{i}", P, QUAD) for i in range(2)]
        o = sb("o", P, QUAD)
        s = {n: core.sem("recall_" + n) for n in "q hid gelu g out o stored".split()}
        w = lambda layer: res["w"][:, (5 + layer) * P:(6 + layer) * P]

        with nc.Block() as block:
            @block.tensor
            def _(pe):
                def step(j, par, a=True, b=True, c=True):
                    i = j - 1
                    if a:
                        pe.wait_ge(s["q"], j + 1)
                        at_least(pe, s["gelu"], j)
                        for half in range(2):
                            out = dbl[0][:, 512 * half:512 * half + PAIR]
                            nc.tensor.matmul(out, w(0), half_of(qd)(half), start=True, stop=False)
                            last = nc.tensor.matmul(out, core.neg1, half_of(qs)(half), start=False, stop=True)
                        last.then_inc(s["hid"], 1)
                    if b:
                        pe.wait_ge(s["g"], i + 1)
                        at_least(pe, s["o"], i - 1)
                        for half in range(2):
                            out = dbl[2 - par][:, 512 * half:512 * half + PAIR]
                            nc.tensor.matmul(out, w(1), half_of(gd)(half), start=True, stop=False)
                            last = nc.tensor.matmul(out, core.neg1, half_of(gs)(half), start=False, stop=True)
                        last.then_inc(s["out"], 1)

                three(pe, NQUAD, step)

            @block.scalar
            def _(act):
                def step(j, par, a=True, b=True):
                    if a:
                        act.wait_ge(s["hid"], j + 1)
                        at_least(act, s["g"], j - 1)
                        nc.scalar.activation(heads(g[par][:, :], 2), halves(dbl[0]), ACT.Gelu).then_inc(s["gelu"], 1)

                both(act, NQUAD, step)

            @block.vector
            def _(dve):
                tt = nc.vector.tensor_tensor
                by = lambda tile: over(tile[:, :], 4)

                def step(j, par, a=True, b=True, c=True):
                    i, n = j - 1, j - 2
                    if a:
                        at_least(dve, s["hid"], j)
                        q = heads(quad(res["q"], j), 4)
                        tt(heads(qd[:, :], 4), q, by(res["decay"]), ALU.mult)
                        tt(heads(qs[:, :], 4), q, by(res["shift"]), ALU.mult).then_inc(s["q"], 1)
                    if b:
                        dve.wait_ge(s["gelu"], i + 1)
                        at_least(dve, s["out"], i)
                        gi = heads(g[1 - par][:, :], 4)
                        tt(heads(gd[:, :], 4), gi, by(res["decay"]), ALU.mult)
                        tt(heads(gs[:, :], 4), gi, by(res["shift"]), ALU.mult).then_inc(s["g"], 1)
                    if c:
                        dve.wait_ge(s["out"], n + 1)
                        at_least(dve, s["stored"], n)
                        tt(heads(o[:, :], 2), halves(dbl[1 + par]), heads(quad(res["q"], n), 2), ALU.add
                           ).then_inc(s["o"], 1)
                        dve.wait_ge(s["o"], n + 1)
                        tt(quad(hT, n), quad(hT, n), o[:, :], ALU.add).then_inc(s["stored"], 1)

                three(dve, NQUAD, step)


def renorm(core, res):
    nc, hT, dbl = core.nc, core.hT, core.dbl
    with ExitStack() as mem:
        sb = core.tiles("renorm", mem)
        square = [sb(f"square{i}", P, QUAD) for i in range(2)]
        lnv, rstd = sb("lnv", P, QUAD), sb("rstd", P, QUAD)
        s = {n: core.sem("renorm_" + n) for n in "ch sq ssq lnv rstd xn".split()}
        with nc.Block() as block:
            @block.tensor
            def _(pe):
                def step(j, par, a=True, b=True):
                    i = j - 1
                    if a:
                        at_least(pe, s["xn"], j - 1)
                        project(core, dbl[par], core.center, half_of(hT, j)).then_inc(s["ch"], 1)
                    if b:
                        pe.wait_ge(s["sq"], i + 1)
                        at_least(pe, s["rstd"], i - 1)
                        project(core, dbl[3 - par], core.mean, half_of(square[1 - par])).then_inc(s["ssq"], 1)

                both(pe, NQUAD, step)

            @block.scalar
            def _(act):
                f = nc.scalar.activation
                nc.scalar.preload_act_table_set("natural_log_exp_and_others")

                def step(j, par, a=True, b=True):
                    i = j - 1
                    if a:
                        act.wait_ge(s["ch"], j + 1)
                        at_least(act, s["ssq"], j - 1)
                        f(heads(square[par][:, :], 2), halves(dbl[par]), ACT.Square).then_inc(s["sq"], 1)
                    if b:
                        act.wait_ge(s["ssq"], i + 1)
                        at_least(act, s["xn"], i)
                        f(heads(lnv[:, :], 2), halves(dbl[3 - par]), ACT.Ln, bias=core.eps).then_inc(s["lnv"], 1)
                        act.wait_ge(s["lnv"], i + 1)
                        f(rstd[:, :], lnv[:, :], ACT.Exp, scale=-0.5).then_inc(s["rstd"], 1)

                both(act, NQUAD, step)

            @block.vector
            def _(dve):
                def step(j, par, a=True, b=True):
                    i = j - 1
                    if b:
                        dve.wait_ge(s["rstd"], i + 1)
                        nc.vector.tensor_tensor(heads(quad(res["x"], i), 2), halves(dbl[1 - par]), heads(rstd[:, :], 2),
                                                ALU.mult).then_inc(s["xn"], 1)

                both(dve, NQUAD, step)


def memory(core):
    res = {"x": core.sb("x", [P, TOK]), "decay": core.sb("decay", [P, L]), "shift": core.sb("shift", [P, L])}
    core.x = res["x"]
    with ExitStack() as mem:
        res["q"] = core.sb("q", [P, TOK], mem)
        res["w"] = core.sb("mem_w", [P, 7 * P], mem)
        convolve(core, res)
        gates(core, res)
        recall(core, res)
        renorm(core, res)


def normal_tail(p):
    lo, hi = -8.0, 8.0
    for _ in range(60):
        mid = (lo + hi) / 2
        lo, hi = (mid, hi) if 0.5 * math.erfc(mid / math.sqrt(2.0)) > p else (lo, mid)
    return lo, math.exp(-lo * lo / 2) / math.sqrt(2 * math.pi)


class TopK:

    def __init__(self, width, k, rounds, goal, damping, floor=None):
        self.width, self.k, self.rounds, self.floor = width, k, rounds, floor
        z, density = normal_tail(goal / width)
        sigma = math.sqrt(2 * math.pi) / width
        self.guess = z * sigma
        self.extra = float(width - 2 * goal)
        self.slopes = [d * sigma / (width * density) / 2 for d in damping]


TAKEN = -1.6e38
SEL_IN = TopK(NIN, K_IN, 2, 55, (1.0, 0.6))
SEL_PROC = TopK(NPROC, K_PROC, 4, 117, (0.8,), floor=1e-30)
SEL_OUT = TopK(NOUT, K_OUT, 2, 55, (1.0, 0.6))


def patterns(core):
    nc, hT, dram, bank = core.nc, core.hT, core.dram, core.bank
    NT = CHUNK // P
    with ExitStack() as mem:
        sb = core.tiles("pat", mem)
        w_in, w_proc, w_val = sb("w_in", P, NIN), sb("w_proc", P, NIN // P * NPROC), sb("w_val", P, NPROC // P * DPV)
        w_ow, w_out = sb("w_ow", DPV, NOUT), sb("w_out", P, NOUT // P * D)
        xs = [sb(f"xs{i}", P, CHUNK) for i in range(2)]
        hs = [sb(f"hs{i}", P, CHUNK) for i in range(2)]
        act_in = [sb(f"act_in{i}", P, NT * NIN) for i in range(2)]
        act_proc = [sb(f"act_proc{i}", P, NT * NPROC) for i in range(2)]
        act_out = [sb(f"act_out{i}", P, NT * NOUT) for i in range(2)]
        sum_in = [sb(f"sum_in{i}", P, NT) for i in range(2)]
        sum_proc, sum_out = [sb(f"sum_proc{i}", P, NT) for i in range(2)], [sb(f"sum_out{i}", P, NT) for i in range(2)]
        signs = sb("signs", P, NOUT)
        neg_in = [[sb(f"neg_in{i}{c}", P, NT) for c in range(2)] for i in range(2)]
        neg_proc = [[sb(f"neg_proc{i}", P, NT)] for i in range(2)]
        neg_out = [[sb(f"neg_out{i}{c}", P, NT) for c in range(2)] for i in range(2)]
        signs_in = [[sb(f"signs_in{i}{c}", P, NT) for c in range(2)] for i in range(2)]
        signs_proc = [[sb(f"signs_proc{i}", P, NT)] for i in range(2)]
        signs_out = [[sb(f"signs_out{i}{c}", P, NT) for c in range(2)] for i in range(2)]
        slope, offset = sb("slope", P, NT), sb("offset", P, NT)
        thr, count, togo = sb("thr", P, NT), sb("count", P, NT), sb("togo", P, NT)
        off, far = sb("off", P, NT), sb("far", P, NT)
        rank = [sb(f"rank{t}", P, 8 * SEL_PROC.rounds) for t in range(NT)]
        redo = sb("redo", 1, NT + 1)
        carrier, best = sb("carrier", P, 4 + NT), sb("best", P, NT)
        top, masked = [sb(f"top{t}", P, 8) for t in range(NT)], [sb(f"masked{t}", P, 8) for t in range(NT)]
        left_in, left_proc, left_out = ([sb(f"left_{n}{t}", P, w) for t in range(NT)]
                                        for n, w in (("in", NIN), ("proc", NPROC), ("out", NOUT)))
        kept_in, kept_out = sb("kept_in", P, NT * NIN), sb("kept_out", P, NT * NOUT)
        keptT = [sb(f"keptT{i}", P, NIN) for i in range(2)]
        expo = [sb(f"expo{i}", P, NT * NPROC) for i in range(2)]
        neg_best, prob, probT = sb("neg_best", P, NT), sb("prob", P, NT * NPROC), sb("probT", P, NPROC)
        psums, rsum = sb("prob_sums", P, NT), sb("rsum", P, NT)
        aggT, outT = sb("aggT", DPV, P), [sb(f"outT{i}", P, NOUT) for i in range(2)]
        final = [sb(f"final{i}", P, CHUNK) for i in range(2)]

        s_w = core.sem("pat_weights_in")
        s_dram = [core.sem(f"pat_stored{i}") for i in range(2)]
        names = ("xs hs act gelu kept_in tr_in keptT proc act_proc best neg_best expo prob tr_prob probT agg aggT "
                 "out act_out kept_out tr_out outT fin final guess_in guess_proc guess_out signs_in signs_proc signs_out far flags "
                 "chain redone")
        s = {n: core.sem("pat_" + n) for n in names.split()}

        def chunks(eng, step):
            for j in range(4):
                step(j, j % 2, j // 2, 3)
            with eng.Fori(0, (NCHUNK - 8) // 2) as t:
                step(t * 2 + 4, 0, t + 2, 3)
                step(t * 2 + 5, 1, t + 2, 3)
            for j in range(NCHUNK - 4, NCHUNK):
                step(j, j % 2, j // 2, NCHUNK - 1 - j)

        def one_ahead(turn, multiply, flag=None):
            turn(0)
            for t in range(NT):
                if t == 1 and flag is not None:
                    flag()
                if t < NT - 1:
                    turn(t + 1)
                multiply(t)

        def at(j, value):
            return isinstance(j, int) and j == value

        def phase(kind, j, more):
            if at(j, 0):
                return {"proc": 2, "in": 3}[kind]
            return 3 * j + (1 if more else 0) + {"proc": 0, "in": 1, "out": 2 if more >= 2 else 1}[kind]

        with nc.Block() as block:
            @block.sync
            def _(sp):
                for dst, name in ((w_in, "pat_in"), (w_proc, "pat_proc"), (w_val, "pat_val"), (w_ow, "pat_ow"),
                                  (w_out, "pat_out")):
                    sp.dma_start(dst[:, :], dram[name]).then_inc(s_w, 16)

                def step(j, par, k, more):
                    sp.wait_ge(s["final"], NT * (j + 1))
                    rows = dram["out"][bass.ds(j * CHUNK, CHUNK), :].rearrange("(t p) d -> p t d", p=P)
                    sp.dma_start(rows, heads(final[par][:, :], NT)).then_inc(s_dram[par], 16)

                chunks(sp, step)
                for par in range(2):
                    sp.wait_ge(s_dram[par], 16 * (NCHUNK // 2))

            @block.gpsimd
            def _(pool):
                def stage_x(j, par):
                    at_least(pool, s["act"], NT * (j - 1))
                    nc.gpsimd.tensor_copy(xs[par][:, :], core.x[:, bass.ds(j * CHUNK, CHUNK)]).then_inc(s["xs"], 1)

                def step(j, par, k, more):
                    at_least(pool, s["fin"], NT * (j - 1))
                    nc.gpsimd.tensor_copy(hs[par][:, :], hT[:, bass.ds(j * CHUNK, CHUNK)]).then_inc(s["hs"], 1)
                    if more == 3:
                        stage_x(j + 3, 1 - par)

                stage_x(0, 0)
                stage_x(1, 1)
                stage_x(2, 0)
                chunks(pool, step)

            @block.tensor
            def _(pe):
                mm, tr = nc.tensor.matmul, nc.tensor.transpose
                pe.wait_ge(s_w, 16 * 5)

                def flags(number):
                    pe.wait_ge(s["far"], number + 1)
                    at_least(pe, s["redone"], number)
                    mm(bank[6][0:1, 0:NT], core.ones[:, 0:1], far[:, :], start=True, stop=True
                       ).then_inc(s["flags"], 1)

                def first(j, par):
                    pe.wait_ge(s["xs"], j + 1)
                    for t in range(NT):
                        n = NT * j + t
                        at_least(pe, s["gelu"], n)
                        mm(bank[0], xs[par][:, t * P:(t + 1) * P], w_in[:, :], start=True, stop=True).then_inc(s["act"], 1)

                def process(j, par, flagged=None):
                    def turn(t):
                        n = NT * j + t
                        pe.wait_ge(s["kept_in"], n + 1)
                        at_least(pe, s["keptT"], n)
                        for c in range(NIN // P):
                            last = tr(bank[2][:, c * P:(c + 1) * P], kept_in[:, t * NIN + c * P:t * NIN + (c + 1) * P],
                                      core.ident)
                        last.then_inc(s["tr_in"], 1)

                    def multiply(t):
                        n = NT * j + t
                        pe.wait_ge(s["keptT"], n + 1)
                        at_least(pe, s["act_proc"], n)
                        for c in range(NIN // P):
                            last = mm(bank[3][:, 0:NPROC], keptT[(par + t) % 2][:, c * P:(c + 1) * P],
                                      w_proc[:, c * NPROC:(c + 1) * NPROC], start=c == 0, stop=c == NIN // P - 1)
                        last.then_inc(s["proc"], 1)

                    one_ahead(turn, multiply, None if flagged is None else lambda: flags(flagged))

                def final_products(c, fpar, flagged=None):
                    def turn(t):
                        n = NT * c + t
                        pe.wait_ge(s["kept_out"], n + 1)
                        at_least(pe, s["outT"], n)
                        for m in range(NOUT // P):
                            last = tr(bank[1][:, m * P:(m + 1) * P], kept_out[:, t * NOUT + m * P:t * NOUT + (m + 1) * P],
                                      core.ident)
                        last.then_inc(s["tr_out"], 1)

                    def multiply(t):
                        n = NT * c + t
                        pe.wait_ge(s["outT"], n + 1)
                        at_least(pe, s["final"], n)
                        for m in range(NOUT // P):
                            mm(bank[7][:, 0:D], outT[(fpar + t) % 2][:, m * P:(m + 1) * P],
                               w_out[:, m * D:(m + 1) * D], start=m == 0, stop=False)
                        mm(bank[7][:, 0:D], hs[fpar][:, t * P:(t + 1) * P], core.ident, start=False, stop=True
                           ).then_inc(s["fin"], 1)

                    pe.wait_ge(s["hs"], c + 1)
                    one_ahead(turn, multiply, None if flagged is None else lambda: flags(flagged))

                def step(j, par, k, more):
                    for t in range(NT):
                        n = NT * j + t
                        if t == NT - 1 and more >= 2:
                            flags(phase("in", j, more))
                        pe.wait_ge(s["prob"], n + 1)
                        at_least(pe, s["aggT"], n)
                        for c in range(NPROC // P):
                            last = tr(bank[4][:, c * P:(c + 1) * P], prob[:, t * NPROC + c * P:t * NPROC + (c + 1) * P],
                                      core.ident)
                        last.then_inc(s["tr_prob"], 1)
                        pe.wait_ge(s["probT"], n + 1)
                        for c in range(NPROC // P):
                            last = mm(bank[4][0:DPV, NPROC:NPROC + P], w_val[:, c * DPV:(c + 1) * DPV],
                                      probT[:, c * P:(c + 1) * P], start=c == 0, stop=c == NPROC // P - 1)
                        last.then_inc(s["agg"], 1)
                        pe.wait_ge(s["aggT"], n + 1)
                        at_least(pe, s["act_out"], n)
                        mm(bank[5], aggT[:, :], w_ow[:, :], start=True, stop=True).then_inc(s["out"], 1)
                    out_phase = None if at(j, 0) else phase("out", j, more)
                    if more >= 2:
                        process(j + 2, par, out_phase)
                    if out_phase is not None and (more < 2):
                        flags(out_phase)
                    if more == 3:
                        first(j + 3, 1 - par)
                    next_phase = phase("proc", j + 1, more - 1) if more else None
                    if at(j, 0):
                        flags(next_phase)
                    else:
                        final_products(j - 1, 1 - par, next_phase)
                    if not more:
                        flags(3 * j + 2)
                        final_products(j, par)

                first(0, 0)
                first(1, 1)
                flags(0)
                process(0, 0)
                first(2, 0)
                flags(1)
                process(1, 1)
                flags(2)
                chunks(pe, step)

            @block.scalar
            def _(act):
                f = nc.scalar.activation

                def guess(sel, what, sums, negs, sign_sums, tiles, j, k, c, t):
                    count, col = NT * len(sel.slopes) * j + k + 1, slice(t, t + 1)
                    if c == 0:
                        if len(sel.slopes) > 1:
                            nc.scalar.mul(slope[:, col], sums[:, col], -sel.slopes[0])
                            nc.scalar.mul(offset[:, col], sums[:, col], -sel.guess - sel.extra * sel.slopes[0])
                        made = nc.scalar.mul(negs[0][:, col], sums[:, col], -sel.guess)
                    else:
                        made = f(negs[1][:, col], sign_sums[0][:, col], ACT.Identity, scale=slope[:, col],
                                 bias=offset[:, col])
                    made.then_inc(s["guess_" + what], 1)
                    act.wait_ge(s["guess_" + what], count)
                    f(signs[:, 0:sel.width], tiles[:, t * sel.width:(t + 1) * sel.width], ACT.Sign,
                      bias=negs[c][:, col], accum_out=sign_sums[c][:, col]).then_inc(s["signs_" + what], 1)
                    act.wait_ge(s["signs_" + what], count)

                def first(j, par):
                    at_least(act, s["kept_in"], NT * (j - 1))
                    for t in range(NT):
                        act.wait_ge(s["act"], NT * j + t + 1)
                        f(act_in[par][:, t * NIN:(t + 1) * NIN], bank[0], ACT.Gelu,
                          accum_out=sum_in[par][:, t:t + 1]).then_inc(s["gelu"], 1)
                    act.wait_ge(s["gelu"], NT * (j + 1))

                def guess_in(j, par, k):
                    guess(SEL_IN, "in", sum_in[par], neg_in[par], signs_in[par], act_in[par], j, k, k // NT, k % NT)

                def process(j, par):
                    def copy(t):
                        n = NT * j + t
                        act.wait_ge(s["tr_in"], n + 1)
                        at_least(act, s["proc"], n - 1)
                        nc.scalar.copy(keptT[(par + t) % 2][:, :], bank[2]).then_inc(s["keptT"], 1)

                    copy(0)
                    for t in range(NT):
                        n = NT * j + t
                        if t < NT - 1:
                            copy(t + 1)
                        act.wait_ge(s["proc"], n + 1)
                        at_least(act, s["prob"], n - 2 * NT + 1)
                        f(act_proc[par][:, t * NPROC:(t + 1) * NPROC], bank[3][:, 0:NPROC], ACT.Gelu,
                          accum_out=sum_proc[par][:, t:t + 1]).then_inc(s["act_proc"], 1)
                        act.wait_ge(s["act_proc"], n + 1)
                        guess(SEL_PROC, "proc", sum_proc[par], neg_proc[par], signs_proc[par], act_proc[par], j, t, 0, t)

                def exponentials(j, par):
                    act.wait_ge(s["best"], j + 1)
                    at_least(act, s["prob"], NT * (j - 1))
                    nc.scalar.mul(neg_best[:, :], best[:, :], -1.0).then_inc(s["neg_best"], 1)
                    act.wait_ge(s["neg_best"], j + 1)
                    for t in range(NT):
                        f(expo[par][:, t * NPROC:(t + 1) * NPROC], act_proc[par][:, t * NPROC:(t + 1) * NPROC], ACT.Exp,
                          bias=neg_best[:, t:t + 1]).then_inc(s["expo"], 1)

                def step(j, par, k, more):
                    guess_out = lambda k, c, t: guess(SEL_OUT, "out", sum_out[par], neg_out[par], signs_out[par],
                                                      act_out[par], j, k, c, t)
                    for t in range(NT):
                        n = NT * j + t
                        act.wait_ge(s["tr_prob"], n + 1)
                        at_least(act, s["agg"], n)
                        nc.scalar.copy(probT[:, :], bank[4][:, 0:NPROC]).then_inc(s["probT"], 1)
                        act.wait_ge(s["agg"], n + 1)
                        at_least(act, s["out"], n)
                        nc.scalar.copy(aggT[:, :], bank[4][0:DPV, NPROC:NPROC + P]).then_inc(s["aggT"], 1)
                        if t:
                            guess_out(t - 1, 0, t - 1)
                        if t == NT - 1:
                            guess_out(t, 1, 0)
                        act.wait_ge(s["out"], n + 1)
                        at_least(act, s["kept_out"], n - 2 * NT + 1)
                        f(act_out[par][:, t * NOUT:(t + 1) * NOUT], bank[5], ACT.Gelu, scale=rsum[:, t:t + 1],
                          accum_out=sum_out[par][:, t:t + 1]).then_inc(s["act_out"], 1)
                        act.wait_ge(s["act_out"], n + 1)
                    guess_out(NT, 0, NT - 1)
                    for t in range(1, NT):
                        guess_out(NT + t, 1, t)
                    if more >= 2:
                        process(j + 2, par)
                    if more == 3:
                        first(j + 3, 1 - par)
                    if more:
                        exponentials(j + 1, 1 - par)
                    guess_next = (lambda n: guess_in(j + 3, 1 - par, n)) if more == 3 else (lambda n: None)
                    if not at(j, 0):
                        turned(j - 1, 1 - par, k if par else k - 1, guess_next)
                    else:
                        for n in range(2 * NT):
                            guess_next(n)
                    if not more:
                        turned(j, par, k, lambda n: None)

                def turned(c, fpar, half, guess_next):
                    def copy(t):
                        n = NT * c + t
                        act.wait_ge(s["tr_out"], n + 1)
                        at_least(act, s["fin"], n - 1)
                        nc.scalar.copy(outT[(fpar + t) % 2][:, :], bank[1]).then_inc(s["outT"], 1)

                    copy(0)
                    for t in range(NT):
                        n = NT * c + t
                        if t < NT - 1:
                            copy(t + 1)
                        guess_next(2 * t)
                        act.wait_ge(s["fin"], n + 1)
                        at_least(act, s_dram[fpar], 16 * half)
                        nc.scalar.copy(final[fpar][:, t * D:(t + 1) * D], bank[7][:, 0:D]).then_inc(s["final"], 1)
                        guess_next(2 * t + 1)

                for j in range(2):
                    first(j, j)
                    for k in range(2 * NT):
                        guess_in(j, j, k)
                process(0, 0)
                first(2, 0)
                for k in range(2 * NT):
                    guess_in(2, 0, k)
                process(1, 1)
                exponentials(0, 0)
                chunks(act, step)

            @block.vector
            def _(dve):
                v, tt = nc.vector, nc.vector.tensor_tensor
                chain = LocalChain(dve, s["chain"])
                flag = core.ctx.enter_context(dve.register("pat_flag"))

                def select(sel, number, left, tiles, sums, negs, sign_sums, ready):
                    src = lambda t: tiles[:, t * sel.width:(t + 1) * sel.width]
                    mark = lambda t: left[t][:, :]
                    v.memset(carrier[:, 1:2], 0.0)
                    chain.begin()
                    dve.wait_ge(*ready)
                    chain.link(v.scalar_tensor_tensor(out=thr[:, :], in0=sign_sums[-1][:, :], scalar=sel.extra,
                                                      in1=sums[:, :], op0=ALU.add, op1=ALU.mult))
                    chain.link(v.scalar_tensor_tensor(out=thr[:, :], in0=thr[:, :], scalar=sel.slopes[-1],
                                                      in1=negs[-1][:, :], op0=ALU.mult, op1=ALU.subtract))
                    if sel.floor is not None:
                        chain.link(v.tensor_scalar(thr[:, :], thr[:, :], sel.floor, None, ALU.max))
                    for t in range(NT):
                        counted = v.tensor_scalar(mark(t), src(t), thr[:, t:t + 1], None, ALU.is_ge, ALU.add,
                                                  accum_out=count[:, t:t + 1])
                    chain.link(counted)
                    chain.link(v.tensor_scalar(togo[:, :], count[:, :], -1.0, float(sel.k), ALU.mult, ALU.add))
                    replaced = []
                    for t in range(NT):
                        if t:
                            chain.after(offset_made)
                        offset_made = chain.mark(
                            v.tensor_scalar(off[:, :], togo[:, :], 4.0 * sel.rounds + 0.5, None, ALU.subtract) if t == 0
                            else tt(off[:, :], off[:, :], off[:, :], ALU.mult) if t == 1
                            else v.tensor_scalar(far[:, :], off[:, :], 16.0 * sel.rounds ** 2, None, ALU.is_gt))
                        v.scalar_tensor_tensor(out=mark(t), in0=mark(t), scalar=TAKEN, in1=src(t),
                                               op0=ALU.mult, op1=ALU.add)
                        replaced.append(chain.mark(v.tensor_scalar(
                            rank[t][:, 0:8 * sel.rounds], core.iota48[:, 0:8 * sel.rounds], togo[:, t:t + 1], 0.5,
                            ALU.is_lt, ALU.subtract)))
                    chain.after(offset_made)
                    v.memset(carrier[:, 2:3], 0.0).then_inc(s["far"], 1)
                    for r in range(sel.rounds):
                        found, cut = [], []
                        for t in range(NT):
                            chain.after(replaced[t])
                            found.append(chain.mark(v.max(top[t][:, :], mark(t))))
                        for t in range(NT):
                            chain.after(found[t])
                            cut.append(chain.mark(v.scalar_tensor_tensor(
                                out=masked[t][:, :], in0=rank[t][:, 8 * r:8 * r + 8], scalar=-2.0 * TAKEN,
                                in1=top[t][:, :], op0=ALU.mult, op1=ALU.min)))
                        if r == sel.rounds - 1:
                            dve.wait_ge(s["flags"], number + 1)
                            v.tensor_copy(redo[:, 0:NT], bank[6][0:1, 0:NT])
                            v.tensor_reduce(redo[:, NT:NT + 1], bank[6][0:1, 0:NT], AX.X, ALU.add
                                            ).then_inc(s["redone"], 1)
                            dve.wait_ge(s["redone"], number + 1)
                            loadable = chain.mark(v.memset(carrier[:, 0:1], 0.0))
                        for t in range(NT):
                            chain.after(cut[t])
                            replaced[t] = chain.mark(v.match_replace(mark(t), masked[t][:, :], mark(t), TAKEN))
                        if r == sel.rounds - 1:
                            chain.after(loadable)
                            dve.reg_load(flag, redo[0:1, NT:NT + 1].bitcast(U32))
                    with dve.If_ne(flag, 0):
                        chain.after(replaced[-1])
                        for t in range(NT):
                            dve.reg_load(flag, redo[0:1, t:t + 1].bitcast(U32))
                            with dve.If_ne(flag, 0):
                                full(sel, mark(t), src(t))
                    return replaced

                def full(sel, mark, src):
                    again.begin()
                    for r in range(sel.k // 8):
                        from_ = mark if r else src
                        again.link(v.max(top[0][:, :], from_))
                        again.link(v.match_replace(mark, top[0][:, :], from_, TAKEN))

                again = LocalChain(dve, core.sem("pat_again"))

                def keep(replaced, dst, left, tiles, done):
                    for t in range(NT):
                        chain.after(replaced[t])
                        v.scalar_tensor_tensor(out=dst[:, t * NIN:(t + 1) * NIN], in0=left[t][:, :], scalar=TAKEN / 2,
                                               in1=tiles[:, t * NIN:(t + 1) * NIN], op0=ALU.is_lt, op1=ALU.mult
                                               ).then_inc(done, 1)

                def select_in(j, par, number):
                    at_least(dve, s["tr_in"], NT * j)
                    replaced = select(SEL_IN, number, left_in, act_in[par], sum_in[par], neg_in[par], signs_in[par],
                                      (s["signs_in"], NT * 2 * (j + 1)))
                    keep(replaced, kept_in, left_in, act_in[par], s["kept_in"])
                    dve.wait_ge(s["kept_in"], NT * (j + 1))

                def step(j, par, k, more):
                    dve.wait_ge(s["act_proc"], NT * (j + 1))
                    at_least(dve, s["neg_best"], j)
                    v.tensor_reduce(best[:, :], heads(act_proc[par][:, :], NT), AX.X, ALU.max).then_inc(s["best"], 1)
                    at_least(dve, s["tr_prob"], NT * j)
                    at_least(dve, s["act_out"], NT * j)
                    replaced = select(SEL_PROC, phase("proc", j, more), left_proc, act_proc[par], sum_proc[par],
                                      neg_proc[par], signs_proc[par],
                                      (s["signs_proc"], NT * (j + 1)))
                    summed = []

                    def invert(t):
                        chain.after(summed[t])
                        v.reciprocal(rsum[:, t:t + 1], psums[:, t:t + 1]).then_inc(s["prob"], 1)

                    for t in range(NT):
                        chain.after(replaced[t])
                        v.memset(carrier[:, 4 + t:5 + t], 0.0)
                        dve.wait_ge(s["expo"], NT * j + t + 1)
                        cut = slice(t * NPROC, (t + 1) * NPROC)
                        summed.append(chain.mark(v.scalar_tensor_tensor(
                            out=prob[:, cut], in0=left_proc[t][:, :], scalar=TAKEN / 2, in1=expo[par][:, cut],
                            op0=ALU.is_lt, op1=ALU.mult, accum_out=psums[:, t:t + 1])))
                        if t:
                            invert(t - 1)
                    invert(NT - 1)
                    dve.wait_ge(s["prob"], NT * (j + 1))
                    if more >= 2:
                        select_in(j + 2, par, phase("in", j, more))
                    if not at(j, 0):
                        select_out(j - 1, 1 - par, phase("out", j, more))
                    if not more:
                        select_out(j, par, 3 * j + 2)

                def select_out(c, opar, number):
                    at_least(dve, s["tr_out"], NT * c)
                    replaced = select(SEL_OUT, number, left_out, act_out[opar], sum_out[opar], neg_out[opar],
                                      signs_out[opar], (s["signs_out"], NT * 2 * (c + 1)))
                    keep(replaced, kept_out, left_out, act_out[opar], s["kept_out"])
                    dve.wait_ge(s["kept_out"], NT * (c + 1))

                select_in(0, 0, 0)
                select_in(1, 1, 1)
                chunks(dve, step)
def vit_tower(nc, dram):
    with ExitStack() as ctx:
        core = Core(nc, ctx, dram)
        embed(core)
        attend(core)
        experts(core)
        memory(core)
        patterns(core)


def laid_out(i):
    a = {k: np.asarray(v) for k, v in i.items()}
    col = lambda v: v.reshape(-1, 1)
    stack = lambda *v: np.stack(v, axis=1)
    r = {"x": a["x"], "const": constants()}
    r["tok_w"] = a["L0_tok_W"].reshape(D, PATCH, PATCH, CH).transpose(3, 1, 2, 0)
    r["tok_w"] = np.concatenate([r["tok_w"][:, :, c::2].reshape(CH * PATCH, -1) for c in (0, 1)])
    r["tok_cols"] = stack(a["L0_tok_b"], a["L0_tok_cls_token"].reshape(D))
    r["tok_pos"] = a["L0_tok_pos_emb"].reshape(1, L)
    by_head = lambda w: w.reshape(-1, KDIM, HEADS).transpose(0, 2, 1).reshape(-1, KDIM * HEADS)
    r["att_qk"] = np.concatenate([by_head(a["L0_attn_qw"]), by_head(a["L0_attn_kw"])], axis=1)
    qkb = np.concatenate([by_head(a["L0_attn_qb"]), by_head(a["L0_attn_kb"])], axis=1)
    r["att_v"] = a["L0_attn_vw"].reshape(D, D, HEADS).transpose(0, 2, 1).reshape(D, HEADS * D)
    r["att_w1"] = a["L0_attn_w1"].reshape(D, HEADS * F1)
    r["att_w2"] = a["L0_attn_w2"].reshape(F1 // P, P, D).transpose(1, 0, 2).reshape(P, F1)
    r["att_cols"] = np.concatenate([col(a["L0_attn_ln0_w"]), col(a["L0_attn_ln0_b"]), qkb.reshape(4, P).T,
                                    a["L0_attn_vb"].reshape(D, HEADS), a["L0_attn_ln1_w"], a["L0_attn_ln1_b"],
                                    a["L0_attn_b1"].reshape(F1 // P, P).T, col(a["L0_attn_b2"])], axis=1)
    r["moe_router"] = a["L0_ffn_router_w"]
    r["moe_router_b"] = a["L0_ffn_router_b"].reshape(1, EXPERTS)
    r["moe_up"] = a["L0_ffn_gate_up_proj"].transpose(1, 0, 2).reshape(D, EXPERTS * 2 * INTER)
    r["moe_up_b"] = a["L0_ffn_gate_up_proj_bias"].reshape(EXPERTS * 4, P).T
    r["moe_down"] = a["L0_ffn_down_proj"].reshape(EXPERTS, 2, P, D).transpose(2, 0, 1, 3).reshape(P, EXPERTS * INTER)
    r["moe_down_b"] = a["L0_ffn_down_proj_bias"]
    r["mem_w"] = np.concatenate([a["L1_attn_q_w"].T, a["L1_attn_eta_w1"], a["L1_attn_eta_w2"], a["L1_attn_alpha_w1"],
                                 a["L1_attn_alpha_w2"], a["L1_attn_mem_w1"], a["L1_attn_mem_w2"]], axis=1)
    r["mem_conv"] = np.concatenate([a["L1_attn_conv_w"].reshape(D, TAPS), col(a["L1_attn_conv_b"])], axis=1)
    r["pat_in"] = a["L1_ffn_input_patterns"].T
    r["pat_proc"] = a["L1_ffn_process_input_weights"].T.reshape(NIN // P, P, NPROC).transpose(1, 0, 2).reshape(P, -1)
    r["pat_val"] = a["L1_ffn_process_values"].reshape(NPROC // P, P, DPV).transpose(1, 0, 2).reshape(P, -1)
    r["pat_ow"] = a["L1_ffn_output_input_weights"].T
    r["pat_out"] = a["L1_ffn_output_patterns"].reshape(NOUT // P, P, D).transpose(1, 0, 2).reshape(P, -1)
    return {k: np.ascontiguousarray(v) for k, v in r.items()}


def kernel(**inputs):
    import concourse.bacc as bacc
    from concourse.bass_utils import run_bass_kernel_spmd

    nc = bacc.Bacc("TRN2", target_bir_lowering=False, num_devices=1)
    arrays = laid_out(inputs)
    dram = {k: nc.dram_tensor(f"in_{k}", v.shape, mybir.dt.from_np(v.dtype), kind="ExternalInput").ap()
            for k, v in arrays.items()}
    dram["out"] = nc.dram_tensor("out_tokens", (TOK, D), F32, kind="ExternalOutput").ap()
    vit_tower(nc, dram)
    r = run_bass_kernel_spmd(nc, [{f"in_{k}": v for k, v in arrays.items()}], core_ids=[0])
    return r.results[0]["out_tokens"].reshape(NIMG, L, D)
```
